# Optimizing a Trainium2 kernel written in Bass

```python
import numpy as np
import jax
import jax.numpy as jnp

def _softmax(x, axis=-1):
    return jax.nn.softmax(x, axis=axis)

def _gelu(x):
    return jax.nn.gelu(x, approximate=True)

def _silu(x):
    return jax.nn.silu(x)

def _sigmoid(x):
    return jax.nn.sigmoid(x)

def _layernorm(x, axis=-1, eps=1e-05):
    m = jnp.mean(x, axis=axis, keepdims=True)
    v = jnp.var(x, axis=axis, keepdims=True)
    return (x - m) / jnp.sqrt(v + eps)

def _scatter_add(tgt, idx, src, axis=0):
    return tgt.at[idx].add(src)

def _segment_sum(src, seg, n):
    return jax.ops.segment_sum(src, seg, n)
kernel_name = 'mk_recurrent_d2_jaxref_r8_4d415b'

def setup_inputs(seed: int=0):
    np.random.seed(seed)
    _w = jnp.asarray

    def _L0_attn_setup():
        import jax, jax.numpy as jnp
        import numpy as np
        NUM_HEADS = 16
        BLOCK_SIZE = 64
        key = jax.random.key(seed)
        ks = jax.random.split(key, 5)
        B, S, C = (2, 2047, 128)
        return {'x': jax.random.normal(ks[0], (B, S, C), dtype=jnp.float32), 'global_token': jax.random.normal(ks[1], (1, 1, C), dtype=jnp.float32), 'qkv_w': jax.random.normal(ks[2], (3 * C, C), dtype=jnp.float32) * 0.02, 'proj_w': jax.random.normal(ks[3], (C, C), dtype=jnp.float32) * 0.02, 'proj_b': jax.random.normal(ks[4], (C,), dtype=jnp.float32) * 0.02}
    _L0_attn_in = _L0_attn_setup()

    def _L0_ffn_setup():
        import jax, jax.numpy as jnp
        import numpy as np
        ALPHA = 1.702
        LIMIT = 7.0
        TOP_K = 2
        key = jax.random.key(seed)
        ks = jax.random.split(key, 4)
        B, S, H, E, I = (2, 128, 128, 8, 256)
        return {'hidden_states': jax.random.normal(ks[0], (B, S, H), jnp.float32), 'router_weight': jax.random.normal(ks[1], (E, H), jnp.float32), 'router_bias': jnp.zeros((E,), jnp.float32), 'gate_up_proj': jax.random.normal(ks[2], (E, H, 2 * I), jnp.float32) * 0.02, 'gate_up_bias': jnp.zeros((E, 2 * I), jnp.float32), 'down_proj': jax.random.normal(ks[3], (E, I, H), jnp.float32) * 0.02, 'down_bias': jnp.zeros((E, H), jnp.float32)}
    _L0_ffn_in = _L0_ffn_setup()

    def _L1_attn_setup():
        import jax, jax.numpy as jnp
        import numpy as np
        HEADS = 16
        DIM_HEAD = 64
        key = jax.random.key(seed)
        k1, k2, k3, k4 = jax.random.split(key, 4)
        B, T, D = (4, 128, 128)
        x = jax.random.normal(k1, (B, T, D), dtype=jnp.float32)
        w_qkv = jax.random.normal(k2, (3 * HEADS * DIM_HEAD, D), dtype=jnp.float32) * (1.0 / np.sqrt(D))
        w_out = jax.random.normal(k3, (D, HEADS * DIM_HEAD), dtype=jnp.float32) * (1.0 / np.sqrt(HEADS * DIM_HEAD))
        rel_bias = jax.random.normal(k4, (2 * 128 - 1, HEADS), dtype=jnp.float32) * 0.02
        return {'x': x, 'w_qkv': w_qkv, 'w_out': w_out, 'rel_bias': rel_bias}
    _L1_attn_in = _L1_attn_setup()

    def _L1_ffn_setup():
        import jax, jax.numpy as jnp
        import numpy as np
        B, L, D = (2, 256, 128)
        E = 15
        H = D * 1
        K = 3
        T = 1.0
        key = jax.random.key(seed)
        ks = jax.random.split(key, 12)
        s = 0.02
        return {'x': jax.random.normal(ks[0], (B, L, D), dtype=jnp.float32), 'router_W': jax.random.normal(ks[1], (D, E), dtype=jnp.float32) * s, 'router_b': jnp.zeros((E,), dtype=jnp.float32), 'sW1': jax.random.normal(ks[2], (D, H), dtype=jnp.float32) * s, 'sb1': jnp.zeros((H,), dtype=jnp.float32), 'sW2': jax.random.normal(ks[3], (H, D), dtype=jnp.float32) * s, 'sb2': jnp.zeros((D,), dtype=jnp.float32), 'eW1': jax.random.normal(ks[4], (E, D, H), dtype=jnp.float32) * s, 'eb1': jnp.zeros((E, H), dtype=jnp.float32), 'eW2': jax.random.normal(ks[5], (E, H, D), dtype=jnp.float32) * s, 'eb2': jnp.zeros((E, D), dtype=jnp.float32)}
    _L1_ffn_in = _L1_ffn_setup()
    _d = {'L0_attn_x': _L0_attn_in['x'], 'L0_attn_global_token': _L0_attn_in['global_token'], 'L0_attn_qkv_w': _L0_attn_in['qkv_w'], 'L0_attn_proj_w': _L0_attn_in['proj_w'], 'L0_attn_proj_b': _L0_attn_in['proj_b'], 'L0_ffn_router_weight': _L0_ffn_in['router_weight'], 'L0_ffn_router_bias': _L0_ffn_in['router_bias'], 'L0_ffn_gate_up_proj': _L0_ffn_in['gate_up_proj'], 'L0_ffn_gate_up_bias': _L0_ffn_in['gate_up_bias'], 'L0_ffn_down_proj': _L0_ffn_in['down_proj'], 'L0_ffn_down_bias': _L0_ffn_in['down_bias'], 'L1_attn_w_qkv': _L1_attn_in['w_qkv'], 'L1_attn_w_out': _L1_attn_in['w_out'], 'L1_attn_rel_bias': _L1_attn_in['rel_bias'], 'L1_ffn_router_W': _L1_ffn_in['router_W'], 'L1_ffn_router_b': _L1_ffn_in['router_b'], 'L1_ffn_sW1': _L1_ffn_in['sW1'], 'L1_ffn_sb1': _L1_ffn_in['sb1'], 'L1_ffn_sW2': _L1_ffn_in['sW2'], 'L1_ffn_sb2': _L1_ffn_in['sb2'], 'L1_ffn_eW1': _L1_ffn_in['eW1'], 'L1_ffn_eb1': _L1_ffn_in['eb1'], 'L1_ffn_eW2': _L1_ffn_in['eW2'], 'L1_ffn_eb2': _L1_ffn_in['eb2']}
    _x0 = _d['L0_attn_x']
    _d['L0_attn_x'] = jax.random.normal(jax.random.fold_in(jax.random.key(seed), 1), (4, 512, 128), dtype=_x0.dtype)
    del _x0
    return _d

def reference(L0_attn_x, L0_attn_global_token, L0_attn_qkv_w, L0_attn_proj_w, L0_attn_proj_b, L0_ffn_router_weight, L0_ffn_router_bias, L0_ffn_gate_up_proj, L0_ffn_gate_up_bias, L0_ffn_down_proj, L0_ffn_down_bias, L1_attn_w_qkv, L1_attn_w_out, L1_attn_rel_bias, L1_ffn_router_W, L1_ffn_router_b, L1_ffn_sW1, L1_ffn_sb1, L1_ffn_sW2, L1_ffn_sb2, L1_ffn_eW1, L1_ffn_eb1, L1_ffn_eW2, L1_ffn_eb2):

    def _L0_attn_ref(x, global_token, qkv_w, proj_w, proj_b):
        import jax, jax.numpy as jnp
        import numpy as np
        NUM_HEADS = 16
        BLOCK_SIZE = 64
        B, S, C = x.shape
        H = NUM_HEADS
        D = C // H
        scale = D ** (-0.5)
        g = jnp.broadcast_to(global_token, (B, 1, C))
        xg = jnp.concatenate([g, x], axis=1)
        N = S + 1
        qkv = (xg @ qkv_w.T).reshape(B, N, 3, H, D)
        qkv = jnp.transpose(qkv, (2, 0, 3, 1, 4))
        q, k, v = (qkv[0], qkv[1], qkv[2])
        blk = jnp.arange(N) // BLOCK_SIZE
        mask = blk[:, None] >= blk[None, :]
        attn = jnp.einsum('bhqd,bhkd->bhqk', q, k) * scale
        attn = jnp.where(mask[None, None], attn, -jnp.inf)
        attn = jax.nn.softmax(attn, axis=-1)
        out = jnp.einsum('bhqk,bhkd->bhqd', attn, v)
        out = jnp.transpose(out, (0, 2, 1, 3)).reshape(B, N, C)
        out = out[:, 1:, :]
        return out @ proj_w.T + proj_b

    def _L0_ffn_ref(hidden_states, router_weight, router_bias, gate_up_proj, gate_up_bias, down_proj, down_bias):
        import jax, jax.numpy as jnp
        import numpy as np
        ALPHA = 1.702
        LIMIT = 7.0
        TOP_K = 2
        B, S, H = hidden_states.shape
        E, _, two_I = gate_up_proj.shape
        I = two_I // 2
        flat = hidden_states.reshape(B * S, H)
        logits = flat @ router_weight.T + router_bias
        scores = jax.nn.softmax(logits, axis=-1)
        topk_w, topk_idx = jax.lax.top_k(scores, TOP_K)
        gu = jnp.einsum('th,ehn->ten', flat, gate_up_proj) + gate_up_bias
        gate = jnp.minimum(gu[..., :I], LIMIT)
        up = jnp.clip(gu[..., I:], -LIMIT, LIMIT)
        glu = gate * jax.nn.sigmoid(gate * ALPHA)
        act = (up + 1.0) * glu
        down = jnp.einsum('tei,eih->teh', act, down_proj) + down_bias
        gathered = jnp.take_along_axis(down, topk_idx[:, :, None], axis=1)
        out = (gathered * topk_w[:, :, None]).sum(axis=1)
        return out.reshape(B, S, H)

    def _L1_attn_ref(x, w_qkv, w_out, rel_bias):
        import jax, jax.numpy as jnp
        import numpy as np
        HEADS = 16
        DIM_HEAD = 64
        b, t, _ = x.shape
        h, dh = (HEADS, DIM_HEAD)
        scale = dh ** (-0.5)
        qkv = x @ w_qkv.T
        qkv = qkv.reshape(b, t, dh, 3, h).transpose(3, 0, 4, 1, 2)
        q, k, v = (qkv[0], qkv[1], qkv[2])
        scores = jnp.einsum('bhid,bhjd->bhij', q, k) * scale
        rel = jnp.arange(t)[None, :] - jnp.arange(t)[:, None] + (t - 1)
        bias = rel_bias[rel]
        scores = scores + bias.transpose(2, 0, 1)[None]
        attn = jax.nn.softmax(scores, axis=-1)
        out = jnp.einsum('bhij,bhjd->bhid', attn, v)
        out = out.transpose(0, 2, 1, 3).reshape(b, t, h * dh)
        return out @ w_out.T

    def _L1_ffn_ref(x, router_W, router_b, sW1, sb1, sW2, sb2, eW1, eb1, eW2, eb2):
        import jax, jax.numpy as jnp
        import numpy as np
        B, L, D = (2, 256, 128)
        E = 15
        H = D * 1
        K = 3
        T = 1.0
        b, l, d = x.shape
        n = b * l
        xt = x.reshape(n, d)
        shared = jax.nn.relu(xt @ sW1 + sb1) @ sW2 + sb2
        logits = xt @ router_W + router_b
        probs = jax.nn.softmax(logits / T, axis=-1)
        top_p, top_i = jax.lax.top_k(probs, K)
        cw = jnp.zeros((n, E), dtype=probs.dtype)
        cw = cw.at[jnp.arange(n)[:, None], top_i].set(top_p)
        h = jax.nn.relu(jnp.einsum('nd,edh->neh', xt, eW1) + eb1)
        ye = jnp.einsum('neh,ehd->ned', h, eW2) + eb2
        routed = jnp.einsum('ned,ne->nd', ye, cw)
        return (shared + routed).reshape(b, l, d)
    x = L0_attn_x
    xn = _layernorm(x, axis=-1)
    s = _L0_attn_ref(xn, L0_attn_global_token, L0_attn_qkv_w, L0_attn_proj_w, L0_attn_proj_b)
    g = _silu(_L0_ffn_ref(xn, L0_ffn_router_weight, L0_ffn_router_bias, L0_ffn_gate_up_proj, L0_ffn_gate_up_bias, L0_ffn_down_proj, L0_ffn_down_bias))
    x = x + s * g
    xn = _layernorm(x, axis=-1)
    s = _L1_attn_ref(xn, L1_attn_w_qkv, L1_attn_w_out, L1_attn_rel_bias)
    g = _silu(_L1_ffn_ref(xn, L1_ffn_router_W, L1_ffn_router_b, L1_ffn_sW1, L1_ffn_sb1, L1_ffn_sW2, L1_ffn_sb2, L1_ffn_eW1, L1_ffn_eb1, L1_ffn_eW2, L1_ffn_eb2))
    x = x + s * g
    return x

_drawn_inputs = setup_inputs


def setup_inputs(seed=0):
    import zlib

    import numpy as np

    out = dict(_drawn_inputs(seed))
    spreads = {'L0_ffn_router_bias': (0.0, 0.8),
     'L0_ffn_gate_up_bias': (0.0, 0.8),
     'L0_ffn_down_bias': (0.0, 0.8),
     'L1_ffn_router_b': (0.0, 0.8),
     'L1_ffn_sb1': (0.0, 0.8),
     'L1_ffn_sb2': (0.0, 0.8),
     'L1_ffn_eb1': (0.0, 0.8),
     'L1_ffn_eb2': (0.0, 0.8)}
    factors = {'L0_attn_global_token': 8.0,
     'L0_attn_qkv_w': 8.0,
     'L0_attn_proj_w': 8.0,
     'L0_attn_proj_b': 8.0,
     'L0_ffn_router_weight': 8.0,
     'L0_ffn_gate_up_proj': 8.0,
     'L0_ffn_down_proj': 8.0,
     'L1_attn_w_qkv': 7.016,
     'L1_attn_w_out': 5.778,
     'L1_attn_rel_bias': 63.32,
     'L1_ffn_router_W': 8.0,
     'L1_ffn_sW1': 8.0,
     'L1_ffn_sW2': 8.0,
     'L1_ffn_eW1': 8.0,
     'L1_ffn_eW2': 8.0}
    for name, (base, spread) in spreads.items():
        noise = np.random.default_rng([zlib.crc32(name.encode()), seed]).standard_normal(out[name].shape)
        drawn = base * np.exp(spread * noise) if base else spread * noise
        out[name] = jnp.asarray(drawn.astype(out[name].dtype))
    for name, factor in factors.items():
        out[name] = (out[name] * factor).astype(out[name].dtype)
    return out
```

```python
from contextlib import ExitStack

import concourse.bass as bass
from concourse import mybir

P = 128
F32 = mybir.dt.float32
F16 = mybir.dt.float16
BF16 = mybir.dt.bfloat16
ALU = mybir.AluOpType
ACT = mybir.ActivationFunctionType
AXX = mybir.AxisListType.X

B, S, C = 4, 512, 128
TPB = S // P
NT = B * TPB
H = 16
D0, D1 = C // H, 64
NH = B * H
G = 4
NG = NH // G
BLK = 64
NBLK = S // BLK + 1
KPAD = 5 * P
E0, TOP0, I0 = 8, 2, 256
E1, TOP1 = 15, 3
NE1 = E1 + 1
ALPHA, LIMIT, EPS = 1.702, 7.0, 1e-5
BIG = -1.0e30

FIRST = [1, 128, 256, 384, 512]
WIDTH = [513 - f for f in FIRST]
BASE = [0, WIDTH[0], WIDTH[0] + WIDTH[1], sum(WIDTH[:3]), sum(WIDTH[:4])]
PW = sum(WIDTH)
QT = [(1, 127), (128, 128), (256, 128), (384, 128), (512, 1)]


class Mem:

    def __init__(self, nc, ctx):
        self.nc, self.ctx = nc, ctx

    def sb(self, name, shape, dt=F32):
        return self.ctx.enter_context(self.nc.sbuf_tensor(name, shape, dt))

    def ps(self, name, shape, dt=F32):
        return self.ctx.enter_context(self.nc.psum_tensor(name, shape, dt))

    def sem(self, name):
        return self.ctx.enter_context(self.nc.semaphore(name))


def own_chain(eng, sem):
    count = [0]

    def link(ins):
        count[0] += 1
        ins.then_inc(sem, 1)
        eng.wait_ge(sem, count[0])

    return link


def three_passes(nc, out, wh, wl, xh, xl):
    nc.tensor.matmul(out, wh, xl, start=True, stop=False)
    nc.tensor.matmul(out, wl, xh, start=False, stop=False)
    return nc.tensor.matmul(out, wh, xh, start=False, stop=True)


def layer_norm_phase(nc, tag, x, xh, xl, ident, glob, loads=None):
    with ExitStack() as ctx:
        m = Mem(nc, ctx)
        stats = m.sb(f"{tag}_stats", [P, NT, 6])
        mv = m.sb(f"{tag}_mv", [P, NT, 2])
        rstd = m.sb(f"{tag}_rstd", [P, NT])
        xn = m.sb(f"{tag}_xn", [P, NT, C])
        xt = m.ps(f"{tag}_xt", [P, B, S])
        chain = m.sem(f"{tag}_chain")
        var_ready = m.sem(f"{tag}_var")
        std_ready = m.sem(f"{tag}_std")
        xn_ready = m.sem(f"{tag}_xn_ready")
        xt_ready = m.sem(f"{tag}_xt_ready")
        hi_ready = m.sem(f"{tag}_hi_ready")
        block = ctx.enter_context(nc.Block())
        if loads is not None:
            block.sync(loads)

        @block.vector
        def _(dve):
            link = own_chain(dve, chain)
            for t in range(NT):
                ins = nc.vector.bn_stats(stats[:, t, :], x[:, t, :])
            link(ins)
            for t in range(NT):
                ins = nc.vector.bn_aggr(mv[:, t, :], stats[:, t, :])
            link(ins)
            nc.vector.tensor_scalar_add(rstd[:], mv[:, :, 1], EPS).then_inc(var_ready, 1)
            dve.wait_ge(std_ready, 1)
            link(nc.vector.reciprocal(rstd[:], rstd[:]))
            for t in range(NT):
                nc.vector.tensor_scalar(xn[:, t, :], x[:, t, :], mv[:, t, 0:1], rstd[:, t:t + 1],
                                        ALU.subtract, ALU.mult).then_inc(xn_ready, 1)
            for b in range(B):
                dve.wait_ge(hi_ready, b + 1)
                nc.vector.tensor_tensor(xl[:, b, 1:1 + S], xt[:, b, :], xh[:, b, 1:1 + S],
                                        ALU.subtract)
            if glob is not None:
                for b in range(B):
                    ins = nc.vector.tensor_copy(xh[:, b, 0:1], glob[:])
                link(ins)
                for b in range(B):
                    nc.vector.tensor_tensor(xl[:, b, 0:1], glob[:], xh[:, 0, 0:1], ALU.subtract)

        @block.scalar
        def _(act):
            act.wait_ge(var_ready, 1)
            nc.scalar.activation(rstd[:], rstd[:], ACT.Sqrt).then_inc(std_ready, 1)
            for b in range(B):
                act.wait_ge(xt_ready, b + 1)
                nc.scalar.activation(xh[:, b, 1:1 + S], xt[:, b, :], ACT.Copy).then_inc(hi_ready, 1)

        @block.tensor
        def _(pe):
            for t in range(NT):
                pe.wait_ge(xn_ready, t + 1)
                ins = nc.tensor.transpose(xt[:, t // TPB, (t % TPB) * P:(t % TPB + 1) * P],
                                          xn[:, t, :], ident[:])
                if t % TPB == TPB - 1:
                    ins.then_inc(xt_ready, 1)


def project0_phase(nc, k, xh, xl, w, q4, kz, v0):
    with ExitStack() as ctx:
        m = Mem(nc, ctx)
        wh = m.sb("p0_wh", [P, 2, 4, P], F16)
        wl = m.sb("p0_wl", [P, 2, 4, P], F16)
        wvh = m.sb("p0_wvh", [P, C], F16)
        wvl = m.sb("p0_wvl", [P, C], F16)
        signed = m.sb("p0_signed", [P, 2, S], F16)
        k4 = m.sb("p0_k4", [P, 2, S], F16)
        last = m.sb("p0_last", [P, 2, 4], F16)
        acc = m.ps("p0_acc", [P, 4, 512])
        klast = m.ps("p0_klast", [P, 512])
        vacc = m.ps("p0_vacc", [P, 512])
        vlast = m.ps("p0_vlast", [P, 512])
        w_ready = m.sem("p0_w_ready")
        zeroed = m.sem("p0_zeroed")
        acc_ready = m.sem("p0_acc_ready")
        signed_ready = m.sem("p0_signed_ready")
        acc_free = m.sem("p0_acc_free")
        kl_ready = m.sem("p0_kl_ready")
        kl_signed = m.sem("p0_kl_signed")
        kl_free = m.sem("p0_kl_free")
        v_ready = m.sem("p0_v_ready")
        vhi_ready = m.sem("p0_vhi_ready")
        v_free = m.sem("p0_v_free")
        chain = m.sem("p0_chain")
        passed = m.sem("p0_passed")
        block = ctx.enter_context(nc.Block())
        kgroups = kz[:, :, :].rearrange("p (n j) s -> p n j s", j=G)

        @block.gpsimd
        def _(pool):
            nc.gpsimd.memset(kz[:, :, S + 1:KPAD], 0.0)
            nc.gpsimd.memset(v0[:, :, TPB, :], 0.0).then_inc(zeroed, 1)
            pool.wait_ge(zeroed, 1)
            nc.gpsimd.memset(v0[:, :, :, D0:D0 + 1], 1.0).then_inc(zeroed, 1)

        @block.vector
        def _(dve):
            link = own_chain(dve, chain)
            dve.sem_inc(acc_free, 4)
            dve.sem_inc(kl_free, 1)
            dve.sem_inc(v_free, 1)
            nc.vector.tensor_copy(wh[:], w["qk0"][:])
            link(nc.vector.tensor_copy(wvh[:], w["v0"][:]))
            nc.vector.tensor_tensor(wl[:], w["qk0"][:], wh[:], ALU.subtract)
            nc.vector.tensor_tensor(wvl[:], w["v0"][:], wvh[:], ALU.subtract).then_inc(w_ready, 1)
            dve.wait_ge(zeroed, 2)
            with dve.Fori(0, B) as b:
                for g in range(4):
                    for s in range(2):
                        u = 2 * g + s
                        dve.wait_ge(signed_ready, b * 8 + (u + 1))
                        out = q4[:, b * 4 + g, :] if s == 0 else k4[:, g % 2, :]
                        low = k["low_q"] if s == 0 else k["low_k"]
                        nc.vector.scalar_tensor_tensor(out, acc[:, u % 4, :], low, signed[:, s, :],
                                                       ALU.mult, ALU.subtract
                                                       ).then_inc(acc_free, 1)
                    dve.wait_ge(acc_free, b * 8 + (2 * g + 6))
                    for j in range(G):
                        nc.vector.tensor_scalar(kz[:, b * 16 + (4 * g + j), 0:S], k4[:, g % 2, :],
                                                k["own"][:, j:j + 1], None, ALU.mult)
                dve.wait_ge(kl_signed, b + 1)
                nc.vector.scalar_tensor_tensor(last[:, 1, :], klast[:, 0:4], k["low_k"],
                                               last[:, 0, :], ALU.mult, ALU.subtract
                                               ).then_inc(kl_free, 1)
                dve.wait_ge(kl_free, b + 2)
                for g in range(4):
                    for j in range(G):
                        nc.vector.tensor_scalar(kz[:, b * 16 + (4 * g + j), S:S + 1],
                                                last[:, 1, g:g + 1],
                                                k["own"][:, j:j + 1], None, ALU.mult)
                dve.wait_ge(vhi_ready, b + 1)
                vb = v0[:, bass.ds(b * 16, 16), :, :]
                for t in range(TPB):
                    nc.vector.tensor_tensor(
                        vb[:, :, t, D0 + 1:2 * D0 + 1],
                        vacc[:, t * C:(t + 1) * C].rearrange("p (h d) -> p h d", h=H),
                        vb[:, :, t, 0:D0], ALU.subtract)
                nc.vector.tensor_tensor(
                    vb[0:1, :, TPB, D0 + 1:2 * D0 + 1],
                    vlast[0:1, 0:C].rearrange("p (h d) -> p h d", h=H),
                    vb[0:1, :, TPB, 0:D0], ALU.subtract).then_inc(v_free, 1)

        @block.scalar
        def _(act):
            act.preload_act_table(ACT.Exp)
            act.wait_ge(zeroed, 2)
            with act.Fori(0, B) as b:
                for u in range(8):
                    act.wait_ge(acc_ready, b * 8 + (u + 1))
                    act.wait_ge(acc_free, b * 8 + (u + 3))
                    nc.scalar.activation(signed[:, u % 2, :], acc[:, u % 4, :], ACT.Copy,
                                         scale=k["sign_q"] if u % 2 == 0 else k["sign_k"]
                                         ).then_inc(signed_ready, 1)
                act.wait_ge(kl_ready, b + 1)
                nc.scalar.activation(last[:, 0, :], klast[:, 0:4], ACT.Copy,
                                     scale=k["sign_k"]).then_inc(kl_signed, 1)
                act.wait_ge(v_ready, b + 1)
                act.sem_inc(passed, 1)
                vb = v0[:, bass.ds(b * 16, 16), :, :]
                for t in range(TPB):
                    nc.scalar.activation(vb[:, :, t, 0:D0],
                                         vacc[:, t * C:(t + 1) * C].rearrange(
                                             "p (h d) -> p h d", h=H), ACT.Copy)
                nc.scalar.activation(vb[0:1, :, TPB, 0:D0],
                                     vlast[0:1, 0:C].rearrange("p (h d) -> p h d", h=H),
                                     ACT.Copy).then_inc(vhi_ready, 1)

        @block.tensor
        def _(pe):
            pe.wait_ge(w_ready, 1)
            with pe.Fori(0, B) as b:
                for g in range(4):
                    for s in range(2):
                        u = 2 * g + s
                        pe.wait_ge(acc_free, b * 8 + (u + 1))
                        off = 1 - s
                        three_passes(nc, acc[:, u % 4, :], wh[:, s, g, :], wl[:, s, g, :],
                                     xh[:, b, off:off + S], xl[:, b, off:off + S]
                                     ).then_inc(acc_ready, 1)
                pe.wait_ge(kl_free, b + 1)
                for g in range(4):
                    ins = three_passes(nc, klast[:, g:g + 1], wh[:, 1, g, :], wl[:, 1, g, :],
                                       xh[:, b, S:S + 1], xl[:, b, S:S + 1])
                ins.then_inc(kl_ready, 1)
                pe.wait_ge(v_free, b + 1)
                for t in range(TPB):
                    three_passes(nc, vacc[:, t * C:(t + 1) * C], xh[:, b, t * P:(t + 1) * P],
                                 xl[:, b, t * P:(t + 1) * P], wvh[:], wvl[:])
                three_passes(nc, vlast[0:1, 0:C], xh[:, b, S:S + 1], xl[:, b, S:S + 1],
                             wvh[:], wvl[:]).then_inc(v_ready, 1)


def by_groups(eng, count, slot, per=4):
    for c in range(per):
        slot(0, c, c == 0, False)
    with eng.Fori(1, count - 1) as k:
        for c in range(per):
            slot(k, c, False, False)
    for c in range(per):
        slot(count - 1, c, False, c == per - 1)


def shift(k, c, by, per=4):
    return k + (c + by) // per, (c + by) % per



def attention0_phase(nc, k, q4, kz, v0, z0, loads):
    scale = float(D0) ** -0.5
    with ExitStack() as ctx:
        m = Mem(nc, ctx)
        smax = m.ps("a0_smax", [P, 2, 512])
        st = m.ps("a0_st", [P, 4, 512])
        o = m.ps("a0_o", [P, 2, 512])
        bm = m.sb("a0_bm", [P, TPB, NBLK])
        bmm = m.sb("a0_bmm", [P, TPB, NBLK])
        mx = m.sb("a0_mx", [P, 2, TPB], F16)
        p32 = m.sb("a0_p32", [P, 2, PW])
        ph = m.sb("a0_ph", [P, 2, PW], F16)
        pl = m.sb("a0_pl", [P, 2, PW], F16)
        r = m.sb("a0_r", [P, 2, 2, 5])
        preset = m.sem("a0_preset")
        smax_ready = m.sem("a0_smax_ready")
        smax_free = m.sem("a0_smax_free")
        bm_ready = m.sem("a0_bm_ready")
        mx_ready = m.sem("a0_mx_ready")
        st_ready = m.sem("a0_st_ready")
        st_free = m.sem("a0_st_free")
        hi_ready = m.sem("a0_hi_ready")
        lo_ready = m.sem("a0_lo_ready")
        pv_done = m.sem("a0_pv_done")
        o_free = m.sem("a0_o_free")
        r_ready = m.sem("a0_r_ready")
        block = ctx.enter_context(nc.Block())
        block.sync(loads)

        @block.tensor
        def _(pe):
            def scores(kk, c, u):
                n = kk * 4 + c
                pe.wait_ge(smax_free, n * 2 + (u + 1))
                for i in (2 * u, 2 * u + 1):
                    w = 5 * BLK if u == 0 else S
                    ins = nc.tensor.matmul(smax[:, i % 2, 0:w], q4[:, kk, i * P:(i + 1) * P],
                                           kz[:, n, 0:w], start=True, stop=True)
                if u == 0:
                    ins = nc.tensor.matmul(smax[:, 0, 5 * BLK:5 * BLK + 1],
                                           q4[:, kk, 3 * P:4 * P], kz[:, n, S:S + 1],
                                           start=True, stop=True)
                ins.then_inc(smax_ready, 1)

            def transposed(kk, c, u):
                n = kk * 4 + c
                pe.wait_ge(st_free, n * 3 + (u + 1))
                bank = (3 * c + u) % 4
                for ch in ((0,), (1,), (2, 3, 4))[u]:
                    col = BASE[ch] - BASE[2] if u == 2 else 0
                    first = FIRST[ch]
                    keys = slice(ch * P, (ch + 1) * P)
                    nc.tensor.matmul(st[:, bank, col:col + WIDTH[ch]], kz[:, n, keys],
                                     q4[:, kk, first - 1:S], start=True, stop=False)
                    if ch < 4:
                        w = P * ch + BLK - first
                        nc.tensor.matmul(st[:, bank, col:col + w], k["mask_keys"][:, 0, :],
                                         k["mask_cols"][:, 0:w], start=False, stop=False)
                    else:
                        nc.tensor.matmul(st[:, bank, col:col + 1], k["mask_keys"][:, 1, :],
                                         k["mask_cols"][:, 0:1], start=False, stop=False)
                    for i in range(max(ch - 1, 0), TPB):
                        lo = max(first - 1, i * P)
                        at = col + lo - (first - 1)
                        w = (i + 1) * P - lo
                        ins = nc.tensor.matmul(st[:, bank, at:at + w],
                                               mx[:, c % 2, i:i + 1].to_broadcast([P, P]),
                                               k["neg_id16"][:, P - w:P],
                                               start=False, stop=i == TPB - 1)
                ins.then_inc(st_ready, 1)

            def weighted(kk, c):
                n = kk * 4 + c
                pe.wait_ge(hi_ready, n + 1)
                pe.wait_ge(lo_ready, n + 3)
                if c % 2 == 0:
                    pe.wait_ge(o_free, kk * 2 + (c // 2 + 1))
                for qi, (q0, cnt) in enumerate(QT):
                    out = (c % 2) * 64 + qi * (D0 + 1)
                    for ch in range(qi + 1):
                        a = BASE[ch] + q0 - FIRST[ch]
                        ob = o[0:cnt, c // 2, out:out + D0 + 1]
                        nc.tensor.matmul(ob, pl[:, c % 2, a:a + cnt], v0[:, n, ch, 0:D0 + 1],
                                         start=ch == 0, stop=False)
                        nc.tensor.matmul(ob[:, 0:D0], ph[:, c % 2, a:a + cnt],
                                         v0[:, n, ch, D0 + 1:2 * D0 + 1], start=False, stop=False)
                        ins = nc.tensor.matmul(ob, ph[:, c % 2, a:a + cnt],
                                               v0[:, n, ch, 0:D0 + 1], start=False, stop=ch == qi)
                ins.then_inc(pv_done, 1)

            pe.sem_inc(pv_done, 2)
            pe.wait_ge(preset, 1)
            scores(0, 0, 0)
            scores(0, 0, 1)

            def slot(kk, c, first, final):
                nk, nx = (kk, c + 1) if c < 3 else (kk + 1, 0)
                pk, pc = (kk, c - 1) if c > 0 else (kk - 1, 3)
                if not final:
                    scores(nk, nx, 0)
                pe.wait_ge(mx_ready, kk * 4 + (c + 1))
                transposed(kk, c, 0)
                transposed(kk, c, 1)
                if not final:
                    scores(nk, nx, 1)
                transposed(kk, c, 2)
                if not first:
                    weighted(pk, pc)

            by_groups(pe, NG, slot)
            weighted(NG - 1, 3)

        @block.vector
        def _(dve):
            dve.sem_inc(smax_free, 1)
            dve.sem_inc(o_free, 2)
            nc.vector.memset(bm[:], 0.0)
            nc.vector.memset(o[:], 1.0).then_inc(preset, 1)
            dve.wait_ge(preset, 1)

            def maxima(kk, c):
                n = kk * 4 + c
                dve.wait_ge(smax_ready, n * 2 + 1)
                nc.vector.tensor_copy(bm[:, TPB - 1, NBLK - 1:NBLK],
                                      smax[:, 0, 5 * BLK:5 * BLK + 1])
                nc.vector.reduce_max(bm[:, 0:2, 0:5], smax[:, :, 0:5 * BLK].rearrange(
                    "p t (a b) -> p t a b", b=BLK), AXX).then_inc(smax_free, 1)
                dve.wait_ge(smax_ready, n * 2 + 2)
                nc.vector.reduce_max(bm[:, 2:4, 0:8], smax[:, :, :].rearrange(
                    "p t (a b) -> p t a b", b=BLK), AXX).then_inc(smax_free, 1)
                dve.wait_ge(smax_free, n * 2 + 3)
                nc.vector.tensor_tensor(bmm[:], bm[:], k["block_mask"], ALU.add
                                        ).then_inc(bm_ready, 1)
                dve.wait_ge(bm_ready, n + 1)
                nc.vector.reduce_max(mx[:, c % 2, :], bmm[:], AXX).then_inc(mx_ready, 1)

            def normalise(kk, c):
                n = kk * 4 + c
                dve.wait_ge(pv_done, n + 3)
                ob = o[:, c // 2, 0:128].rearrange("p (h x) -> p h x", h=2)[:, :, 0:5 * (D0 + 1)]
                ob = ob.rearrange("p h (t d) -> p h t d", d=D0 + 1)
                nc.vector.reciprocal(r[:, c // 2], ob[:, :, :, D0]).then_inc(r_ready, 1)
                dve.wait_ge(r_ready, kk * 2 + (c // 2 + 1))
                for e in range(2):
                    ins = nc.vector.tensor_tensor(
                        z0[:, :, kk * 4 + (c - 1 + e), :], ob[:, e, :, 0:D0],
                        r[:, c // 2, e, :].unsqueeze(2).to_broadcast([P, 5, D0]), ALU.mult)
                ins.then_inc(o_free, 1)

            maxima(0, 0)

            def slot(kk, c, first, final):
                if not final:
                    maxima(*((kk, c + 1) if c < 3 else (kk + 1, 0)))
                if c % 2 == 0 and not first:
                    normalise(*((kk, c - 1) if c > 0 else (kk - 1, 3)))

            by_groups(dve, NG, slot)
            normalise(NG - 1, 3)

        @block.scalar
        def _(act):
            act.sem_inc(st_free, 4)
            act.preload_act_table(ACT.Exp)

            def slot(kk, c, first, final):
                n = kk * 4 + c
                act.wait_ge(lo_ready, n + 1)
                act.wait_ge(pv_done, n + 1)
                for u in range(3):
                    a, w = BASE[u], (PW - BASE[2] if u == 2 else WIDTH[u])
                    act.wait_ge(st_ready, n * 3 + (u + 1))
                    nc.scalar.activation(p32[:, c % 2, a:a + w], st[:, (3 * c + u) % 4, 0:w],
                                         ACT.Exp, scale=scale).then_inc(st_free, 1)
                act.wait_ge(st_free, n * 3 + 7)
                nc.scalar.activation(ph[:, c % 2, :], p32[:, c % 2, :], ACT.Copy
                                     ).then_inc(hi_ready, 1)

            by_groups(act, NG, slot)

        @block.gpsimd
        def _(pool):
            pool.sem_inc(lo_ready, 2)

            def slot(kk, c, first, final):
                n = kk * 4 + c
                pool.wait_ge(hi_ready, n + 1)
                pool.wait_ge(pv_done, n + 1)
                nc.gpsimd.tensor_tensor(pl[:, c % 2, :], p32[:, c % 2, :], ph[:, c % 2, :],
                                        ALU.subtract).then_inc(lo_ready, 1)

            by_groups(pool, NG, slot)


def out0_phase(nc, k, z0, w, s):
    with ExitStack() as ctx:
        m = Mem(nc, ctx)
        zt = m.ps("o0_zt", [P, 2, S])
        out = m.ps("o0_out", [P, 2, S])
        zts = m.sb("o0_zts", [P, 2, S])
        zt_ready = m.sem("o0_zt_ready")
        zts_ready = m.sem("o0_zts_ready")
        out_ready = m.sem("o0_out_ready")
        s_ready = m.sem("o0_s_ready")
        block = ctx.enter_context(nc.Block())

        @block.tensor
        def _(pe):
            def turn(b):
                for qi, (q0, cnt) in enumerate(QT):
                    ins = nc.tensor.transpose(zt[:, b % 2, q0 - 1:q0 - 1 + cnt],
                                              z0[0:cnt, qi, b * H:(b + 1) * H, :],
                                              k["id"][0:cnt, 0:cnt])
                ins.then_inc(zt_ready, 1)

            turn(0)
            turn(1)
            for b in range(B):
                pe.wait_ge(zts_ready, b + 1)
                if b >= 2:
                    pe.wait_ge(s_ready, b - 1)
                for i in range(TPB):
                    ins = nc.tensor.matmul(out[:, b % 2, i * C:(i + 1) * C],
                                           zts[:, b % 2, i * P:(i + 1) * P], w["proj0"][:],
                                           start=True, stop=True)
                ins.then_inc(out_ready, 1)
                if b + 2 < B:
                    turn(b + 2)

        @block.scalar
        def _(act):
            for b in range(B):
                act.wait_ge(zt_ready, b + 1)
                if b >= 2:
                    act.wait_ge(out_ready, b - 1)
                nc.scalar.activation(zts[:, b % 2, :], zt[:, b % 2, :], ACT.Copy
                                     ).then_inc(zts_ready, 1)

        @block.vector
        def _(dve):
            for b in range(B):
                dve.wait_ge(out_ready, b + 1)
                nc.vector.tensor_tensor(
                    s[:, b * TPB:(b + 1) * TPB, :],
                    out[:, b % 2, :].rearrange("p (t c) -> p t c", t=TPB),
                    w["proj0_b"][:].unsqueeze(1).to_broadcast([P, TPB, C]), ALU.add
                    ).then_inc(s_ready, 1)


def router_phase(nc, k, tag, xh, xl, off, w, cw, acc, n_routed, n_all, top,
                 loads=None):
    spare = 8 - top
    wide = n_routed + spare
    with ExitStack() as ctx:
        m = Mem(nc, ctx)
        rwh = m.sb(f"{tag}_rwh", [P, n_routed], F16)
        rwl = m.sb(f"{tag}_rwl", [P, n_routed], F16)
        lg = m.ps(f"{tag}_lg", [P, NT, n_routed])
        ct = m.ps(f"{tag}_ct", [n_all, B, S])
        ob = m.ps(f"{tag}_ob", [P, 2, S])
        cts = m.sb(f"{tag}_cts", [n_all, B, S])
        e = m.sb(f"{tag}_e", [P, NT, n_routed])
        red = m.sb(f"{tag}_red", [P, NT])
        row = m.sb(f"{tag}_row", [P, NT, wide])
        rest = m.sb(f"{tag}_rest", [P, NT, wide])
        top8 = m.sb(f"{tag}_top8", [P, NT, 8])
        chain = m.sem(f"{tag}_chain")
        rw_ready = m.sem(f"{tag}_rw_ready")
        lg_ready = m.sem(f"{tag}_lg_ready")
        shifted = m.sem(f"{tag}_shifted")
        exp_ready = m.sem(f"{tag}_exp_ready")
        cw_ready = m.sem(f"{tag}_cw_ready")
        ct_ready = m.sem(f"{tag}_ct_ready")
        cts_ready = m.sem(f"{tag}_cts_ready")
        ob_ready = m.sem(f"{tag}_ob_ready")
        ob_free = m.sem(f"{tag}_ob_free")
        block = ctx.enter_context(nc.Block())
        if loads is not None:
            block.sync(loads)

        @block.vector
        def _(dve):
            link = own_chain(dve, chain)
            link(nc.vector.tensor_copy(rwh[:], w["router"][:]))
            nc.vector.tensor_tensor(rwl[:], w["router"][:], rwh[:], ALU.subtract
                                    ).then_inc(rw_ready, 1)
            for i in range(spare):
                nc.vector.memset(row[:, :, n_routed + i:n_routed + i + 1], 2.0 + i)
            if n_all > n_routed:
                nc.vector.memset(cw[:, :, n_routed:n_all], 1.0)
            dve.wait_ge(lg_ready, 1)
            link(nc.vector.tensor_tensor(e[:], lg[:], w["router_b"][:].unsqueeze(1).to_broadcast(
                [P, NT, n_routed]), ALU.add))
            link(nc.vector.reduce_max(red[:], e[:], AXX))
            nc.vector.tensor_tensor(e[:], e[:], red[:].unsqueeze(2).to_broadcast(
                [P, NT, n_routed]), ALU.subtract).then_inc(shifted, 1)
            dve.wait_ge(exp_ready, 1)
            link(nc.vector.reduce_sum(red[:], e[:], AXX))
            link(nc.vector.reciprocal(red[:], red[:]))
            link(nc.vector.tensor_tensor(row[:, :, 0:n_routed], e[:], red[:].unsqueeze(2)
                                         .to_broadcast([P, NT, n_routed]), ALU.mult))
            for t in range(NT):
                ins = nc.vector.max(top8[:, t, :], row[:, t, :])
            link(ins)
            for t in range(NT):
                ins = nc.vector.match_replace(rest[:, t, :], top8[:, t, :], row[:, t, :], 0.0)
            link(ins)
            nc.vector.tensor_tensor(cw[:, :, 0:n_routed], row[:, :, 0:n_routed],
                                    rest[:, :, 0:n_routed], ALU.subtract).then_inc(cw_ready, 1)
            for b in range(B):
                dve.wait_ge(ob_ready, b + 1)
                nc.vector.tensor_copy(acc[:, b * TPB:(b + 1) * TPB, :],
                                      ob[:, b % 2, :].rearrange("p (t c) -> p t c", t=TPB)
                                      ).then_inc(ob_free, 1)

        @block.scalar
        def _(act):
            act.wait_ge(shifted, 1)
            nc.scalar.activation(e[:], e[:], ACT.Exp).then_inc(exp_ready, 1)
            for b in range(B):
                act.wait_ge(ct_ready, b + 1)
                nc.scalar.activation(cts[:, b, :], ct[:, b, :], ACT.Copy).then_inc(cts_ready, 1)

        @block.tensor
        def _(pe):
            pe.wait_ge(rw_ready, 1)
            for t in range(NT):
                b, a = t // TPB, off + (t % TPB) * P
                ins = three_passes(nc, lg[:, t, :], xh[:, b, a:a + P], xl[:, b, a:a + P],
                                   rwh[:], rwl[:])
            ins.then_inc(lg_ready, 1)
            pe.wait_ge(cw_ready, 1)
            for t in range(NT):
                ins = nc.tensor.transpose(ct[:, t // TPB, (t % TPB) * P:(t % TPB + 1) * P],
                                          cw[:, t, :], k["id"][:])
                if t % TPB == TPB - 1:
                    ins.then_inc(ct_ready, 1)
            for b in range(B):
                pe.wait_ge(cts_ready, b + 1)
                if b >= 2:
                    pe.wait_ge(ob_free, b - 1)
                for i in range(TPB):
                    ins = nc.tensor.matmul(ob[:, b % 2, i * C:(i + 1) * C],
                                           cts[:, b, i * P:(i + 1) * P], w["out_b"][:],
                                           start=True, stop=True)
                ins.then_inc(ob_ready, 1)


def experts0_phase(nc, k, xh, xl, w, cw, acc):
    U = 2 * B
    NB = 4
    with ExitStack() as ctx:
        m = Mem(nc, ctx)
        wh = m.sb("e0_wh", [P, E0, 2 * I0], F16)
        wl = m.sb("e0_wl", [P, E0, 2 * I0], F16)
        upb = m.sb("e0_upb", [P, E0, 2])
        gate = m.sb("e0_gate", [P, NB, S])
        sig = m.sb("e0_sig", [P, NB, S])
        up = m.sb("e0_up", [P, NB, S])
        gs = m.sb("e0_gs", [P, NB, S])
        hid = m.sb("e0_hid", [P, NB, S])
        gu = m.ps("e0_gu", [P, 2, 2, S])
        out = m.ps("e0_out", [P, 4, S])
        w_ready = m.sem("e0_w_ready")
        gate_made = m.sem("e0_gate_made")
        up_made = m.sem("e0_up_made")
        gate_ready = m.sem("e0_gate_ready")
        up_ready = m.sem("e0_up_ready")
        sig_ready = m.sem("e0_sig_ready")
        clip_ready = m.sem("e0_clip_ready")
        gs_ready = m.sem("e0_gs_ready")
        hid_ready = m.sem("e0_hid_ready")
        out_ready = m.sem("e0_out_ready")
        out_free = m.sem("e0_out_free")
        passed = m.sem("e0_passed")
        block = ctx.enter_context(nc.Block())

        @block.gpsimd
        def _(pool):
            pool.sem_inc(gs_ready, 4)

            def slot(e, u, first, final):
                pool.wait_ge(sig_ready, e * U + (u + 1))
                nc.gpsimd.tensor_tensor(gs[:, u % NB, :], gate[:, u % NB, :], sig[:, u % NB, :],
                                        ALU.mult).then_inc(gs_ready, 1)

            by_groups(pool, E0, slot, U)

        @block.scalar
        def _(act):
            act.sem_inc(up_ready, 2)
            act.preload_act_table(ACT.Sigmoid)
            act.wait_ge(w_ready, 2)

            def slot(e, u, first, final):
                n1 = e * U + (u + 1)
                act.wait_ge(up_made, n1)
                act.wait_ge(hid_ready, n1)
                act.sem_inc(passed, 1)
                nc.scalar.activation(up[:, u % NB, :], gu[:, u % 2, 1, :], ACT.Identity,
                                     bias=upb[:, e, u % 2:u % 2 + 1]).then_inc(up_ready, 1)
                act.wait_ge(gate_ready, e * U + (u + 3))
                act.wait_ge(gs_ready, n1)
                nc.scalar.activation(sig[:, u % NB, :], gate[:, u % NB, :], ACT.Sigmoid,
                                     scale=ALPHA).then_inc(sig_ready, 1)

            by_groups(act, E0, slot, U)

        @block.vector
        def _(dve):
            dve.sem_inc(gate_ready, 2)
            dve.sem_inc(hid_ready, 4)
            dve.sem_inc(out_free, 4)
            nc.vector.tensor_scalar_add(upb[:], w["gu_b"][:, :, 2:4], 1.0)
            nc.vector.tensor_copy(wh[:], w["gu"][:]).then_inc(w_ready, 1)
            dve.wait_ge(w_ready, 1)
            nc.vector.tensor_tensor(wl[:], w["gu"][:], wh[:], ALU.subtract).then_inc(w_ready, 1)

            def product(e, u):
                dve.wait_ge(clip_ready, e * U + (u + 1))
                dve.wait_ge(gs_ready, e * U + (u + 5))
                dve.wait_ge(out_ready, e * (U // 2) + (u // 2 + 1))
                nc.vector.tensor_tensor(hid[:, u % NB, :], up[:, u % NB, :], gs[:, u % NB, :],
                                        ALU.mult).then_inc(hid_ready, 1)

            def accumulate(e, b):
                g = e * B + b
                dve.wait_ge(out_ready, g + 3)
                dve.wait_ge(out_free, g + 1)
                for i in range(TPB):
                    t = b * TPB + i
                    ins = nc.vector.scalar_tensor_tensor(
                        acc[:, t, :], out[:, b % 4, i * C:(i + 1) * C], cw[:, t, bass.ds(e, 1)],
                        acc[:, t, :], ALU.mult, ALU.add)
                ins.then_inc(out_free, 1)

            def slot(e, u, first, final):
                dve.wait_ge(gate_made, e * U + (u + 1))
                nc.vector.tensor_scalar(gate[:, u % NB, :], gu[:, u % 2, 0, :],
                                        w["gu_b"][:, e, u % 2:u % 2 + 1], LIMIT, ALU.add, ALU.min
                                        ).then_inc(gate_ready, 1)
                dve.wait_ge(up_ready, e * U + (u + 3))
                nc.vector.tensor_scalar(up[:, u % NB, :], up[:, u % NB, :], LIMIT + 1.0,
                                        1.0 - LIMIT, ALU.min, ALU.max).then_inc(clip_ready, 1)
                if not first:
                    product(*shift(e, u, -1, U))
                if u % 2 == 0:
                    ge, gb = shift(e, u // 2, -2, B)
                    if not (isinstance(ge, int) and ge < 0):
                        accumulate(ge, gb)

            by_groups(dve, E0, slot, U)
            product(E0 - 1, U - 1)
            accumulate(E0 - 1, B - 2)
            accumulate(E0 - 1, B - 1)

        @block.tensor
        def _(pe):
            pe.sem_inc(out_ready, 2)
            pe.wait_ge(w_ready, 2)

            def down(e, b):
                g = e * B + b
                pe.wait_ge(hid_ready, e * U + (2 * b + 6))
                pe.wait_ge(out_free, g + 1)
                for i in range(TPB):
                    for half in range(2):
                        ins = nc.tensor.matmul(out[:, b % 4, i * C:(i + 1) * C],
                                               hid[:, (2 * b + half) % NB, i * P:(i + 1) * P],
                                               w["down"][:, e, half, :],
                                               start=half == 0, stop=half == 1)
                ins.then_inc(out_ready, 1)

            def slot(e, u, first, final):
                b, half = u // 2, u % 2
                pe.wait_ge(gate_ready, e * U + (u + 1))
                pe.wait_ge(up_ready, e * U + (u + 1))
                for s, made in ((0, gate_made), (1, up_made)):
                    rows = slice(s * I0 + half * P, s * I0 + (half + 1) * P)
                    three_passes(nc, gu[:, u % 2, s, :], wh[:, e, rows], wl[:, e, rows],
                                 xh[:, b, 1:1 + S], xl[:, b, 1:1 + S]).then_inc(made, 1)
                if half == 1:
                    ge, gb = shift(e, b, -1, B)
                    if not (isinstance(ge, int) and ge < 0):
                        down(ge, gb)

            by_groups(pe, E0, slot, U)
            down(E0 - 1, B - 1)


def experts1_phase(nc, k, xh, xl, w, cw, acc):
    with ExitStack() as ctx:
        m = Mem(nc, ctx)
        wh = m.sb("e1_wh", [P, NE1, C], F16)
        wl = m.sb("e1_wl", [P, NE1, C], F16)
        hid = m.sb("e1_hid", [P, 4, S])
        a = m.ps("e1_a", [P, 4, S])
        out = m.ps("e1_out", [P, 4, S])
        w_ready = m.sem("e1_w_ready")
        a_ready = m.sem("e1_a_ready")
        hid_ready = m.sem("e1_hid_ready")
        out_ready = m.sem("e1_out_ready")
        out_free = m.sem("e1_out_free")
        passed = m.sem("e1_passed")
        block = ctx.enter_context(nc.Block())

        @block.scalar
        def _(act):
            act.sem_inc(hid_ready, 4)
            act.preload_act_table(ACT.Relu)

            def slot(e, b, first, final):
                n = e * B + b
                act.wait_ge(a_ready, n + 1)
                act.wait_ge(out_ready, n + 1)
                act.sem_inc(passed, 1)
                nc.scalar.activation(hid[:, b, :], a[:, b, :], ACT.Relu,
                                     bias=w["e1_b"][:, bass.ds(e, 1)]).then_inc(hid_ready, 1)

            by_groups(act, NE1, slot)

        @block.vector
        def _(dve):
            dve.sem_inc(out_free, 4)
            nc.vector.tensor_copy(wh[:], w["e1_w1"][:]).then_inc(w_ready, 1)
            dve.wait_ge(w_ready, 1)
            nc.vector.tensor_tensor(wl[:], w["e1_w1"][:], wh[:], ALU.subtract).then_inc(w_ready, 1)

            def slot(e, b, first, final):
                n = e * B + b
                dve.wait_ge(out_ready, n + 5)
                dve.wait_ge(out_free, n + 1)
                for i in range(TPB):
                    t = b * TPB + i
                    ins = nc.vector.scalar_tensor_tensor(
                        acc[:, t, :], out[:, b, i * C:(i + 1) * C], cw[:, t, bass.ds(e, 1)],
                        acc[:, t, :], ALU.mult, ALU.add)
                ins.then_inc(out_free, 1)

            by_groups(dve, NE1, slot)

        @block.tensor
        def _(pe):
            pe.sem_inc(out_ready, 4)
            pe.wait_ge(w_ready, 2)

            def down(e, b):
                n = e * B + b
                pe.wait_ge(hid_ready, n + 5)
                pe.wait_ge(out_free, n + 1)
                for i in range(TPB):
                    ins = nc.tensor.matmul(out[:, b, i * C:(i + 1) * C],
                                           hid[:, b, i * P:(i + 1) * P], w["e1_w2"][:, e, :],
                                           start=True, stop=True)
                ins.then_inc(out_ready, 1)

            def slot(e, b, first, final):
                n = e * B + b
                pe.wait_ge(hid_ready, n + 1)
                three_passes(nc, a[:, b, :], wh[:, e, :], wl[:, e, :],
                             xh[:, b, 1:1 + S], xl[:, b, 1:1 + S]).then_inc(a_ready, 1)
                de, db = shift(e, b, -2, B)
                if not (isinstance(de, int) and de < 0):
                    down(de, db)

            by_groups(pe, NE1, slot)
            down(NE1 - 1, B - 2)
            down(NE1 - 1, B - 1)


def update_phase(nc, tag, x, s, acc, out_dram=None):
    with ExitStack() as ctx:
        m = Mem(nc, ctx)
        sig = m.sb(f"{tag}_sig", [P, NT, C])
        sig_ready = m.sem(f"{tag}_sig_ready")
        prod_ready = m.sem(f"{tag}_prod_ready")
        gated = m.sem(f"{tag}_gated")
        x_ready = m.sem(f"{tag}_x_ready")
        stored = m.sem(f"{tag}_stored")
        block = ctx.enter_context(nc.Block())
        part = lambda t, b: t[:, b * TPB:(b + 1) * TPB, :]

        @block.scalar
        def _(act):
            for b in range(B):
                nc.scalar.activation(part(sig, b), part(acc, b), ACT.Sigmoid
                                     ).then_inc(sig_ready, 1)

        @block.gpsimd
        def _(pool):
            for b in range(B):
                nc.gpsimd.tensor_tensor(part(s, b), part(s, b), part(acc, b), ALU.mult
                                        ).then_inc(prod_ready, 1)

        @block.vector
        def _(dve):
            for b in range(B):
                dve.wait_ge(sig_ready, b + 1)
                dve.wait_ge(prod_ready, b + 1)
                nc.vector.tensor_tensor(part(s, b), part(s, b), part(sig, b), ALU.mult
                                        ).then_inc(gated, 1)
                dve.wait_ge(gated, b + 1)
                nc.vector.tensor_tensor(part(x, b), part(x, b), part(s, b), ALU.add
                                        ).then_inc(x_ready, 1)

        if out_dram is not None:
            @block.sync
            def _(sp):
                for b in range(B):
                    sp.wait_ge(x_ready, b + 1)
                    sp.dma_start(out_dram[b].rearrange("(t p) c -> p t c", p=P), part(x, b)
                                 ).then_inc(stored, 16)
                sp.wait_ge(stored, 16 * B)


def prepare1_phase(nc, k, rb_scratch, rb, han, wqk, wv, w):
    with ExitStack() as ctx:
        m = Mem(nc, ctx)
        tab = m.sb("r1_tab", [H, 2, 3 * P])
        parts = m.sb("r1_parts", [H, 3, 3 * P], F16)
        chain = m.sem("r1_chain")
        parts_ready = m.sem("r1_parts_ready")
        saved = m.sem("r1_saved")
        loaded = m.sem("r1_loaded")
        block = ctx.enter_context(nc.Block())

        @block.vector
        def _(dve):
            link = own_chain(dve, chain)
            link(nc.vector.memset(tab[:], 0.0))
            nc.vector.tensor_scalar(tab[:, 0, P:P + 255], rb[:, 0, :], rb[:, 0, 0:1], None,
                                    ALU.subtract)
            link(nc.vector.tensor_scalar(tab[:, 1, 0:255], rb[:, 1, :], rb[:, 0, 0:1], None,
                                         ALU.subtract))
            nc.vector.tensor_copy(parts[:, 0, :], tab[:, 0, :])
            link(nc.vector.tensor_copy(parts[:, 2, :], tab[:, 1, :]))
            nc.vector.tensor_tensor(parts[:, 1, :], tab[:, 0, :], parts[:, 0, :], ALU.subtract
                                    ).then_inc(parts_ready, 1)
            for s in range(2):
                nc.vector.tensor_copy(wqk[:, 0, s], w["qk1"][:, s])
            link(nc.vector.tensor_copy(wv[:, 0, :], w["v1"][:]))
            for s in range(2):
                nc.vector.tensor_tensor(wqk[:, 1, s], w["qk1"][:, s], wqk[:, 0, s], ALU.subtract)
            nc.vector.tensor_tensor(wv[:, 1, :], w["v1"][:], wv[:, 0, :], ALU.subtract)

        @block.sync
        def _(sp):
            sp.wait_ge(parts_ready, 1)
            sp.dma_start(rb_scratch.rearrange("a h n -> h a n"), parts[:]).then_inc(saved, 16)
            sp.wait_ge(saved, 16)
            for a in range(3):
                src = bass.AP(rb_scratch.tensor, a * H * 3 * P, [[1, P], [3 * P, H], [1, 2 * P]])
                sp.dma_start(han[:, a], src).then_inc(loaded, 16)
            sp.wait_ge(loaded, 48)


def attention1_phase(nc, k, xh, xl, wqk, wv, han, z1, loads):
    DV = D1 + 1
    with ExitStack() as ctx:
        m = Mem(nc, ctx)
        smax = m.ps("a1_smax", [P, 2, S])
        st = m.ps("a1_st", [P, 2, 2, S])
        o = m.ps("a1_o", [P, S])
        pr = m.ps("a1_pr", [P, S])
        signed = m.sb("a1_signed", [P, S], F16)
        q1 = m.sb("a1_q1", [P, 4, S], F16)
        k1 = m.sb("a1_k1", [P, 4, S], F16)
        k2 = m.sb("a1_k2", [P, 4, S], F16)
        v1 = m.sb("a1_v1", [P, 4, TPB, 2 * D1 + 1], F16)
        mx = m.sb("a1_mx", [P, 2, TPB], F16)
        p32 = m.sb("a1_p32", [P, 2, TPB, S])
        ph = m.sb("a1_ph", [P, 2, TPB, S], F16)
        pl = m.sb("a1_pl", [P, 2, TPB, S], F16)
        r = m.sb("a1_r", [P, TPB])
        pr_ready = m.sem("a1_pr_ready")
        pr_hi = m.sem("a1_pr_hi")
        pr_free = m.sem("a1_pr_free")
        smax_ready = m.sem("a1_smax_ready")
        smax_free = m.sem("a1_smax_free")
        st_ready = m.sem("a1_st_ready")
        st_free = m.sem("a1_st_free")
        hi_ready = m.sem("a1_hi_ready")
        lo_ready = m.sem("a1_lo_ready")
        pv_done = m.sem("a1_pv_done")
        r_ready = m.sem("a1_r_ready")
        o_free = m.sem("a1_o_free")
        ones = m.sem("a1_ones")
        block = ctx.enter_context(nc.Block())
        block.sync(loads)

        @block.tensor
        def _(pe):
            def project(h, b, s):
                pe.wait_ge(pr_free, (h * B + b) * 3 + (s + 1))
                if s < 2:
                    ins = three_passes(nc, pr[:], wqk[:, 0, s, h, :], wqk[:, 1, s, h, :],
                                       xh[:, b, 1:1 + S], xl[:, b, 1:1 + S])
                else:
                    cols = bass.ds(h * D1, D1)
                    for t in range(TPB):
                        a = 1 + t * P
                        ins = three_passes(nc, pr[:, t * D1:(t + 1) * D1], xh[:, b, a:a + P],
                                           xl[:, b, a:a + P], wv[:, 0, cols], wv[:, 1, cols])
                ins.then_inc(pr_ready, 1)

            def scores(h, b, u):
                pe.wait_ge(smax_free, (h * B + b) * 2 + (u + 1))
                for i in (2 * u, 2 * u + 1):
                    ins = nc.tensor.matmul(smax[:, i % 2, :], q1[:, b, i * P:(i + 1) * P],
                                           k1[:, b, :], start=True, stop=i < 2)
                    if i >= 2:
                        ins = nc.tensor.matmul(smax[:, i % 2, 0:(i - 1) * P], k["anti16"],
                                               han[:, 2, h, (3 - i) * P:2 * P],
                                               start=False, stop=True)
                ins.then_inc(smax_ready, 1)

            def transposed(h, b, u):
                pe.wait_ge(st_free, (h * B + b) * 2 + (u + 1))
                if u == 0:
                    pe.wait_ge(smax_free, (h * B + b) * 2 + 3)
                for ch in (2 * u, 2 * u + 1):
                    ob = st[:, u, ch % 2, :]
                    keys = slice(ch * P, (ch + 1) * P)
                    nc.tensor.matmul(ob, k2[:, b, keys], q1[:, b, :], start=True, stop=False)
                    nc.tensor.matmul(ob, k1[:, b, keys], q1[:, b, :], start=False, stop=False)
                    for part in range(2 if ch < 2 else 0):
                        nc.tensor.matmul(ob[:, (2 + ch) * P:S], k["anti16"],
                                         han[:, part, h, 0:(2 - ch) * P], start=False, stop=False)
                    for i in range(TPB):
                        ins = nc.tensor.matmul(ob[:, i * P:(i + 1) * P],
                                               mx[:, b % 2, i:i + 1].to_broadcast([P, P]),
                                               k["neg_id16"], start=False, stop=i == TPB - 1)
                ins.then_inc(st_ready, 1)

            def weighted(h, b):
                n = h * B + b
                pe.wait_ge(o_free, n + 1)
                pe.wait_ge(lo_ready, n * 2 + 6)
                for i in range(TPB):
                    ob = o[:, i * DV:(i + 1) * DV]
                    for ch in range(TPB):
                        cols = slice(i * P, (i + 1) * P)
                        nc.tensor.matmul(ob, pl[:, b % 2, ch, cols], v1[:, b, ch, 0:DV],
                                         start=ch == 0, stop=False)
                        nc.tensor.matmul(ob[:, 0:D1], ph[:, b % 2, ch, cols],
                                         v1[:, b, ch, DV:], start=False, stop=False)
                        ins = nc.tensor.matmul(ob, ph[:, b % 2, ch, cols], v1[:, b, ch, 0:DV],
                                               start=False, stop=ch == TPB - 1)
                ins.then_inc(pv_done, 1)

            pe.sem_inc(pv_done, 2)
            pe.wait_ge(ones, 1)
            for b in range(2):
                for s in range(3):
                    project(0, b, s)
            scores(0, 0, 0)
            scores(0, 0, 1)

            def slot(h, b, first, final):
                last_two = isinstance(h, int) and h == H - 1 and b >= 2
                ahead = None if last_two else shift(h, b, 2)
                if ahead:
                    project(*ahead, 0)
                if not final:
                    scores(*shift(h, b, 1), 0)
                transposed(h, b, 0)
                if ahead:
                    project(*ahead, 1)
                if not final:
                    scores(*shift(h, b, 1), 1)
                transposed(h, b, 1)
                if ahead:
                    project(*ahead, 2)
                if not first:
                    weighted(*shift(h, b, -1))

            by_groups(pe, H, slot)
            weighted(H - 1, B - 1)

        @block.vector
        def _(dve):
            dve.sem_inc(pr_free, 1)
            dve.sem_inc(smax_free, 1)
            dve.sem_inc(o_free, 1)
            nc.vector.memset(v1[:, :, :, D1:DV], 1.0).then_inc(ones, 1)

            def low(h, b, s):
                dve.wait_ge(pr_hi, (h * B + b) * 3 + (s + 1))
                if s == 0:
                    ins = nc.vector.scalar_tensor_tensor(q1[:, b, :], pr[:], k["low_q1"],
                                                         signed[:], ALU.mult, ALU.subtract)
                elif s == 1:
                    ins = nc.vector.tensor_tensor(k2[:, b, :], pr[:], k1[:, b, :], ALU.subtract)
                else:
                    ins = nc.vector.tensor_tensor(
                        v1[:, b, :, DV:], pr[:, 0:TPB * D1].rearrange("p (t d) -> p t d", t=TPB),
                        v1[:, b, :, 0:D1], ALU.subtract)
                ins.then_inc(pr_free, 1)

            def maximum(h, b, u):
                dve.wait_ge(smax_ready, (h * B + b) * 2 + (u + 1))
                nc.vector.reduce_max(mx[:, b % 2, 2 * u:2 * u + 2], smax[:], AXX
                                     ).then_inc(smax_free, 1)

            def normalise(h, b):
                n = h * B + b
                dve.wait_ge(pv_done, n + 3)
                ob = o[:, 0:TPB * DV].rearrange("p (t d) -> p t d", t=TPB)
                nc.vector.reciprocal(r[:], ob[:, :, D1]).then_inc(r_ready, 1)
                dve.wait_ge(r_ready, n + 1)
                nc.vector.tensor_tensor(z1[:, b * TPB:(b + 1) * TPB, bass.ds(h * D1, D1)],
                                        ob[:, :, 0:D1],
                                        r[:].unsqueeze(2).to_broadcast([P, TPB, D1]), ALU.mult
                                        ).then_inc(o_free, 1)

            for b in range(2):
                for s in range(3):
                    low(0, b, s)
            maximum(0, 0, 0)
            maximum(0, 0, 1)

            def slot(h, b, first, final):
                last_two = isinstance(h, int) and h == H - 1 and b >= 2
                ahead = None if last_two else shift(h, b, 2)
                if ahead:
                    low(*ahead, 0)
                if not final:
                    maximum(*shift(h, b, 1), 0)
                if ahead:
                    low(*ahead, 1)
                if not final:
                    maximum(*shift(h, b, 1), 1)
                if ahead:
                    low(*ahead, 2)
                if not first:
                    normalise(*shift(h, b, -1))

            by_groups(dve, H, slot)
            normalise(H - 1, B - 1)

        @block.scalar
        def _(act):
            act.sem_inc(st_free, 2)
            act.preload_act_table(ACT.Exp)
            act.wait_ge(ones, 1)

            def high(h, b, s):
                act.wait_ge(pr_ready, (h * B + b) * 3 + (s + 1))
                if s == 0:
                    ins = nc.scalar.activation(signed[:], pr[:], ACT.Copy, scale=k["sign_q1"])
                elif s == 1:
                    ins = nc.scalar.activation(k1[:, b, :], pr[:], ACT.Copy)
                else:
                    ins = nc.scalar.activation(
                        v1[:, b, :, 0:D1], pr[:, 0:TPB * D1].rearrange("p (t d) -> p t d", t=TPB),
                        ACT.Copy)
                ins.then_inc(pr_hi, 1)

            def exponent(h, b, u):
                n = h * B + b
                act.wait_ge(st_ready, n * 2 + (u + 1))
                act.wait_ge(lo_ready, n * 2 + (u + 1))
                nc.scalar.activation(p32[:, b % 2, 2 * u:2 * u + 2, :], st[:, u, :, :], ACT.Exp
                                     ).then_inc(st_free, 1)
                act.wait_ge(st_free, n * 2 + (u + 3))
                act.wait_ge(pv_done, n + 1)
                nc.scalar.activation(ph[:, b % 2, 2 * u:2 * u + 2, :],
                                     p32[:, b % 2, 2 * u:2 * u + 2, :], ACT.Copy
                                     ).then_inc(hi_ready, 1)

            for b in range(2):
                for s in range(3):
                    high(0, b, s)

            def slot(h, b, first, final):
                last_two = isinstance(h, int) and h == H - 1 and b >= 2
                ahead = None if last_two else shift(h, b, 2)
                if ahead:
                    high(*ahead, 0)
                exponent(h, b, 0)
                if ahead:
                    high(*ahead, 1)
                exponent(h, b, 1)
                if ahead:
                    high(*ahead, 2)

            by_groups(act, H, slot)

        @block.gpsimd
        def _(pool):
            pool.sem_inc(lo_ready, 4)

            def slot(h, b, first, final):
                n = h * B + b
                for u in range(2):
                    half = slice(2 * u, 2 * u + 2)
                    pool.wait_ge(hi_ready, n * 2 + (u + 1))
                    pool.wait_ge(pv_done, n + 1)
                    nc.gpsimd.tensor_tensor(pl[:, b % 2, half, :], p32[:, b % 2, half, :],
                                            ph[:, b % 2, half, :], ALU.subtract
                                            ).then_inc(lo_ready, 1)

            by_groups(pool, H, slot)


def out1_phase(nc, k, z1, w, s):
    NK = H * D1 // P
    with ExitStack() as ctx:
        m = Mem(nc, ctx)
        zt = m.ps("o1_zt", [P, 2, NK, P])
        out = m.ps("o1_out", [P, 2, 512])
        zts = m.sb("o1_zts", [P, 2, NK, P])
        zt_ready = m.sem("o1_zt_ready")
        act_half = m.sem("o1_act_half")
        dve_half = m.sem("o1_dve_half")
        out_ready = m.sem("o1_out_ready")
        s_ready = m.sem("o1_s_ready")
        block = ctx.enter_context(nc.Block())
        half = NK // 2

        @block.tensor
        def _(pe):
            def turn(t):
                if t >= 2:
                    pe.wait_ge(act_half, t - 1)
                    pe.wait_ge(dve_half, t - 1)
                for c in range(NK):
                    ins = nc.tensor.transpose(zt[:, t % 2, c, :], z1[:, t, c * P:(c + 1) * P],
                                              k["id"])
                ins.then_inc(zt_ready, 1)

            turn(0)
            for t in range(NT):
                if t + 1 < NT:
                    turn(t + 1)
                pe.wait_ge(act_half, t + 1)
                pe.wait_ge(dve_half, t + 1)
                if t >= 2:
                    pe.wait_ge(s_ready, t - 1)
                for c in range(NK):
                    ins = nc.tensor.matmul(out[:, t % 2, 0:C], zts[:, t % 2, c, :],
                                           w["out1"][:, c, :], start=c == 0, stop=c == NK - 1)
                ins.then_inc(out_ready, 1)

        @block.scalar
        def _(act):
            for t in range(NT):
                act.wait_ge(zt_ready, t + 1)
                if t >= 2:
                    act.wait_ge(out_ready, t - 1)
                nc.scalar.activation(zts[:, t % 2, 0:half, :], zt[:, t % 2, 0:half, :], ACT.Copy
                                     ).then_inc(act_half, 1)

        @block.vector
        def _(dve):
            for t in range(NT):
                dve.wait_ge(zt_ready, t + 1)
                if t >= 2:
                    dve.wait_ge(out_ready, t - 1)
                nc.vector.tensor_copy(zts[:, t % 2, half:NK, :], zt[:, t % 2, half:NK, :]
                                      ).then_inc(dve_half, 1)
                if t >= 1:
                    dve.wait_ge(out_ready, t)
                    nc.vector.tensor_copy(s[:, t - 1, :], out[:, (t - 1) % 2, 0:C]
                                          ).then_inc(s_ready, 1)
            dve.wait_ge(out_ready, NT)
            nc.vector.tensor_copy(s[:, NT - 1, :], out[:, (NT - 1) % 2, 0:C]).then_inc(s_ready, 1)


CONSTS = [("id", P), ("neg_id", P), ("anti", P), ("mask_keys", 2 * P), ("mask_cols", BLK),
          ("block_mask", TPB * NBLK), ("low_q", 1), ("low_k", 1), ("sign_q", 1), ("sign_k", 1),
          ("own", G), ("low_q1", 1), ("sign_q1", 1)]


def program(nc, a, out, stop=99):
    with ExitStack() as ctx:
        m = Mem(nc, ctx)
        x = m.sb("x", [P, NT, C])
        s = m.sb("s", [P, NT, C])
        acc = m.sb("acc", [P, NT, C])
        xh = m.sb("xh", [P, B, S + 2], F16)
        xl = m.sb("xl", [P, B, S + 2], F16)
        cw = m.sb("cw", [P, NT, NE1])
        const = m.sb("const", [P, sum(n for _, n in CONSTS)])
        neg16 = m.sb("neg16", [P, P], F16)
        anti16 = m.sb("anti16", [P, P], F16)
        mask_keys = m.sb("mask_keys", [P, 2, P], BF16)
        mask_cols = m.sb("mask_cols", [P, BLK], BF16)
        glob = m.sb("glob", [P, 1])
        rb = m.sb("rb", [H, 2, 255])
        w = {
            "qk0": m.sb("w_qk0", [P, 2, 4, P]), "v0": m.sb("w_v0", [P, C]),
            "proj0": m.sb("w_proj0", [P, C]), "proj0_b": m.sb("w_proj0_b", [P, C]),
            "gu_b": m.sb("w_gu_b", [P, E0, 4]),
            "e1_b": m.sb("w_e1_b", [P, NE1]),
        }
        r0 = {"router": m.sb("r0_w", [P, E0]), "router_b": m.sb("r0_wb", [P, E0]),
              "out_b": m.sb("r0_ob", [E0, C])}
        r1 = {"router": m.sb("r1_w", [P, E1]), "router_b": m.sb("r1_wb", [P, E1]),
              "out_b": m.sb("r1_ob", [NE1, C])}
        k, at = {}, 0
        for name, n in CONSTS:
            k[name] = const[:, at:at + n]
            at += n
        k32 = dict(k)
        k["block_mask"] = k["block_mask"].rearrange("p (t b) -> p t b", t=TPB)
        k["neg_id16"], k["anti16"] = neg16[:], anti16[:]
        k["mask_keys"], k["mask_cols"] = mask_keys[:], mask_cols[:]

        first_loads = m.sem("first_loads")
        x_loads = m.sem("x_loads")
        more_loads = m.sem("more_loads")
        expert_loads = m.sem("expert_loads")
        late_loads = m.sem("late_loads")

        with nc.Block() as block:
            @block.sync
            def _(sp):
                for b in range(B):
                    sp.dma_start(x[:, b * TPB:(b + 1) * TPB, :],
                                 a["x"][b].rearrange("(t p) c -> p t c", p=P)).then_inc(x_loads, 16)
                sp.wait_ge(x_loads, 16 * B)

            @block.scalar
            def _(act):
                act.dma_start(const[:], a["const"]).then_inc(first_loads, 16)
                act.dma_start(glob[:], a["glob"]).then_inc(first_loads, 16)
                act.dma_start(w["qk0"][:], a["qk0"]).then_inc(first_loads, 16)
                act.dma_start(w["v0"][:], a["v0"]).then_inc(first_loads, 16)
                act.wait_ge(first_loads, 64)

        with nc.Block() as block:
            @block.vector
            def _(dve):
                nc.vector.tensor_copy(neg16[:], k32["neg_id"])
                nc.vector.tensor_copy(anti16[:], k32["anti"])
                nc.vector.tensor_copy(mask_cols[:], k32["mask_cols"])
                nc.vector.tensor_copy(mask_keys[:].rearrange("p a b -> p (a b)"),
                                      k32["mask_keys"])

        def loads1(sp):
            for dst, src in ((w["proj0"], "proj0"), (r0["router"], "router0"),
                             (r0["out_b"], "down_b"), (w["gu_b"], "gu_b"), (w["gu"], "gu"),
                             (w["down"], "down"), (r1["router"], "router1"),
                             (r1["out_b"], "e1_b2"), (w["e1_b"], "e1_b1"), (rb, "rb")):
                sp.dma_start(dst[:], a[src]).then_inc(more_loads, 16)
            for dst, src in ((w["proj0_b"], "proj0_b"), (r0["router_b"], "router0_b"),
                             (r1["router_b"], "router1_b")):
                sp.dma_start(dst[:], a[src].partition_broadcast(P)).then_inc(more_loads, 16)
            sp.wait_ge(more_loads, 13 * 16)

        def loads2(sp):
            sp.dma_start(w["qk1"][:], a["qk1"]).then_inc(expert_loads, 16)
            sp.dma_start(w["v1"][:], a["v1"]).then_inc(expert_loads, 16)
            sp.wait_ge(expert_loads, 32)

        def loads3(sp):
            sp.dma_start(w["out1"][:], a["out1"]).then_inc(late_loads, 16)
            sp.wait_ge(late_loads, 16)

        def loads4(sp):
            sp.dma_start(w["e1_w1"][:], a["e1_w1"]).then_inc(late_loads, 16)
            sp.dma_start(w["e1_w2"][:], a["e1_w2"]).then_inc(late_loads, 16)
            sp.wait_ge(late_loads, 48)

        layer_norm_phase(nc, "n0", x, xh, xl, k["id"], glob)
        with ExitStack() as ph:
            p = Mem(nc, ph)
            w["gu"] = p.sb("w_gu", [P, E0, 2 * I0])
            w["down"] = p.sb("w_down", [P, E0, 2, C])
            with ExitStack() as pa:
                q = Mem(nc, pa)
                z0 = q.sb("z0", [P, 5, NH, D0])
                q4 = q.sb("q4", [P, NG, S], F16)
                v0 = q.sb("v0", [P, NH, 5, 2 * D0 + 1], F16)
                with ExitStack() as pk:
                    kz = Mem(nc, pk).sb("kz", [P, NH, KPAD], F16)
                    project0_phase(nc, k, xh, xl, w, q4, kz, v0)
                    attention0_phase(nc, k, q4, kz, v0, z0, loads1)
                out0_phase(nc, k, z0, w, s)
            router_phase(nc, k, "g0", xh, xl, 1, r0, cw[:, :, 0:E0], acc, E0, E0, TOP0)
            experts0_phase(nc, k, xh, xl, w, cw, acc)
        update_phase(nc, "u0", x, s, acc)
        with ExitStack() as ph:
            p = Mem(nc, ph)
            w["out1"] = p.sb("w_out1", [P, H * D1 // P, C])
            wqk = p.sb("wqk1", [P, 2, 2, H, P], F16)
            wv = p.sb("wv1", [P, 2, H * D1], F16)
            han = p.sb("han", [P, 3, H, 2 * P], F16)
            with ExitStack() as pw:
                q = Mem(nc, pw)
                w["qk1"] = q.sb("w_qk1", [P, 2, H, P])
                w["v1"] = q.sb("w_v1", [P, H * D1])
                layer_norm_phase(nc, "n1", x, xh, xl, k["id"], None, loads2)
                prepare1_phase(nc, k, a["rb_scratch"], rb, han, wqk, wv, w)
            z1 = p.sb("z1", [P, NT, H * D1])
            attention1_phase(nc, k, xh, xl, wqk, wv, han, z1, loads3)
            out1_phase(nc, k, z1, w, s)
        w["e1_w1"] = m.sb("w_e1_w1", [P, NE1, C])
        w["e1_w2"] = m.sb("w_e1_w2", [P, NE1, C])
        router_phase(nc, k, "g1", xh, xl, 1, r1, cw, acc, E1, NE1, TOP1, loads4)
        experts1_phase(nc, k, xh, xl, w, cw, acc)
        update_phase(nc, "u1", x, s, acc, out)


def shape_constants():
    import numpy as np

    c = {name: np.zeros((P, n), np.float32) for name, n in CONSTS}
    row = np.arange(P)
    c["id"][row, row] = 1
    c["neg_id"][row, row] = -1
    c["anti"][row, P - 1 - row] = 1
    c["mask_keys"][0, BLK:P] = 1
    c["mask_keys"][0, P + 1:] = 1
    c["mask_cols"][0, :] = BIG
    for t in range(S):
        for blk in range(NBLK):
            if blk > (t + 1) // BLK:
                c["block_mask"][t % P, (t // P) * NBLK + blk] = BIG
    copy = row // D0 % 4
    c["low_q"][:, 0] = copy >= 2
    c["low_k"][:, 0] = copy % 2
    for s in "qk":
        c[f"sign_{s}"][:] = 2 * c[f"low_{s}"] - 1
    c["own"][row, row // 32] = 1
    c["low_q1"][:, 0] = (row >= D1) * D1 ** -0.5
    c["sign_q1"][:, 0] = np.where(row >= D1, 1, -1) * D1 ** -0.5
    return np.concatenate([c[name] for name, _ in CONSTS], axis=1)


def laid_out(i):
    import numpy as np

    a = {n: np.asarray(v) for n, v in i.items()}
    o = {"x": a["L0_attn_x"], "const": shape_constants()}
    o["glob"] = a["L0_attn_global_token"].reshape(C, 1)
    wt = a["L0_attn_qkv_w"].reshape(3, 4, G, 1, D0, C)
    o["qk0"] = np.repeat(wt[:2], 4, axis=3).reshape(2, 4, P, C).transpose(3, 0, 1, 2)
    o["v0"] = a["L0_attn_qkv_w"][2 * C:].T
    o["proj0"] = a["L0_attn_proj_w"].T
    o["proj0_b"] = a["L0_attn_proj_b"]
    o["router0"] = a["L0_ffn_router_weight"].T
    o["router0_b"] = a["L0_ffn_router_bias"]
    o["gu"] = a["L0_ffn_gate_up_proj"].transpose(1, 0, 2)
    o["gu_b"] = a["L0_ffn_gate_up_bias"].reshape(E0, 4, P).transpose(2, 0, 1)
    o["down"] = a["L0_ffn_down_proj"].reshape(E0, 2, P, C).transpose(2, 0, 1, 3)
    o["down_b"] = a["L0_ffn_down_bias"]
    wt = a["L1_attn_w_qkv"].reshape(D1, 3, H, C)
    qk = wt[:, :2].transpose(3, 1, 2, 0)
    o["qk1"] = np.concatenate([qk, qk], axis=3)
    o["v1"] = wt[:, 2].transpose(2, 1, 0).reshape(C, H * D1)
    o["out1"] = a["L1_attn_w_out"].T.reshape(H * D1 // P, P, C).transpose(1, 0, 2)
    rb = a["L1_attn_rel_bias"].T
    o["rb"] = np.stack([rb[:, ::-1], rb], axis=1)
    o["router1"] = a["L1_ffn_router_W"]
    o["router1_b"] = a["L1_ffn_router_b"]
    o["e1_w1"] = np.concatenate([a["L1_ffn_eW1"], a["L1_ffn_sW1"][None]]).transpose(1, 0, 2)
    o["e1_b1"] = np.concatenate([a["L1_ffn_eb1"], a["L1_ffn_sb1"][None]]).T
    o["e1_w2"] = np.concatenate([a["L1_ffn_eW2"], a["L1_ffn_sW2"][None]]).transpose(1, 0, 2)
    o["e1_b2"] = np.concatenate([a["L1_ffn_eb2"], a["L1_ffn_sb2"][None]])
    return {n: np.ascontiguousarray(v) for n, v in o.items()}


def kernel(**inputs):
    import concourse.bacc as bacc
    import numpy as np
    from concourse import mybir as mb
    from concourse.bass_utils import run_bass_kernel_spmd

    nc = bacc.Bacc("TRN2", target_bir_lowering=False, num_devices=1)
    arrays = laid_out(inputs)
    a = {n: nc.dram_tensor(f"in_{n}", v.shape, mb.dt.from_np(v.dtype), kind="ExternalInput").ap()
         for n, v in arrays.items()}
    a["rb_scratch"] = nc.dram_tensor("rb_scratch", (3, H, 3 * P), mb.dt.float16,
                                     kind="Internal").ap()
    out = nc.dram_tensor("out", (B, S, C), mb.dt.float32, kind="ExternalOutput").ap()
    program(nc, a, out)
    r = run_bass_kernel_spmd(nc, [{f"in_{n}": v for n, v in arrays.items()}], core_ids=[0])
    return r.results[0]["out"]
```

```python
from contextlib import ExitStack

import concourse.bass as bass
from concourse import mybir

P = 128
F32 = mybir.dt.float32
F16 = mybir.dt.float16
BF16 = mybir.dt.bfloat16
ALU = mybir.AluOpType
ACT = mybir.ActivationFunctionType
AXX = mybir.AxisListType.X

B, S, C = 4, 512, 128
TPB = S // P
NT = B * TPB
H = 16
D0, D1 = C // H, 64
NH = B * H
G = 4
NG = NH // G
BLK = 64
NBLK = S // BLK + 1
KPAD = 5 * P
E0, TOP0, I0 = 8, 2, 256
E1, TOP1 = 15, 3
NE1 = E1 + 1
ALPHA, LIMIT, EPS = 1.702, 7.0, 1e-5
BIG = -1.0e30

FIRST = [1, 128, 256, 384, 512]
WIDTH = [513 - f for f in FIRST]
BASE = [0, WIDTH[0], WIDTH[0] + WIDTH[1], sum(WIDTH[:3]), sum(WIDTH[:4])]
PW = sum(WIDTH)
QT = [(1, 127), (128, 128), (256, 128), (384, 128), (512, 1)]


class Mem:

    def __init__(self, nc, ctx):
        self.nc, self.ctx = nc, ctx

    def sb(self, name, shape, dt=F32):
        return self.ctx.enter_context(self.nc.sbuf_tensor(name, shape, dt))

    def ps(self, name, shape, dt=F32):
        return self.ctx.enter_context(self.nc.psum_tensor(name, shape, dt))

    def sem(self, name):
        return self.ctx.enter_context(self.nc.semaphore(name))


def own_chain(eng, sem):
    count = [0]

    def link(ins):
        count[0] += 1
        ins.then_inc(sem, 1)
        eng.wait_ge(sem, count[0])

    return link


def three_passes(nc, out, wh, wl, xh, xl):
    nc.tensor.matmul(out, wh, xl, start=True, stop=False)
    nc.tensor.matmul(out, wl, xh, start=False, stop=False)
    return nc.tensor.matmul(out, wh, xh, start=False, stop=True)


def layer_norm_phase(nc, tag, x, xh, xl, ident, glob, loads=None):
    with ExitStack() as ctx:
        m = Mem(nc, ctx)
        stats = m.sb(f"{tag}_stats", [P, NT, 6])
        mv = m.sb(f"{tag}_mv", [P, NT, 2])
        rstd = m.sb(f"{tag}_rstd", [P, NT])
        xn = m.sb(f"{tag}_xn", [P, NT, C])
        xt = m.ps(f"{tag}_xt", [P, B, S])
        chain = m.sem(f"{tag}_chain")
        var_ready = m.sem(f"{tag}_var")
        std_ready = m.sem(f"{tag}_std")
        xn_ready = m.sem(f"{tag}_xn_ready")
        xt_ready = m.sem(f"{tag}_xt_ready")
        hi_ready = m.sem(f"{tag}_hi_ready")
        block = ctx.enter_context(nc.Block())
        if loads is not None:
            block.sync(loads)

        @block.vector
        def _(dve):
            link = own_chain(dve, chain)
            for t in range(NT):
                ins = nc.vector.bn_stats(stats[:, t, :], x[:, t, :])
            link(ins)
            for t in range(NT):
                ins = nc.vector.bn_aggr(mv[:, t, :], stats[:, t, :])
            link(ins)
            nc.vector.tensor_scalar_add(rstd[:], mv[:, :, 1], EPS).then_inc(var_ready, 1)
            dve.wait_ge(std_ready, 1)
            link(nc.vector.reciprocal(rstd[:], rstd[:]))
            for t in range(NT):
                nc.vector.tensor_scalar(xn[:, t, :], x[:, t, :], mv[:, t, 0:1], rstd[:, t:t + 1],
                                        ALU.subtract, ALU.mult).then_inc(xn_ready, 1)
            for b in range(B):
                dve.wait_ge(hi_ready, b + 1)
                nc.vector.tensor_tensor(xl[:, b, 1:1 + S], xt[:, b, :], xh[:, b, 1:1 + S],
                                        ALU.subtract)
            if glob is not None:
                for b in range(B):
                    ins = nc.vector.tensor_copy(xh[:, b, 0:1], glob[:])
                link(ins)
                for b in range(B):
                    nc.vector.tensor_tensor(xl[:, b, 0:1], glob[:], xh[:, 0, 0:1], ALU.subtract)

        @block.scalar
        def _(act):
            act.wait_ge(var_ready, 1)
            nc.scalar.activation(rstd[:], rstd[:], ACT.Sqrt).then_inc(std_ready, 1)
            for b in range(B):
                act.wait_ge(xt_ready, b + 1)
                nc.scalar.activation(xh[:, b, 1:1 + S], xt[:, b, :], ACT.Copy).then_inc(hi_ready, 1)

        @block.tensor
        def _(pe):
            for t in range(NT):
                pe.wait_ge(xn_ready, t + 1)
                ins = nc.tensor.transpose(xt[:, t // TPB, (t % TPB) * P:(t % TPB + 1) * P],
                                          xn[:, t, :], ident[:])
                if t % TPB == TPB - 1:
                    ins.then_inc(xt_ready, 1)


def project0_phase(nc, k, xh, xl, w, q4, kz, v0):
    with ExitStack() as ctx:
        m = Mem(nc, ctx)
        wh = m.sb("p0_wh", [P, 2, 4, P], F16)
        wl = m.sb("p0_wl", [P, 2, 4, P], F16)
        wvh = m.sb("p0_wvh", [P, C], F16)
        wvl = m.sb("p0_wvl", [P, C], F16)
        signed = m.sb("p0_signed", [P, 2, S], F16)
        k4 = m.sb("p0_k4", [P, 2, S], F16)
        last = m.sb("p0_last", [P, 2, 4], F16)
        acc = m.ps("p0_acc", [P, 4, 512])
        klast = m.ps("p0_klast", [P, 512])
        vacc = m.ps("p0_vacc", [P, 512])
        vlast = m.ps("p0_vlast", [P, 512])
        w_ready = m.sem("p0_w_ready")
        zeroed = m.sem("p0_zeroed")
        acc_ready = m.sem("p0_acc_ready")
        signed_ready = m.sem("p0_signed_ready")
        acc_free = m.sem("p0_acc_free")
        kl_ready = m.sem("p0_kl_ready")
        kl_signed = m.sem("p0_kl_signed")
        kl_free = m.sem("p0_kl_free")
        v_ready = m.sem("p0_v_ready")
        vhi_ready = m.sem("p0_vhi_ready")
        v_free = m.sem("p0_v_free")
        chain = m.sem("p0_chain")
        passed = m.sem("p0_passed")
        block = ctx.enter_context(nc.Block())
        kgroups = kz[:, :, :].rearrange("p (n j) s -> p n j s", j=G)

        @block.gpsimd
        def _(pool):
            nc.gpsimd.memset(kz[:, :, S + 1:KPAD], 0.0)
            nc.gpsimd.memset(v0[:, :, TPB, :], 0.0).then_inc(zeroed, 1)
            pool.wait_ge(zeroed, 1)
            nc.gpsimd.memset(v0[:, :, :, D0:D0 + 1], 1.0).then_inc(zeroed, 1)

        @block.vector
        def _(dve):
            link = own_chain(dve, chain)
            dve.sem_inc(acc_free, 4)
            dve.sem_inc(kl_free, 1)
            dve.sem_inc(v_free, 1)
            nc.vector.tensor_copy(wh[:], w["qk0"][:])
            link(nc.vector.tensor_copy(wvh[:], w["v0"][:]))
            nc.vector.tensor_tensor(wl[:], w["qk0"][:], wh[:], ALU.subtract)
            nc.vector.tensor_tensor(wvl[:], w["v0"][:], wvh[:], ALU.subtract).then_inc(w_ready, 1)
            dve.wait_ge(zeroed, 2)
            with dve.Fori(0, B) as b:
                for g in range(4):
                    for s in range(2):
                        u = 2 * g + s
                        dve.wait_ge(signed_ready, b * 8 + (u + 1))
                        out = q4[:, b * 4 + g, :] if s == 0 else k4[:, g % 2, :]
                        low = k["low_q"] if s == 0 else k["low_k"]
                        nc.vector.scalar_tensor_tensor(out, acc[:, u % 4, :], low, signed[:, s, :],
                                                       ALU.mult, ALU.subtract
                                                       ).then_inc(acc_free, 1)
                    dve.wait_ge(acc_free, b * 8 + (2 * g + 6))
                    for j in range(G):
                        nc.vector.tensor_scalar(kz[:, b * 16 + (4 * g + j), 0:S], k4[:, g % 2, :],
                                                k["own"][:, j:j + 1], None, ALU.mult)
                dve.wait_ge(kl_signed, b + 1)
                nc.vector.scalar_tensor_tensor(last[:, 1, :], klast[:, 0:4], k["low_k"],
                                               last[:, 0, :], ALU.mult, ALU.subtract
                                               ).then_inc(kl_free, 1)
                dve.wait_ge(kl_free, b + 2)
                for g in range(4):
                    for j in range(G):
                        nc.vector.tensor_scalar(kz[:, b * 16 + (4 * g + j), S:S + 1],
                                                last[:, 1, g:g + 1],
                                                k["own"][:, j:j + 1], None, ALU.mult)
                dve.wait_ge(vhi_ready, b + 1)
                vb = v0[:, bass.ds(b * 16, 16), :, :]
                for t in range(TPB):
                    nc.vector.tensor_tensor(
                        vb[:, :, t, D0 + 1:2 * D0 + 1],
                        vacc[:, t * C:(t + 1) * C].rearrange("p (h d) -> p h d", h=H),
                        vb[:, :, t, 0:D0], ALU.subtract)
                nc.vector.tensor_tensor(
                    vb[0:1, :, TPB, D0 + 1:2 * D0 + 1],
                    vlast[0:1, 0:C].rearrange("p (h d) -> p h d", h=H),
                    vb[0:1, :, TPB, 0:D0], ALU.subtract).then_inc(v_free, 1)

        @block.scalar
        def _(act):
            act.preload_act_table(ACT.Exp)
            act.wait_ge(zeroed, 2)
            with act.Fori(0, B) as b:
                for u in range(8):
                    act.wait_ge(acc_ready, b * 8 + (u + 1))
                    act.wait_ge(acc_free, b * 8 + (u + 3))
                    nc.scalar.activation(signed[:, u % 2, :], acc[:, u % 4, :], ACT.Copy,
                                         scale=k["sign_q"] if u % 2 == 0 else k["sign_k"]
                                         ).then_inc(signed_ready, 1)
                act.wait_ge(kl_ready, b + 1)
                nc.scalar.activation(last[:, 0, :], klast[:, 0:4], ACT.Copy,
                                     scale=k["sign_k"]).then_inc(kl_signed, 1)
                act.wait_ge(v_ready, b + 1)
                act.sem_inc(passed, 1)
                vb = v0[:, bass.ds(b * 16, 16), :, :]
                for t in range(TPB):
                    nc.scalar.activation(vb[:, :, t, 0:D0],
                                         vacc[:, t * C:(t + 1) * C].rearrange(
                                             "p (h d) -> p h d", h=H), ACT.Copy)
                nc.scalar.activation(vb[0:1, :, TPB, 0:D0],
                                     vlast[0:1, 0:C].rearrange("p (h d) -> p h d", h=H),
                                     ACT.Copy).then_inc(vhi_ready, 1)

        @block.tensor
        def _(pe):
            pe.wait_ge(w_ready, 1)
            with pe.Fori(0, B) as b:
                for g in range(4):
                    for s in range(2):
                        u = 2 * g + s
                        pe.wait_ge(acc_free, b * 8 + (u + 1))
                        off = 1 - s
                        three_passes(nc, acc[:, u % 4, :], wh[:, s, g, :], wl[:, s, g, :],
                                     xh[:, b, off:off + S], xl[:, b, off:off + S]
                                     ).then_inc(acc_ready, 1)
                pe.wait_ge(kl_free, b + 1)
                for g in range(4):
                    ins = three_passes(nc, klast[:, g:g + 1], wh[:, 1, g, :], wl[:, 1, g, :],
                                       xh[:, b, S:S + 1], xl[:, b, S:S + 1])
                ins.then_inc(kl_ready, 1)
                pe.wait_ge(v_free, b + 1)
                for t in range(TPB):
                    three_passes(nc, vacc[:, t * C:(t + 1) * C], xh[:, b, t * P:(t + 1) * P],
                                 xl[:, b, t * P:(t + 1) * P], wvh[:], wvl[:])
                three_passes(nc, vlast[0:1, 0:C], xh[:, b, S:S + 1], xl[:, b, S:S + 1],
                             wvh[:], wvl[:]).then_inc(v_ready, 1)


def by_groups(eng, count, slot, per=4):
    for c in range(per):
        slot(0, c, c == 0, False)
    with eng.Fori(1, count - 1) as k:
        for c in range(per):
            slot(k, c, False, False)
    for c in range(per):
        slot(count - 1, c, False, c == per - 1)


def shift(k, c, by, per=4):
    return k + (c + by) // per, (c + by) % per



def attention0_phase(nc, k, q4, kz, v0, z0, loads):
    scale = float(D0) ** -0.5
    with ExitStack() as ctx:
        m = Mem(nc, ctx)
        smax = m.ps("a0_smax", [P, 2, 2, 512])
        st = m.ps("a0_st", [P, 3, 512])
        o = m.ps("a0_o", [P, 512])
        bm = m.sb("a0_bm", [P, TPB, NBLK])
        bmm = m.sb("a0_bmm", [P, TPB, NBLK])
        mx = m.sb("a0_mx", [P, 2, TPB], F16)
        p32 = m.sb("a0_p32", [P, 2, PW])
        ph = m.sb("a0_ph", [P, 4, PW], F16)
        pl = m.sb("a0_pl", [P, 4, PW], F16)
        r = m.sb("a0_r", [P, 2, 2, 5])
        preset = m.sem("a0_preset")
        smax_ready = m.sem("a0_smax_ready")
        smax_free = m.sem("a0_smax_free")
        bm_ready = m.sem("a0_bm_ready")
        mx_ready = m.sem("a0_mx_ready")
        st_ready = m.sem("a0_st_ready")
        st_free = m.sem("a0_st_free")
        hi_ready = m.sem("a0_hi_ready")
        lo_ready = m.sem("a0_lo_ready")
        pv_done = m.sem("a0_pv_done")
        o_free = m.sem("a0_o_free")
        r_ready = m.sem("a0_r_ready")
        block = ctx.enter_context(nc.Block())
        block.sync(loads)

        @block.tensor
        def _(pe):
            def scores(kk, c, u):
                n = kk * 4 + c
                pe.wait_ge(smax_free, n * 2 + (u + 1))
                for i in (2 * u, 2 * u + 1):
                    w = 5 * BLK if u == 0 else S
                    ins = nc.tensor.matmul(smax[:, u, i % 2, 0:w], q4[:, kk, i * P:(i + 1) * P],
                                           kz[:, n, 0:w], start=True, stop=True)
                if u == 0:
                    ins = nc.tensor.matmul(smax[:, 0, 0, 5 * BLK:5 * BLK + 1],
                                           q4[:, kk, 3 * P:4 * P], kz[:, n, S:S + 1],
                                           start=True, stop=True)
                ins.then_inc(smax_ready, 1)

            def transposed(kk, c, u):
                n = kk * 4 + c
                pe.wait_ge(st_free, n * 3 + (u + 1))
                for ch in ((0,), (1,), (2, 3, 4))[u]:
                    col = BASE[ch] - BASE[2] if u == 2 else 0
                    first = FIRST[ch]
                    keys = slice(ch * P, (ch + 1) * P)
                    nc.tensor.matmul(st[:, u, col:col + WIDTH[ch]], kz[:, n, keys],
                                     q4[:, kk, first - 1:S], start=True, stop=False)
                    if ch < 4:
                        w = P * ch + BLK - first
                        nc.tensor.matmul(st[:, u, col:col + w], k["mask_keys"][:, 0, :],
                                         k["mask_cols"][:, 0:w], start=False, stop=False)
                    else:
                        nc.tensor.matmul(st[:, u, col:col + 1], k["mask_keys"][:, 1, :],
                                         k["mask_cols"][:, 0:1], start=False, stop=False)
                    for i in range(max(ch - 1, 0), TPB):
                        lo = max(first - 1, i * P)
                        at = col + lo - (first - 1)
                        w = (i + 1) * P - lo
                        ins = nc.tensor.matmul(st[:, u, at:at + w],
                                               mx[:, c % 2, i:i + 1].to_broadcast([P, P]),
                                               k["neg_id16"][:, P - w:P],
                                               start=False, stop=i == TPB - 1)
                ins.then_inc(st_ready, 1)

            def weighted(kk, c):
                n = kk * 4 + c
                pe.wait_ge(hi_ready, n + 1)
                pe.wait_ge(lo_ready, n + 3)
                if c % 2 == 0:
                    pe.wait_ge(o_free, kk * 2 + (c // 2 + 1))
                for qi, (q0, cnt) in enumerate(QT):
                    out = (c % 2) * 64 + qi * (D0 + 1)
                    for ch in range(qi + 1):
                        a = BASE[ch] + q0 - FIRST[ch]
                        ob = o[0:cnt, out:out + D0 + 1]
                        nc.tensor.matmul(ob, pl[:, c, a:a + cnt], v0[:, n, ch, 0:D0 + 1],
                                         start=ch == 0, stop=False)
                        nc.tensor.matmul(ob[:, 0:D0], ph[:, c, a:a + cnt],
                                         v0[:, n, ch, D0 + 1:2 * D0 + 1], start=False, stop=False)
                        ins = nc.tensor.matmul(ob, ph[:, c, a:a + cnt],
                                               v0[:, n, ch, 0:D0 + 1], start=False, stop=ch == qi)
                ins.then_inc(pv_done, 1)

            pe.sem_inc(pv_done, 4)
            pe.wait_ge(preset, 1)
            scores(0, 0, 0)
            scores(0, 0, 1)

            def slot(kk, c, first, final):
                if not final:
                    scores(*shift(kk, c, 1), 0)
                    scores(*shift(kk, c, 1), 1)
                pe.wait_ge(mx_ready, kk * 4 + (c + 1))
                for u in range(3):
                    transposed(kk, c, u)
                if not (isinstance(kk, int) and kk == 0 and c < 2):
                    weighted(*shift(kk, c, -2))

            by_groups(pe, NG, slot)
            weighted(NG - 1, 2)
            weighted(NG - 1, 3)

        @block.vector
        def _(dve):
            dve.sem_inc(smax_free, 2)
            dve.sem_inc(o_free, 1)
            nc.vector.memset(bm[:], 0.0)
            nc.vector.memset(o[:], 1.0).then_inc(preset, 1)
            dve.wait_ge(preset, 1)

            def maxima(kk, c):
                n = kk * 4 + c
                dve.wait_ge(smax_ready, n * 2 + 1)
                nc.vector.tensor_copy(bm[:, TPB - 1, NBLK - 1:NBLK],
                                      smax[:, 0, 0, 5 * BLK:5 * BLK + 1])
                nc.vector.reduce_max(bm[:, 0:2, 0:5], smax[:, 0, :, 0:5 * BLK].rearrange(
                    "p t (a b) -> p t a b", b=BLK), AXX).then_inc(smax_free, 1)
                dve.wait_ge(smax_ready, n * 2 + 2)
                nc.vector.reduce_max(bm[:, 2:4, 0:8], smax[:, 1, :, :].rearrange(
                    "p t (a b) -> p t a b", b=BLK), AXX).then_inc(smax_free, 1)
                dve.wait_ge(smax_free, n * 2 + 4)
                nc.vector.tensor_tensor(bmm[:], bm[:], k["block_mask"], ALU.add
                                        ).then_inc(bm_ready, 1)
                dve.wait_ge(bm_ready, n + 1)
                nc.vector.reduce_max(mx[:, c % 2, :], bmm[:], AXX).then_inc(mx_ready, 1)

            def normalise(kk, c):
                n = kk * 4 + c
                dve.wait_ge(pv_done, n + 5)
                ob = o[:, 0:128].rearrange("p (h x) -> p h x", h=2)[:, :, 0:5 * (D0 + 1)]
                ob = ob.rearrange("p h (t d) -> p h t d", d=D0 + 1)
                nc.vector.reciprocal(r[:, c // 2], ob[:, :, :, D0]).then_inc(r_ready, 1)
                dve.wait_ge(r_ready, kk * 2 + (c // 2 + 1))
                for e in range(2):
                    ins = nc.vector.tensor_tensor(
                        z0[:, :, kk * 4 + (c - 1 + e), :], ob[:, e, :, 0:D0],
                        r[:, c // 2, e, :].unsqueeze(2).to_broadcast([P, 5, D0]), ALU.mult)
                ins.then_inc(o_free, 1)

            maxima(0, 0)

            def slot(kk, c, first, final):
                if c % 2 == 0 and not (isinstance(kk, int) and kk == 0):
                    normalise(*shift(kk, c, -3))
                if not final:
                    maxima(*shift(kk, c, 1))

            by_groups(dve, NG, slot)
            normalise(NG - 1, 1)
            normalise(NG - 1, 3)

        @block.scalar
        def _(act):
            act.sem_inc(st_free, 3)
            act.preload_act_table(ACT.Exp)

            def slot(kk, c, first, final):
                n = kk * 4 + c
                act.wait_ge(lo_ready, n + 1)
                act.wait_ge(pv_done, n + 1)
                for u in range(3):
                    a, w = BASE[u], (PW - BASE[2] if u == 2 else WIDTH[u])
                    act.wait_ge(st_ready, n * 3 + (u + 1))
                    nc.scalar.activation(p32[:, c % 2, a:a + w], st[:, u, 0:w],
                                         ACT.Exp, scale=scale).then_inc(st_free, 1)
                act.wait_ge(st_free, n * 3 + 6)
                nc.scalar.activation(ph[:, c, :], p32[:, c % 2, :], ACT.Copy
                                     ).then_inc(hi_ready, 1)

            by_groups(act, NG, slot)

        @block.gpsimd
        def _(pool):
            pool.sem_inc(lo_ready, 2)

            def slot(kk, c, first, final):
                n = kk * 4 + c
                pool.wait_ge(hi_ready, n + 1)
                pool.wait_ge(pv_done, n + 1)
                nc.gpsimd.tensor_tensor(pl[:, c, :], p32[:, c % 2, :], ph[:, c, :],
                                        ALU.subtract).then_inc(lo_ready, 1)

            by_groups(pool, NG, slot)


def out0_phase(nc, k, z0, w, s, loads):
    with ExitStack() as ctx:
        m = Mem(nc, ctx)
        zt = m.ps("o0_zt", [P, 2, S])
        out = m.ps("o0_out", [P, 2, S])
        zts = m.sb("o0_zts", [P, 2, S])
        zt_ready = m.sem("o0_zt_ready")
        zts_ready = m.sem("o0_zts_ready")
        out_ready = m.sem("o0_out_ready")
        s_ready = m.sem("o0_s_ready")
        block = ctx.enter_context(nc.Block())
        block.sync(loads)

        @block.tensor
        def _(pe):
            def turn(b):
                for qi, (q0, cnt) in enumerate(QT):
                    ins = nc.tensor.transpose(zt[:, b % 2, q0 - 1:q0 - 1 + cnt],
                                              z0[0:cnt, qi, b * H:(b + 1) * H, :],
                                              k["id"][0:cnt, 0:cnt])
                ins.then_inc(zt_ready, 1)

            turn(0)
            turn(1)
            for b in range(B):
                pe.wait_ge(zts_ready, b + 1)
                if b >= 2:
                    pe.wait_ge(s_ready, b - 1)
                for i in range(TPB):
                    ins = nc.tensor.matmul(out[:, b % 2, i * C:(i + 1) * C],
                                           zts[:, b % 2, i * P:(i + 1) * P], w["proj0"][:],
                                           start=True, stop=True)
                ins.then_inc(out_ready, 1)
                if b + 2 < B:
                    turn(b + 2)

        @block.scalar
        def _(act):
            for b in range(B):
                act.wait_ge(zt_ready, b + 1)
                if b >= 2:
                    act.wait_ge(out_ready, b - 1)
                nc.scalar.activation(zts[:, b % 2, :], zt[:, b % 2, :], ACT.Copy
                                     ).then_inc(zts_ready, 1)

        @block.vector
        def _(dve):
            for b in range(B):
                dve.wait_ge(out_ready, b + 1)
                nc.vector.tensor_tensor(
                    s[:, b * TPB:(b + 1) * TPB, :],
                    out[:, b % 2, :].rearrange("p (t c) -> p t c", t=TPB),
                    w["proj0_b"][:].unsqueeze(1).to_broadcast([P, TPB, C]), ALU.add
                    ).then_inc(s_ready, 1)


def router_phase(nc, k, tag, xh, xl, off, w, cw, acc, n_routed, n_all, top,
                 loads=None):
    spare = 8 - top
    wide = n_routed + spare
    with ExitStack() as ctx:
        m = Mem(nc, ctx)
        rwh = m.sb(f"{tag}_rwh", [P, n_routed], F16)
        rwl = m.sb(f"{tag}_rwl", [P, n_routed], F16)
        lg = m.ps(f"{tag}_lg", [P, NT, n_routed])
        ct = m.ps(f"{tag}_ct", [n_all, B, S])
        ob = m.ps(f"{tag}_ob", [P, 2, S])
        cts = m.sb(f"{tag}_cts", [n_all, B, S])
        e = m.sb(f"{tag}_e", [P, NT, n_routed])
        red = m.sb(f"{tag}_red", [P, NT])
        row = m.sb(f"{tag}_row", [P, NT, wide])
        rest = m.sb(f"{tag}_rest", [P, NT, wide])
        top8 = m.sb(f"{tag}_top8", [P, NT, 8])
        chain = m.sem(f"{tag}_chain")
        rw_ready = m.sem(f"{tag}_rw_ready")
        lg_ready = m.sem(f"{tag}_lg_ready")
        shifted = m.sem(f"{tag}_shifted")
        exp_ready = m.sem(f"{tag}_exp_ready")
        cw_ready = m.sem(f"{tag}_cw_ready")
        ct_ready = m.sem(f"{tag}_ct_ready")
        cts_ready = m.sem(f"{tag}_cts_ready")
        ob_ready = m.sem(f"{tag}_ob_ready")
        ob_free = m.sem(f"{tag}_ob_free")
        block = ctx.enter_context(nc.Block())
        if loads is not None:
            block.sync(loads)

        @block.vector
        def _(dve):
            link = own_chain(dve, chain)
            link(nc.vector.tensor_copy(rwh[:], w["router"][:]))
            nc.vector.tensor_tensor(rwl[:], w["router"][:], rwh[:], ALU.subtract
                                    ).then_inc(rw_ready, 1)
            for i in range(spare):
                nc.vector.memset(row[:, :, n_routed + i:n_routed + i + 1], 2.0 + i)
            if n_all > n_routed:
                nc.vector.memset(cw[:, :, n_routed:n_all], 1.0)
            dve.wait_ge(lg_ready, 1)
            link(nc.vector.tensor_tensor(e[:], lg[:], w["router_b"][:].unsqueeze(1).to_broadcast(
                [P, NT, n_routed]), ALU.add))
            link(nc.vector.reduce_max(red[:], e[:], AXX))
            nc.vector.tensor_tensor(e[:], e[:], red[:].unsqueeze(2).to_broadcast(
                [P, NT, n_routed]), ALU.subtract).then_inc(shifted, 1)
            dve.wait_ge(exp_ready, 1)
            link(nc.vector.reduce_sum(red[:], e[:], AXX))
            link(nc.vector.reciprocal(red[:], red[:]))
            link(nc.vector.tensor_tensor(row[:, :, 0:n_routed], e[:], red[:].unsqueeze(2)
                                         .to_broadcast([P, NT, n_routed]), ALU.mult))
            for t in range(NT):
                ins = nc.vector.max(top8[:, t, :], row[:, t, :])
            link(ins)
            for t in range(NT):
                ins = nc.vector.match_replace(rest[:, t, :], top8[:, t, :], row[:, t, :], 0.0)
            link(ins)
            nc.vector.tensor_tensor(cw[:, :, 0:n_routed], row[:, :, 0:n_routed],
                                    rest[:, :, 0:n_routed], ALU.subtract).then_inc(cw_ready, 1)
            for b in range(B):
                dve.wait_ge(ob_ready, b + 1)
                nc.vector.tensor_copy(acc[:, b * TPB:(b + 1) * TPB, :],
                                      ob[:, b % 2, :].rearrange("p (t c) -> p t c", t=TPB)
                                      ).then_inc(ob_free, 1)

        @block.scalar
        def _(act):
            act.wait_ge(shifted, 1)
            nc.scalar.activation(e[:], e[:], ACT.Exp).then_inc(exp_ready, 1)
            for b in range(B):
                act.wait_ge(ct_ready, b + 1)
                nc.scalar.activation(cts[:, b, :], ct[:, b, :], ACT.Copy).then_inc(cts_ready, 1)

        @block.tensor
        def _(pe):
            pe.wait_ge(rw_ready, 1)
            for t in range(NT):
                b, a = t // TPB, off + (t % TPB) * P
                ins = three_passes(nc, lg[:, t, :], xh[:, b, a:a + P], xl[:, b, a:a + P],
                                   rwh[:], rwl[:])
            ins.then_inc(lg_ready, 1)
            pe.wait_ge(cw_ready, 1)
            for t in range(NT):
                ins = nc.tensor.transpose(ct[:, t // TPB, (t % TPB) * P:(t % TPB + 1) * P],
                                          cw[:, t, :], k["id"][:])
                if t % TPB == TPB - 1:
                    ins.then_inc(ct_ready, 1)
            for b in range(B):
                pe.wait_ge(cts_ready, b + 1)
                if b >= 2:
                    pe.wait_ge(ob_free, b - 1)
                for i in range(TPB):
                    ins = nc.tensor.matmul(ob[:, b % 2, i * C:(i + 1) * C],
                                           cts[:, b, i * P:(i + 1) * P], w["out_b"][:],
                                           start=True, stop=True)
                ins.then_inc(ob_ready, 1)


def experts0_phase(nc, k, xh, xl, w, cw, acc):
    U = 2 * B
    NB = 4
    with ExitStack() as ctx:
        m = Mem(nc, ctx)
        wh = m.sb("e0_wh", [P, E0, 2 * I0], F16)
        wl = m.sb("e0_wl", [P, E0, 2 * I0], F16)
        upb = m.sb("e0_upb", [P, E0, 2])
        gate = m.sb("e0_gate", [P, NB, S])
        sig = m.sb("e0_sig", [P, NB, S])
        up = m.sb("e0_up", [P, NB, S])
        gs = m.sb("e0_gs", [P, NB, S])
        hid = m.sb("e0_hid", [P, NB, S])
        gu = m.ps("e0_gu", [P, 2, 2, S])
        out = m.ps("e0_out", [P, 4, S])
        w_ready = m.sem("e0_w_ready")
        gate_made = m.sem("e0_gate_made")
        up_made = m.sem("e0_up_made")
        gate_ready = m.sem("e0_gate_ready")
        up_ready = m.sem("e0_up_ready")
        sig_ready = m.sem("e0_sig_ready")
        clip_ready = m.sem("e0_clip_ready")
        gs_ready = m.sem("e0_gs_ready")
        hid_ready = m.sem("e0_hid_ready")
        out_ready = m.sem("e0_out_ready")
        out_free = m.sem("e0_out_free")
        passed = m.sem("e0_passed")
        block = ctx.enter_context(nc.Block())

        @block.gpsimd
        def _(pool):
            pool.sem_inc(gs_ready, 4)

            def slot(e, u, first, final):
                pool.wait_ge(sig_ready, e * U + (u + 1))
                nc.gpsimd.tensor_tensor(gs[:, u % NB, :], gate[:, u % NB, :], sig[:, u % NB, :],
                                        ALU.mult).then_inc(gs_ready, 1)

            by_groups(pool, E0, slot, U)

        @block.scalar
        def _(act):
            act.sem_inc(up_ready, 2)
            act.preload_act_table(ACT.Sigmoid)
            act.wait_ge(w_ready, 2)

            def slot(e, u, first, final):
                n1 = e * U + (u + 1)
                act.wait_ge(up_made, n1)
                act.wait_ge(hid_ready, n1)
                act.sem_inc(passed, 1)
                nc.scalar.activation(up[:, u % NB, :], gu[:, u % 2, 1, :], ACT.Identity,
                                     bias=upb[:, e, u % 2:u % 2 + 1]).then_inc(up_ready, 1)
                act.wait_ge(gate_ready, e * U + (u + 3))
                act.wait_ge(gs_ready, n1)
                nc.scalar.activation(sig[:, u % NB, :], gate[:, u % NB, :], ACT.Sigmoid,
                                     scale=ALPHA).then_inc(sig_ready, 1)

            by_groups(act, E0, slot, U)

        @block.vector
        def _(dve):
            dve.sem_inc(gate_ready, 2)
            dve.sem_inc(hid_ready, 4)
            dve.sem_inc(out_free, 4)
            nc.vector.tensor_scalar_add(upb[:], w["gu_b"][:, :, 2:4], 1.0)
            nc.vector.tensor_copy(wh[:], w["gu"][:]).then_inc(w_ready, 1)
            dve.wait_ge(w_ready, 1)
            nc.vector.tensor_tensor(wl[:], w["gu"][:], wh[:], ALU.subtract).then_inc(w_ready, 1)

            def product(e, u):
                dve.wait_ge(clip_ready, e * U + (u + 1))
                dve.wait_ge(gs_ready, e * U + (u + 5))
                dve.wait_ge(out_ready, e * (U // 2) + (u // 2 + 1))
                nc.vector.tensor_tensor(hid[:, u % NB, :], up[:, u % NB, :], gs[:, u % NB, :],
                                        ALU.mult).then_inc(hid_ready, 1)

            def accumulate(e, b):
                g = e * B + b
                dve.wait_ge(out_ready, g + 3)
                dve.wait_ge(out_free, g + 1)
                for i in range(TPB):
                    t = b * TPB + i
                    ins = nc.vector.scalar_tensor_tensor(
                        acc[:, t, :], out[:, b % 4, i * C:(i + 1) * C], cw[:, t, bass.ds(e, 1)],
                        acc[:, t, :], ALU.mult, ALU.add)
                ins.then_inc(out_free, 1)

            def slot(e, u, first, final):
                dve.wait_ge(gate_made, e * U + (u + 1))
                nc.vector.tensor_scalar(gate[:, u % NB, :], gu[:, u % 2, 0, :],
                                        w["gu_b"][:, e, u % 2:u % 2 + 1], LIMIT, ALU.add, ALU.min
                                        ).then_inc(gate_ready, 1)
                dve.wait_ge(up_ready, e * U + (u + 3))
                nc.vector.tensor_scalar(up[:, u % NB, :], up[:, u % NB, :], LIMIT + 1.0,
                                        1.0 - LIMIT, ALU.min, ALU.max).then_inc(clip_ready, 1)
                if not first:
                    product(*shift(e, u, -1, U))
                if u % 2 == 0:
                    ge, gb = shift(e, u // 2, -2, B)
                    if not (isinstance(ge, int) and ge < 0):
                        accumulate(ge, gb)

            by_groups(dve, E0, slot, U)
            product(E0 - 1, U - 1)
            accumulate(E0 - 1, B - 2)
            accumulate(E0 - 1, B - 1)

        @block.tensor
        def _(pe):
            pe.sem_inc(out_ready, 2)
            pe.wait_ge(w_ready, 2)

            def down(e, b):
                g = e * B + b
                pe.wait_ge(hid_ready, e * U + (2 * b + 6))
                pe.wait_ge(out_free, g + 1)
                for i in range(TPB):
                    for half in range(2):
                        ins = nc.tensor.matmul(out[:, b % 4, i * C:(i + 1) * C],
                                               hid[:, (2 * b + half) % NB, i * P:(i + 1) * P],
                                               w["down"][:, e, half, :],
                                               start=half == 0, stop=half == 1)
                ins.then_inc(out_ready, 1)

            def slot(e, u, first, final):
                b, half = u // 2, u % 2
                pe.wait_ge(gate_ready, e * U + (u + 1))
                pe.wait_ge(up_ready, e * U + (u + 1))
                for s, made in ((0, gate_made), (1, up_made)):
                    rows = slice(s * I0 + half * P, s * I0 + (half + 1) * P)
                    three_passes(nc, gu[:, u % 2, s, :], wh[:, e, rows], wl[:, e, rows],
                                 xh[:, b, 1:1 + S], xl[:, b, 1:1 + S]).then_inc(made, 1)
                if half == 1:
                    ge, gb = shift(e, b, -1, B)
                    if not (isinstance(ge, int) and ge < 0):
                        down(ge, gb)

            by_groups(pe, E0, slot, U)
            down(E0 - 1, B - 1)


def experts1_phase(nc, k, xh, xl, w, cw, acc):
    with ExitStack() as ctx:
        m = Mem(nc, ctx)
        wh = m.sb("e1_wh", [P, NE1, C], F16)
        wl = m.sb("e1_wl", [P, NE1, C], F16)
        hid = m.sb("e1_hid", [P, 4, S])
        a = m.ps("e1_a", [P, 4, S])
        out = m.ps("e1_out", [P, 4, S])
        w_ready = m.sem("e1_w_ready")
        a_ready = m.sem("e1_a_ready")
        hid_ready = m.sem("e1_hid_ready")
        out_ready = m.sem("e1_out_ready")
        out_free = m.sem("e1_out_free")
        passed = m.sem("e1_passed")
        block = ctx.enter_context(nc.Block())

        @block.scalar
        def _(act):
            act.sem_inc(hid_ready, 4)
            act.preload_act_table(ACT.Relu)

            def slot(e, b, first, final):
                n = e * B + b
                act.wait_ge(a_ready, n + 1)
                act.wait_ge(out_ready, n + 1)
                act.sem_inc(passed, 1)
                nc.scalar.activation(hid[:, b, :], a[:, b, :], ACT.Relu,
                                     bias=w["e1_b"][:, bass.ds(e, 1)]).then_inc(hid_ready, 1)

            by_groups(act, NE1, slot)

        @block.vector
        def _(dve):
            dve.sem_inc(out_free, 4)
            nc.vector.tensor_copy(wh[:], w["e1_w1"][:]).then_inc(w_ready, 1)
            dve.wait_ge(w_ready, 1)
            nc.vector.tensor_tensor(wl[:], w["e1_w1"][:], wh[:], ALU.subtract).then_inc(w_ready, 1)

            def slot(e, b, first, final):
                n = e * B + b
                dve.wait_ge(out_ready, n + 5)
                dve.wait_ge(out_free, n + 1)
                for i in range(TPB):
                    t = b * TPB + i
                    ins = nc.vector.scalar_tensor_tensor(
                        acc[:, t, :], out[:, b, i * C:(i + 1) * C], cw[:, t, bass.ds(e, 1)],
                        acc[:, t, :], ALU.mult, ALU.add)
                ins.then_inc(out_free, 1)

            by_groups(dve, NE1, slot)

        @block.tensor
        def _(pe):
            pe.sem_inc(out_ready, 4)
            pe.wait_ge(w_ready, 2)

            def down(e, b):
                n = e * B + b
                pe.wait_ge(hid_ready, n + 5)
                pe.wait_ge(out_free, n + 1)
                for i in range(TPB):
                    ins = nc.tensor.matmul(out[:, b, i * C:(i + 1) * C],
                                           hid[:, b, i * P:(i + 1) * P], w["e1_w2"][:, e, :],
                                           start=True, stop=True)
                ins.then_inc(out_ready, 1)

            def slot(e, b, first, final):
                n = e * B + b
                pe.wait_ge(hid_ready, n + 1)
                three_passes(nc, a[:, b, :], wh[:, e, :], wl[:, e, :],
                             xh[:, b, 1:1 + S], xl[:, b, 1:1 + S]).then_inc(a_ready, 1)
                de, db = shift(e, b, -2, B)
                if not (isinstance(de, int) and de < 0):
                    down(de, db)

            by_groups(pe, NE1, slot)
            down(NE1 - 1, B - 2)
            down(NE1 - 1, B - 1)


def update_phase(nc, tag, x, s, acc, out_dram=None):
    with ExitStack() as ctx:
        m = Mem(nc, ctx)
        sig = m.sb(f"{tag}_sig", [P, NT, C])
        sig_ready = m.sem(f"{tag}_sig_ready")
        prod_ready = m.sem(f"{tag}_prod_ready")
        gated = m.sem(f"{tag}_gated")
        x_ready = m.sem(f"{tag}_x_ready")
        stored = m.sem(f"{tag}_stored")
        block = ctx.enter_context(nc.Block())
        part = lambda t, b: t[:, b * TPB:(b + 1) * TPB, :]

        @block.scalar
        def _(act):
            for b in range(B):
                nc.scalar.activation(part(sig, b), part(acc, b), ACT.Sigmoid
                                     ).then_inc(sig_ready, 1)

        @block.gpsimd
        def _(pool):
            for b in range(B):
                nc.gpsimd.tensor_tensor(part(s, b), part(s, b), part(acc, b), ALU.mult
                                        ).then_inc(prod_ready, 1)

        @block.vector
        def _(dve):
            for b in range(B):
                dve.wait_ge(sig_ready, b + 1)
                dve.wait_ge(prod_ready, b + 1)
                nc.vector.tensor_tensor(part(s, b), part(s, b), part(sig, b), ALU.mult
                                        ).then_inc(gated, 1)
                dve.wait_ge(gated, b + 1)
                nc.vector.tensor_tensor(part(x, b), part(x, b), part(s, b), ALU.add
                                        ).then_inc(x_ready, 1)

        if out_dram is not None:
            @block.sync
            def _(sp):
                for b in range(B):
                    sp.wait_ge(x_ready, b + 1)
                    sp.dma_start(out_dram[b].rearrange("(t p) c -> p t c", p=P), part(x, b)
                                 ).then_inc(stored, 16)
                sp.wait_ge(stored, 16 * B)


def prepare1_phase(nc, k, rb_scratch, rb, han, wqk, wv, w):
    with ExitStack() as ctx:
        m = Mem(nc, ctx)
        tab = m.sb("r1_tab", [H, 2, 3 * P])
        parts = m.sb("r1_parts", [H, 3, 3 * P], F16)
        chain = m.sem("r1_chain")
        parts_ready = m.sem("r1_parts_ready")
        saved = m.sem("r1_saved")
        loaded = m.sem("r1_loaded")
        block = ctx.enter_context(nc.Block())

        @block.vector
        def _(dve):
            link = own_chain(dve, chain)
            link(nc.vector.memset(tab[:], 0.0))
            nc.vector.tensor_scalar(tab[:, 0, P:P + 255], rb[:, 0, :], rb[:, 0, 0:1], None,
                                    ALU.subtract)
            link(nc.vector.tensor_scalar(tab[:, 1, 0:255], rb[:, 1, :], rb[:, 0, 0:1], None,
                                         ALU.subtract))
            nc.vector.tensor_copy(parts[:, 0, :], tab[:, 0, :])
            link(nc.vector.tensor_copy(parts[:, 2, :], tab[:, 1, :]))
            nc.vector.tensor_tensor(parts[:, 1, :], tab[:, 0, :], parts[:, 0, :], ALU.subtract
                                    ).then_inc(parts_ready, 1)
            nc.vector.tensor_copy(wqk[:, 0], w["qk1"][:])
            link(nc.vector.tensor_copy(wv[:, 0, :], w["v1"][:]))
            nc.vector.tensor_tensor(wqk[:, 1], w["qk1"][:], wqk[:, 0], ALU.subtract)
            nc.vector.tensor_tensor(wv[:, 1, :], w["v1"][:], wv[:, 0, :], ALU.subtract)

        @block.sync
        def _(sp):
            sp.wait_ge(parts_ready, 1)
            sp.dma_start(rb_scratch.rearrange("a h n -> h a n"), parts[:]).then_inc(saved, 16)
            sp.wait_ge(saved, 16)
            for a in range(3):
                src = bass.AP(rb_scratch.tensor, a * H * 3 * P, [[1, P], [3 * P, H], [1, 2 * P]])
                sp.dma_start(han[:, a], src).then_inc(loaded, 16)
            sp.wait_ge(loaded, 48)


def attention1_phase(nc, k, xh, xl, wqk, wv, han, z1, loads):
    DV = D1 + 1
    Q, K = slice(0, D1), slice(D1, P)
    scale = float(D1) ** -0.5
    with ExitStack() as ctx:
        m = Mem(nc, ctx)
        smax = m.ps("a1_smax", [P, 2, S])
        st = m.ps("a1_st", [P, 3, S])
        o = m.ps("a1_o", [P, S])
        qk = m.ps("a1_qk", [P, S])
        vp = m.ps("a1_vp", [P, S])
        q1 = m.sb("a1_q1", [P, 4, S], F16)
        k1 = m.sb("a1_k1", [P, 4, S], F16)
        k2 = m.sb("a1_k2", [P, 4, S], F16)
        v1 = m.sb("a1_v1", [P, 4, TPB, 2 * D1 + 1], F16)
        mx = m.sb("a1_mx", [P, 2, TPB], F16)
        p32 = m.sb("a1_p32", [P, 2, TPB, S])
        ph = m.sb("a1_ph", [P, 2, TPB, S], F16)
        pl = m.sb("a1_pl", [P, 2, TPB, S], F16)
        r = m.sb("a1_r", [P, TPB])
        qk_made = m.sem("a1_qk_made")
        q_high = m.sem("a1_q_high")
        k_high = m.sem("a1_k_high")
        qk_split = m.sem("a1_qk_split")
        v_made = m.sem("a1_v_made")
        v_high = m.sem("a1_v_high")
        v_split = m.sem("a1_v_split")
        smax_ready = m.sem("a1_smax_ready")
        smax_free = m.sem("a1_smax_free")
        st_ready = m.sem("a1_st_ready")
        st_free = m.sem("a1_st_free")
        hi_ready = m.sem("a1_hi_ready")
        lo_ready = m.sem("a1_lo_ready")
        pv_done = m.sem("a1_pv_done")
        r_ready = m.sem("a1_r_ready")
        o_free = m.sem("a1_o_free")
        preset = m.sem("a1_preset")
        block = ctx.enter_context(nc.Block())
        block.sync(loads)

        @block.tensor
        def _(pe):
            def project_qk(h, b):
                pe.wait_ge(qk_split, h * B + (b + 1))
                three_passes(nc, qk[:], wqk[:, 0, h, :], wqk[:, 1, h, :],
                             xh[:, b, 1:1 + S], xl[:, b, 1:1 + S]).then_inc(qk_made, 1)

            def project_v(h, b):
                pe.wait_ge(v_split, h * B + (b + 1))
                cols = bass.ds(h * D1, D1)
                for t in range(TPB):
                    a = 1 + t * P
                    ins = three_passes(nc, vp[:, t * D1:(t + 1) * D1], xh[:, b, a:a + P],
                                       xl[:, b, a:a + P], wv[:, 0, cols], wv[:, 1, cols])
                ins.then_inc(v_made, 1)

            def scores(h, b, i):
                n = h * B + b
                if i == 0:
                    pe.wait_ge(qk_split, n + 2)
                pe.wait_ge(smax_free, n * TPB + (i + 1))
                ins = nc.tensor.matmul(smax[:, i % 2, :], q1[:, b, i * P:(i + 1) * P],
                                       k1[:, b, :], start=True, stop=i < 2)
                if i >= 2:
                    ins = nc.tensor.matmul(smax[:, i % 2, 0:(i - 1) * P], k["anti16"],
                                           han[:, 2, h, (3 - i) * P:2 * P],
                                           start=False, stop=True)
                ins.then_inc(smax_ready, 1)

            def transposed(h, b, ch):
                n = h * B + b
                if ch == 0:
                    pe.wait_ge(smax_free, n * TPB + 6)
                pe.wait_ge(st_free, n * TPB + (4, 2, 3, 5)[ch])
                ob = st[:, ch % 3, :]
                keys = slice(ch * P, (ch + 1) * P)
                nc.tensor.matmul(ob, k2[:, b, keys], q1[:, b, :], start=True, stop=False)
                nc.tensor.matmul(ob, k1[:, b, keys], q1[:, b, :], start=False, stop=False)
                for part in range(2 if ch < 2 else 0):
                    nc.tensor.matmul(ob[:, (2 + ch) * P:S], k["anti16"],
                                     han[:, part, h, 0:(2 - ch) * P], start=False, stop=False)
                for i in range(TPB):
                    ins = nc.tensor.matmul(ob[:, i * P:(i + 1) * P],
                                           mx[:, b % 2, i:i + 1].to_broadcast([P, P]),
                                           k["neg_id16"], start=False, stop=i == TPB - 1)
                ins.then_inc(st_ready, 1)

            def weighted(h, b, u):
                n = h * B + b
                if u == 0:
                    pe.wait_ge(v_split, n + 2)
                    pe.wait_ge(o_free, n + 1)
                    pe.wait_ge(lo_ready, n * 2 + 6)
                for i in (2 * u, 2 * u + 1):
                    ob = o[:, i * DV:(i + 1) * DV]
                    for ch in range(TPB):
                        cols = slice(i * P, (i + 1) * P)
                        nc.tensor.matmul(ob, pl[:, b % 2, ch, cols], v1[:, b, ch, 0:DV],
                                         start=ch == 0, stop=False)
                        nc.tensor.matmul(ob[:, 0:D1], ph[:, b % 2, ch, cols],
                                         v1[:, b, ch, DV:], start=False, stop=False)
                        ins = nc.tensor.matmul(ob, ph[:, b % 2, ch, cols], v1[:, b, ch, 0:DV],
                                               start=False, stop=ch == TPB - 1)
                if u == 1:
                    ins.then_inc(pv_done, 1)

            pe.sem_inc(pv_done, 2)
            pe.wait_ge(preset, 1)
            for b in range(2):
                project_qk(0, b)
                project_v(0, b)
            for i in range(TPB):
                scores(0, 0, i)

            def slot(h, b, first, final):
                ahead = None if isinstance(h, int) and h == H - 1 and b >= 2 else shift(h, b, 2)
                for i in range(TPB):
                    if not final:
                        scores(*shift(h, b, 1), i)
                    transposed(h, b, i)
                    if i == 0 and ahead:
                        project_qk(*ahead)
                    if i == 1 and ahead:
                        project_v(*ahead)
                    if i >= 2 and not first:
                        weighted(*shift(h, b, -1), i - 2)

            by_groups(pe, H, slot)
            weighted(H - 1, B - 1, 0)
            weighted(H - 1, B - 1, 1)

        @block.vector
        def _(dve):
            dve.sem_inc(qk_split, 1)
            dve.sem_inc(v_split, 1)
            dve.sem_inc(smax_free, 2)
            dve.sem_inc(o_free, 1)
            nc.vector.memset(k2[K], 0.0)
            nc.vector.memset(v1[:, :, :, D1:DV], 1.0).then_inc(preset, 1)

            def low_q(h, b):
                dve.wait_ge(q_high, h * B + (b + 1))
                nc.vector.scalar_tensor_tensor(q1[K, b, :], qk[Q], scale, q1[Q, b, :],
                                               ALU.mult, ALU.subtract)

            def low_k(h, b):
                dve.wait_ge(k_high, h * B + (b + 1))
                nc.vector.tensor_copy(k1[Q, b, :], k1[K, b, :])
                nc.vector.tensor_tensor(k2[Q, b, :], qk[K], k1[K, b, :], ALU.subtract
                                        ).then_inc(qk_split, 1)

            def low_v(h, b):
                dve.wait_ge(v_high, h * B + (b + 1))
                nc.vector.tensor_tensor(
                    v1[:, b, :, DV:], vp[:, 0:TPB * D1].rearrange("p (t d) -> p t d", t=TPB),
                    v1[:, b, :, 0:D1], ALU.subtract).then_inc(v_split, 1)

            def maximum(h, b, i):
                dve.wait_ge(smax_ready, (h * B + b) * TPB + (i + 1))
                nc.vector.reduce_max(mx[:, b % 2, i:i + 1], smax[:, i % 2, :], AXX
                                     ).then_inc(smax_free, 1)

            def normalise(h, b):
                n = h * B + b
                dve.wait_ge(pv_done, n + 3)
                ob = o[:, 0:TPB * DV].rearrange("p (t d) -> p t d", t=TPB)
                nc.vector.reciprocal(r[:], ob[:, :, D1]).then_inc(r_ready, 1)
                dve.wait_ge(r_ready, n + 1)
                nc.vector.tensor_tensor(z1[:, b * TPB:(b + 1) * TPB, bass.ds(h * D1, D1)],
                                        ob[:, :, 0:D1],
                                        r[:].unsqueeze(2).to_broadcast([P, TPB, D1]), ALU.mult
                                        ).then_inc(o_free, 1)

            dve.wait_ge(preset, 1)
            low_q(0, 0)
            low_k(0, 0)
            low_v(0, 0)
            low_q(0, 1)
            low_k(0, 1)
            for i in range(TPB):
                maximum(0, 0, i)

            def slot(h, b, first, final):
                ahead = None if isinstance(h, int) and h == H - 1 and b >= 2 else shift(h, b, 2)
                if not final:
                    maximum(*shift(h, b, 1), 0)
                    low_v(*shift(h, b, 1))
                    maximum(*shift(h, b, 1), 1)
                if ahead:
                    low_q(*ahead)
                if not final:
                    maximum(*shift(h, b, 1), 2)
                if ahead:
                    low_k(*ahead)
                if not final:
                    maximum(*shift(h, b, 1), 3)
                if not first:
                    normalise(*shift(h, b, -1))

            by_groups(dve, H, slot)
            normalise(H - 1, B - 1)

        @block.scalar
        def _(act):
            act.sem_inc(st_free, 4)
            act.preload_act_table(ACT.Exp)
            act.wait_ge(preset, 1)

            def high_q(h, b):
                act.wait_ge(qk_made, h * B + (b + 1))
                nc.scalar.activation(q1[Q, b, :], qk[Q], ACT.Copy, scale=scale
                                     ).then_inc(q_high, 1)

            def high_k(h, b):
                act.wait_ge(qk_made, h * B + (b + 1))
                nc.scalar.activation(k1[K, b, :], qk[K], ACT.Copy).then_inc(k_high, 1)

            def high_v(h, b):
                act.wait_ge(v_made, h * B + (b + 1))
                nc.scalar.activation(
                    v1[:, b, :, 0:D1], vp[:, 0:TPB * D1].rearrange("p (t d) -> p t d", t=TPB),
                    ACT.Copy).then_inc(v_high, 1)

            def exponent(h, b, ch):
                n = h * B + b
                act.wait_ge(st_ready, n * TPB + (ch + 1))
                act.wait_ge(lo_ready, n * 2 + (ch // 2 + 1))
                nc.scalar.activation(p32[:, b % 2, ch, :], st[:, ch % 3, :], ACT.Exp
                                     ).then_inc(st_free, 1)

            def high_p(h, b, u):
                n = h * B + b
                act.wait_ge(st_free, n * TPB + (2 * u + 6))
                act.wait_ge(pv_done, n + 1)
                nc.scalar.activation(ph[:, b % 2, 2 * u:2 * u + 2, :],
                                     p32[:, b % 2, 2 * u:2 * u + 2, :], ACT.Copy
                                     ).then_inc(hi_ready, 1)

            high_q(0, 0)
            high_k(0, 0)
            high_v(0, 0)
            high_q(0, 1)
            high_k(0, 1)

            def slot(h, b, first, final):
                ahead = None if isinstance(h, int) and h == H - 1 and b >= 2 else shift(h, b, 2)
                exponent(h, b, 0)
                if not final:
                    high_v(*shift(h, b, 1))
                if ahead:
                    high_q(*ahead)
                exponent(h, b, 1)
                if ahead:
                    high_k(*ahead)
                exponent(h, b, 2)
                high_p(h, b, 0)
                exponent(h, b, 3)
                high_p(h, b, 1)

            by_groups(act, H, slot)

        @block.gpsimd
        def _(pool):
            pool.sem_inc(lo_ready, 4)

            def slot(h, b, first, final):
                n = h * B + b
                for u in range(2):
                    half = slice(2 * u, 2 * u + 2)
                    pool.wait_ge(hi_ready, n * 2 + (u + 1))
                    pool.wait_ge(pv_done, n + 1)
                    nc.gpsimd.tensor_tensor(pl[:, b % 2, half, :], p32[:, b % 2, half, :],
                                            ph[:, b % 2, half, :], ALU.subtract
                                            ).then_inc(lo_ready, 1)

            by_groups(pool, H, slot)


def out1_phase(nc, k, z1, w, s):
    NK = H * D1 // P
    with ExitStack() as ctx:
        m = Mem(nc, ctx)
        zt = m.ps("o1_zt", [P, 2, NK, P])
        out = m.ps("o1_out", [P, 2, 512])
        zts = m.sb("o1_zts", [P, 2, NK, P])
        zt_ready = m.sem("o1_zt_ready")
        act_half = m.sem("o1_act_half")
        dve_half = m.sem("o1_dve_half")
        out_ready = m.sem("o1_out_ready")
        s_ready = m.sem("o1_s_ready")
        block = ctx.enter_context(nc.Block())
        half = NK // 2

        @block.tensor
        def _(pe):
            def turn(t):
                if t >= 2:
                    pe.wait_ge(act_half, t - 1)
                    pe.wait_ge(dve_half, t - 1)
                for c in range(NK):
                    ins = nc.tensor.transpose(zt[:, t % 2, c, :], z1[:, t, c * P:(c + 1) * P],
                                              k["id"])
                ins.then_inc(zt_ready, 1)

            turn(0)
            for t in range(NT):
                if t + 1 < NT:
                    turn(t + 1)
                pe.wait_ge(act_half, t + 1)
                pe.wait_ge(dve_half, t + 1)
                if t >= 2:
                    pe.wait_ge(s_ready, t - 1)
                for c in range(NK):
                    ins = nc.tensor.matmul(out[:, t % 2, 0:C], zts[:, t % 2, c, :],
                                           w["out1"][:, c, :], start=c == 0, stop=c == NK - 1)
                ins.then_inc(out_ready, 1)

        @block.scalar
        def _(act):
            for t in range(NT):
                act.wait_ge(zt_ready, t + 1)
                if t >= 2:
                    act.wait_ge(out_ready, t - 1)
                nc.scalar.activation(zts[:, t % 2, 0:half, :], zt[:, t % 2, 0:half, :], ACT.Copy
                                     ).then_inc(act_half, 1)

        @block.vector
        def _(dve):
            for t in range(NT):
                dve.wait_ge(zt_ready, t + 1)
                if t >= 2:
                    dve.wait_ge(out_ready, t - 1)
                nc.vector.tensor_copy(zts[:, t % 2, half:NK, :], zt[:, t % 2, half:NK, :]
                                      ).then_inc(dve_half, 1)
                if t >= 1:
                    dve.wait_ge(out_ready, t)
                    nc.vector.tensor_copy(s[:, t - 1, :], out[:, (t - 1) % 2, 0:C]
                                          ).then_inc(s_ready, 1)
            dve.wait_ge(out_ready, NT)
            nc.vector.tensor_copy(s[:, NT - 1, :], out[:, (NT - 1) % 2, 0:C]).then_inc(s_ready, 1)


CONSTS = [("id", P), ("neg_id", P), ("anti", P), ("mask_keys", 2 * P), ("mask_cols", BLK),
          ("block_mask", TPB * NBLK), ("low_q", 1), ("low_k", 1), ("sign_q", 1), ("sign_k", 1),
          ("own", G)]


def program(nc, a, out, stop=99):
    with ExitStack() as ctx:
        m = Mem(nc, ctx)
        x = m.sb("x", [P, NT, C])
        s = m.sb("s", [P, NT, C])
        acc = m.sb("acc", [P, NT, C])
        xh = m.sb("xh", [P, B, S + 2], F16)
        xl = m.sb("xl", [P, B, S + 2], F16)
        cw = m.sb("cw", [P, NT, NE1])
        const = m.sb("const", [P, sum(n for _, n in CONSTS)])
        neg16 = m.sb("neg16", [P, P], F16)
        anti16 = m.sb("anti16", [P, P], F16)
        mask_keys = m.sb("mask_keys", [P, 2, P], BF16)
        mask_cols = m.sb("mask_cols", [P, BLK], BF16)
        glob = m.sb("glob", [P, 1])
        rb = m.sb("rb", [H, 2, 255])
        w = {
            "qk0": m.sb("w_qk0", [P, 2, 4, P]), "v0": m.sb("w_v0", [P, C]),
            "proj0": m.sb("w_proj0", [P, C]), "proj0_b": m.sb("w_proj0_b", [P, C]),
            "gu_b": m.sb("w_gu_b", [P, E0, 4]),
            "e1_b": m.sb("w_e1_b", [P, NE1]),
        }
        r0 = {"router": m.sb("r0_w", [P, E0]), "router_b": m.sb("r0_wb", [P, E0]),
              "out_b": m.sb("r0_ob", [E0, C])}
        r1 = {"router": m.sb("r1_w", [P, E1]), "router_b": m.sb("r1_wb", [P, E1]),
              "out_b": m.sb("r1_ob", [NE1, C])}
        k, at = {}, 0
        for name, n in CONSTS:
            k[name] = const[:, at:at + n]
            at += n
        k32 = dict(k)
        k["block_mask"] = k["block_mask"].rearrange("p (t b) -> p t b", t=TPB)
        k["neg_id16"], k["anti16"] = neg16[:], anti16[:]
        k["mask_keys"], k["mask_cols"] = mask_keys[:], mask_cols[:]

        first_loads = m.sem("first_loads")
        x_loads = m.sem("x_loads")
        more_loads = m.sem("more_loads")
        gu_loads = m.sem("gu_loads")
        expert_loads = m.sem("expert_loads")
        late_loads = m.sem("late_loads")

        with nc.Block() as block:
            @block.sync
            def _(sp):
                for b in range(B):
                    sp.dma_start(x[:, b * TPB:(b + 1) * TPB, :],
                                 a["x"][b].rearrange("(t p) c -> p t c", p=P)).then_inc(x_loads, 16)
                sp.wait_ge(x_loads, 16 * B)

            @block.scalar
            def _(act):
                act.dma_start(const[:], a["const"]).then_inc(first_loads, 16)
                act.dma_start(glob[:], a["glob"]).then_inc(first_loads, 16)
                act.dma_start(w["qk0"][:], a["qk0"]).then_inc(first_loads, 16)
                act.dma_start(w["v0"][:], a["v0"]).then_inc(first_loads, 16)
                act.wait_ge(first_loads, 64)

        with nc.Block() as block:
            @block.vector
            def _(dve):
                nc.vector.tensor_copy(neg16[:], k32["neg_id"])
                nc.vector.tensor_copy(anti16[:], k32["anti"])
                nc.vector.tensor_copy(mask_cols[:], k32["mask_cols"])
                nc.vector.tensor_copy(mask_keys[:].rearrange("p a b -> p (a b)"),
                                      k32["mask_keys"])

        def loads1(sp):
            for dst, src in ((w["proj0"], "proj0"), (r0["router"], "router0"),
                             (r0["out_b"], "down_b"), (w["gu_b"], "gu_b"),
                             (r1["router"], "router1"),
                             (r1["out_b"], "e1_b2"), (w["e1_b"], "e1_b1"), (rb, "rb")):
                sp.dma_start(dst[:], a[src]).then_inc(more_loads, 16)
            for dst, src in ((w["proj0_b"], "proj0_b"), (r0["router_b"], "router0_b"),
                             (r1["router_b"], "router1_b")):
                sp.dma_start(dst[:], a[src].partition_broadcast(P)).then_inc(more_loads, 16)
            sp.wait_ge(more_loads, 11 * 16)

        def start_gu(sp):
            sp.dma_start(w["gu"][:], a["gu"]).then_inc(gu_loads, 16)
            sp.dma_start(w["down"][:], a["down"]).then_inc(gu_loads, 16)

        def await_gu(sp):
            sp.wait_ge(gu_loads, 32)

        def loads2(sp):
            sp.dma_start(w["qk1"][:], a["qk1"]).then_inc(expert_loads, 16)
            sp.dma_start(w["v1"][:], a["v1"]).then_inc(expert_loads, 16)
            sp.wait_ge(expert_loads, 32)

        def loads3(sp):
            sp.dma_start(w["out1"][:], a["out1"]).then_inc(late_loads, 16)
            sp.wait_ge(late_loads, 16)

        def loads4(sp):
            sp.dma_start(w["e1_w1"][:], a["e1_w1"]).then_inc(late_loads, 16)
            sp.dma_start(w["e1_w2"][:], a["e1_w2"]).then_inc(late_loads, 16)
            sp.wait_ge(late_loads, 48)

        layer_norm_phase(nc, "n0", x, xh, xl, k["id"], glob)
        with ExitStack() as pa:
            q = Mem(nc, pa)
            z0 = q.sb("z0", [P, 5, NH, D0])
            q4 = q.sb("q4", [P, NG, S], F16)
            v0 = q.sb("v0", [P, NH, 5, 2 * D0 + 1], F16)
            with ExitStack() as pk:
                kz = Mem(nc, pk).sb("kz", [P, NH, KPAD], F16)
                project0_phase(nc, k, xh, xl, w, q4, kz, v0)
                attention0_phase(nc, k, q4, kz, v0, z0, loads1)
            w["gu"] = q.sb("w_gu", [P, E0, 2 * I0])
            w["down"] = q.sb("w_down", [P, E0, 2, C])
            out0_phase(nc, k, z0, w, s, start_gu)
            router_phase(nc, k, "g0", xh, xl, 1, r0, cw[:, :, 0:E0], acc, E0, E0, TOP0,
                         await_gu)
            experts0_phase(nc, k, xh, xl, w, cw, acc)
        update_phase(nc, "u0", x, s, acc)
        with ExitStack() as ph:
            p = Mem(nc, ph)
            w["out1"] = p.sb("w_out1", [P, H * D1 // P, C])
            wqk = p.sb("wqk1", [P, 2, H, P], F16)
            wv = p.sb("wv1", [P, 2, H * D1], F16)
            han = p.sb("han", [P, 3, H, 2 * P], F16)
            with ExitStack() as pw:
                q = Mem(nc, pw)
                w["qk1"] = q.sb("w_qk1", [P, H, P])
                w["v1"] = q.sb("w_v1", [P, H * D1])
                layer_norm_phase(nc, "n1", x, xh, xl, k["id"], None, loads2)
                prepare1_phase(nc, k, a["rb_scratch"], rb, han, wqk, wv, w)
            z1 = p.sb("z1", [P, NT, H * D1])
            attention1_phase(nc, k, xh, xl, wqk, wv, han, z1, loads3)
            out1_phase(nc, k, z1, w, s)
        w["e1_w1"] = m.sb("w_e1_w1", [P, NE1, C])
        w["e1_w2"] = m.sb("w_e1_w2", [P, NE1, C])
        router_phase(nc, k, "g1", xh, xl, 1, r1, cw, acc, E1, NE1, TOP1, loads4)
        experts1_phase(nc, k, xh, xl, w, cw, acc)
        update_phase(nc, "u1", x, s, acc, out)


def shape_constants():
    import numpy as np

    c = {name: np.zeros((P, n), np.float32) for name, n in CONSTS}
    row = np.arange(P)
    c["id"][row, row] = 1
    c["neg_id"][row, row] = -1
    c["anti"][row, P - 1 - row] = 1
    c["mask_keys"][0, BLK:P] = 1
    c["mask_keys"][0, P + 1:] = 1
    c["mask_cols"][0, :] = BIG
    for t in range(S):
        for blk in range(NBLK):
            if blk > (t + 1) // BLK:
                c["block_mask"][t % P, (t // P) * NBLK + blk] = BIG
    copy = row // D0 % 4
    c["low_q"][:, 0] = copy >= 2
    c["low_k"][:, 0] = copy % 2
    for s in "qk":
        c[f"sign_{s}"][:] = 2 * c[f"low_{s}"] - 1
    c["own"][row, row // 32] = 1
    return np.concatenate([c[name] for name, _ in CONSTS], axis=1)


def laid_out(i):
    import numpy as np

    a = {n: np.asarray(v) for n, v in i.items()}
    o = {"x": a["L0_attn_x"], "const": shape_constants()}
    o["glob"] = a["L0_attn_global_token"].reshape(C, 1)
    wt = a["L0_attn_qkv_w"].reshape(3, 4, G, 1, D0, C)
    o["qk0"] = np.repeat(wt[:2], 4, axis=3).reshape(2, 4, P, C).transpose(3, 0, 1, 2)
    o["v0"] = a["L0_attn_qkv_w"][2 * C:].T
    o["proj0"] = a["L0_attn_proj_w"].T
    o["proj0_b"] = a["L0_attn_proj_b"]
    o["router0"] = a["L0_ffn_router_weight"].T
    o["router0_b"] = a["L0_ffn_router_bias"]
    o["gu"] = a["L0_ffn_gate_up_proj"].transpose(1, 0, 2)
    o["gu_b"] = a["L0_ffn_gate_up_bias"].reshape(E0, 4, P).transpose(2, 0, 1)
    o["down"] = a["L0_ffn_down_proj"].reshape(E0, 2, P, C).transpose(2, 0, 1, 3)
    o["down_b"] = a["L0_ffn_down_bias"]
    wt = a["L1_attn_w_qkv"].reshape(D1, 3, H, C)
    o["qk1"] = wt[:, :2].transpose(3, 2, 1, 0).reshape(C, H, P)
    o["v1"] = wt[:, 2].transpose(2, 1, 0).reshape(C, H * D1)
    o["out1"] = a["L1_attn_w_out"].T.reshape(H * D1 // P, P, C).transpose(1, 0, 2)
    rb = a["L1_attn_rel_bias"].T
    o["rb"] = np.stack([rb[:, ::-1], rb], axis=1)
    o["router1"] = a["L1_ffn_router_W"]
    o["router1_b"] = a["L1_ffn_router_b"]
    o["e1_w1"] = np.concatenate([a["L1_ffn_eW1"], a["L1_ffn_sW1"][None]]).transpose(1, 0, 2)
    o["e1_b1"] = np.concatenate([a["L1_ffn_eb1"], a["L1_ffn_sb1"][None]]).T
    o["e1_w2"] = np.concatenate([a["L1_ffn_eW2"], a["L1_ffn_sW2"][None]]).transpose(1, 0, 2)
    o["e1_b2"] = np.concatenate([a["L1_ffn_eb2"], a["L1_ffn_sb2"][None]])
    return {n: np.ascontiguousarray(v) for n, v in o.items()}


def kernel(**inputs):
    import concourse.bacc as bacc
    import numpy as np
    from concourse import mybir as mb
    from concourse.bass_utils import run_bass_kernel_spmd

    nc = bacc.Bacc("TRN2", target_bir_lowering=False, num_devices=1)
    arrays = laid_out(inputs)
    a = {n: nc.dram_tensor(f"in_{n}", v.shape, mb.dt.from_np(v.dtype), kind="ExternalInput").ap()
         for n, v in arrays.items()}
    a["rb_scratch"] = nc.dram_tensor("rb_scratch", (3, H, 3 * P), mb.dt.float16,
                                     kind="Internal").ap()
    out = nc.dram_tensor("out", (B, S, C), mb.dt.float32, kind="ExternalOutput").ap()
    program(nc, a, out)
    r = run_bass_kernel_spmd(nc, [{f"in_{n}": v for n, v in arrays.items()}], core_ids=[0])
    return r.results[0]["out"]
```

```python
from contextlib import ExitStack

import concourse.bass as bass
from concourse import mybir

P = 128
F32 = mybir.dt.float32
F16 = mybir.dt.float16
BF16 = mybir.dt.bfloat16
ALU = mybir.AluOpType
ACT = mybir.ActivationFunctionType
AXX = mybir.AxisListType.X

B, S, C = 4, 512, 128
TPB = S // P
NT = B * TPB
H = 16
D0, D1 = C // H, 64
NH = B * H
G = 4
NG = NH // G
BLK = 64
NBLK = S // BLK + 1
KPAD = 5 * P
E0, TOP0, I0 = 8, 2, 256
E1, TOP1 = 15, 3
NE1 = E1 + 1
ALPHA, LIMIT, EPS = 1.702, 7.0, 1e-5
BIG = -1.0e30

FIRST = [1, 128, 256, 384, 512]
WIDTH = [513 - f for f in FIRST]
BASE = [0, WIDTH[0], WIDTH[0] + WIDTH[1], sum(WIDTH[:3]), sum(WIDTH[:4])]
PW = sum(WIDTH)
QT = [(1, 127), (128, 128), (256, 128), (384, 128), (512, 1)]


class Mem:

    def __init__(self, nc, ctx):
        self.nc, self.ctx = nc, ctx

    def sb(self, name, shape, dt=F32):
        return self.ctx.enter_context(self.nc.sbuf_tensor(name, shape, dt))

    def ps(self, name, shape, dt=F32):
        return self.ctx.enter_context(self.nc.psum_tensor(name, shape, dt))

    def sem(self, name):
        return self.ctx.enter_context(self.nc.semaphore(name))


def own_chain(eng, sem):
    count = [0]

    def link(ins):
        count[0] += 1
        ins.then_inc(sem, 1)
        eng.wait_ge(sem, count[0])

    return link


def three_passes(nc, out, wh, wl, xh, xl):
    nc.tensor.matmul(out, wh, xl, start=True, stop=False)
    nc.tensor.matmul(out, wl, xh, start=False, stop=False)
    return nc.tensor.matmul(out, wh, xh, start=False, stop=True)


def layer_norm_phase(nc, tag, x, xh, xl, ident, glob, loads=None, fills=None,
                     x_ready=None, const_ready=None, on_scalar=None, update=None,
                     after_update=None):
    with ExitStack() as ctx:
        m = Mem(nc, ctx)
        stats = m.sb(f"{tag}_stats", [P, NT, 6])
        mv = m.sb(f"{tag}_mv", [P, NT, 2])
        rstd = m.sb(f"{tag}_rstd", [P, NT])
        xn = m.sb(f"{tag}_xn", [P, NT, C])
        xt = m.ps(f"{tag}_xt", [P, B, S])
        chain = m.sem(f"{tag}_chain")
        var_ready = m.sem(f"{tag}_var")
        std_ready = m.sem(f"{tag}_std")
        xn_ready = m.sem(f"{tag}_xn_ready")
        xt_ready = m.sem(f"{tag}_xt_ready")
        hi_ready = m.sem(f"{tag}_hi_ready")
        block = ctx.enter_context(nc.Block())
        if loads is not None:
            block.sync(loads)
        if fills is not None:
            block.gpsimd(fills)
        if update is not None:
            @block.gpsimd
            def _(pool):
                update["gpsimd"](pool)
                after_update(pool)

        @block.vector
        def _(dve):
            link = own_chain(dve, chain)
            if update is not None:
                update["vector"](dve)
            for t in range(NT):
                if x_ready is not None and t % TPB == 0:
                    dve.wait_ge(x_ready[t // TPB], 16)
                if update is not None and t % TPB == 0:
                    dve.wait_ge(update["x_ready"], t // TPB + 1)
                ins = nc.vector.bn_stats(stats[:, t, :], x[:, t, :])
            link(ins)
            for t in range(NT):
                ins = nc.vector.bn_aggr(mv[:, t, :], stats[:, t, :])
            link(ins)
            nc.vector.tensor_scalar_add(rstd[:], mv[:, :, 1], EPS).then_inc(var_ready, 1)
            dve.wait_ge(std_ready, 1)
            link(nc.vector.reciprocal(rstd[:], rstd[:]))
            for t in range(NT):
                nc.vector.tensor_scalar(xn[:, t, :], x[:, t, :], mv[:, t, 0:1], rstd[:, t:t + 1],
                                        ALU.subtract, ALU.mult).then_inc(xn_ready, 1)
            for b in range(B):
                dve.wait_ge(hi_ready, b + 1)
                nc.vector.tensor_tensor(xl[:, b, 1:1 + S], xt[:, b, :], xh[:, b, 1:1 + S],
                                        ALU.subtract)
            if glob is not None:
                dve.wait_ge(const_ready, 32)
                for b in range(B):
                    ins = nc.vector.tensor_copy(xh[:, b, 0:1], glob[:])
                link(ins)
                for b in range(B):
                    nc.vector.tensor_tensor(xl[:, b, 0:1], glob[:], xh[:, 0, 0:1], ALU.subtract)

        @block.scalar
        def _(act):
            if on_scalar is not None:
                on_scalar(act)
            if update is not None:
                update["scalar"](act)
            act.wait_ge(var_ready, 1)
            nc.scalar.activation(rstd[:], rstd[:], ACT.Sqrt).then_inc(std_ready, 1)
            for b in range(B):
                act.wait_ge(xt_ready, b + 1)
                nc.scalar.activation(xh[:, b, 1:1 + S], xt[:, b, :], ACT.Copy).then_inc(hi_ready, 1)

        @block.tensor
        def _(pe):
            if const_ready is not None:
                pe.wait_ge(const_ready, 32)
            for t in range(NT):
                pe.wait_ge(xn_ready, t + 1)
                ins = nc.tensor.transpose(xt[:, t // TPB, (t % TPB) * P:(t % TPB + 1) * P],
                                          xn[:, t, :], ident[:])
                if t % TPB == TPB - 1:
                    ins.then_inc(xt_ready, 1)


def split_weights0(nc, m, w):
    parts = {"wh": m.sb("p0_wh", [P, 8, G, 4, D0], F16), "wl": m.sb("p0_wl", [P, 8, G, 4, D0], F16),
             "wvh": m.sb("p0_wvh", [P, C], F16), "wvl": m.sb("p0_wvl", [P, C], F16)}
    high = m.sem("p0_w_high")

    def copies(which):
        return w["qk0"][:, which].unsqueeze(2).to_broadcast([P, G, 4, D0])

    def scalar(act):
        for i in range(8):
            nc.scalar.activation(parts["wh"][:, i], copies(i), ACT.Copy)
        nc.scalar.activation(parts["wvh"][:], w["v0"][:], ACT.Copy).then_inc(high, 1)

    def gpsimd(pool):
        pool.wait_ge(high, 1)
        for i in range(8):
            nc.gpsimd.tensor_tensor(parts["wl"][:, i], copies(i), parts["wh"][:, i], ALU.subtract)
        nc.gpsimd.tensor_tensor(parts["wvl"][:], w["v0"][:], parts["wvh"][:], ALU.subtract)

    return parts, scalar, gpsimd


def project0_phase(nc, k, xh, xl, parts, q4, kz, v0):
    with ExitStack() as ctx:
        m = Mem(nc, ctx)
        wh = parts["wh"][:].rearrange("p (s g) j c d -> p s g (j c d)", s=2)
        wl = parts["wl"][:].rearrange("p (s g) j c d -> p s g (j c d)", s=2)
        wvh, wvl = parts["wvh"], parts["wvl"]
        signed = m.sb("p0_signed", [P, 2, S], F16)
        k4 = m.sb("p0_k4", [P, 4, S], F16)
        last = m.sb("p0_last", [P, 4], F16)
        lasts = m.sb("p0_lasts", [P, B, 4], F16)
        acc = m.ps("p0_acc", [P, 4, 512])
        klast = m.ps("p0_klast", [P, 512])
        vacc = m.ps("p0_vacc", [P, 512])
        vlast = m.ps("p0_vlast", [P, 512])
        act_spread = m.sem("p0_act_spread")
        pool_spread = m.sem("p0_pool_spread")
        dve_spread = m.sem("p0_dve_spread")
        acc_ready = m.sem("p0_acc_ready")
        signed_ready = m.sem("p0_signed_ready")
        acc_free = m.sem("p0_acc_free")
        kl_ready = m.sem("p0_kl_ready")
        kl_signed = m.sem("p0_kl_signed")
        kl_free = m.sem("p0_kl_free")
        v_ready = m.sem("p0_v_ready")
        vhi_ready = m.sem("p0_vhi_ready")
        v_free = m.sem("p0_v_free")
        passed = m.sem("p0_passed")
        block = ctx.enter_context(nc.Block())
        kgroups = kz[:, :, :].rearrange("p (n j) s -> p n j s", j=G)

        def own_head(eng, b, g, j):
            out, own = kz[:, b * 16 + (4 * g + j), 0:S], k["own"][:, j:j + 1]
            if eng is nc.scalar:
                return eng.activation(out, k4[:, g, :], ACT.Copy, scale=own)
            if eng is nc.gpsimd:
                return eng.tensor_tensor(out, k4[:, g, :], own.to_broadcast([P, S]), ALU.mult)
            return eng.tensor_scalar(out, k4[:, g, :], own, None, ALU.mult)

        @block.gpsimd
        def _(pool):
            pool.sem_inc(pool_spread, 4)
            with pool.Fori(0, B) as b:
                for g in range(4):
                    pool.wait_ge(acc_free, b * 8 + (2 * g + 6))
                    own_head(nc.gpsimd, b, g, 3).then_inc(pool_spread, 1)

        @block.vector
        def _(dve):
            dve.sem_inc(acc_free, 4)
            dve.sem_inc(kl_free, 1)
            dve.sem_inc(dve_spread, 4)
            dve.sem_inc(v_free, 1)

            def spread(b, g):
                dve.wait_ge(acc_free, b * 8 + (2 * g + 6))
                own_head(nc.vector, b, g, 0)
                own_head(nc.vector, b, g, 1).then_inc(dve_spread, 1)

            def low_v(b):
                dve.wait_ge(kl_signed, b + 1)
                nc.vector.scalar_tensor_tensor(lasts[:, b, :], klast[:, 0:4], k["low_k"],
                                               last[:], ALU.mult, ALU.subtract
                                               ).then_inc(kl_free, 1)
                dve.wait_ge(vhi_ready, b + 1)
                vb = v0[:, bass.ds(b * 16, 16), :, :]
                for t in range(TPB):
                    nc.vector.tensor_tensor(
                        vb[:, :, t, D0 + 1:2 * D0 + 1],
                        vacc[:, t * C:(t + 1) * C].rearrange("p (h d) -> p h d", h=H),
                        vb[:, :, t, 0:D0], ALU.subtract)
                nc.vector.tensor_tensor(
                    vb[0:1, :, TPB, D0 + 1:2 * D0 + 1],
                    vlast[0:1, 0:C].rearrange("p (h d) -> p h d", h=H),
                    vb[0:1, :, TPB, 0:D0], ALU.subtract).then_inc(v_free, 1)

            with dve.Fori(0, B) as b:
                for g in range(4):
                    for s in range(2):
                        u = 2 * g + s
                        dve.wait_ge(signed_ready, b * 8 + (u + 1))
                        out = q4[:, b * 4 + g, :] if s == 0 else k4[:, g, :]
                        low = k["low_q"] if s == 0 else k["low_k"]
                        if s == 1:
                            dve.wait_ge(dve_spread, b * 4 + (g + 1))
                            dve.wait_ge(act_spread, b * 4 + (g + 1))
                            dve.wait_ge(pool_spread, b * 4 + (g + 1))
                        nc.vector.scalar_tensor_tensor(out, acc[:, u % 4, :], low, signed[:, s, :],
                                                       ALU.mult, ALU.subtract
                                                       ).then_inc(acc_free, 1)
                    if g > 0:
                        spread(b, g - 1)
                    if g == 2:
                        low_v(b)
                spread(b, 3)
            dve.wait_ge(kl_free, B + 1)
            for j in range(G):
                nc.vector.tensor_scalar(kgroups[:, :, j, S],
                                        lasts[:].rearrange("p b g -> p (b g)"),
                                        k["own"][:, j:j + 1], None, ALU.mult)

        @block.scalar
        def _(act):
            act.preload_act_table(ACT.Exp)
            act.sem_inc(act_spread, 4)

            def spread(b, g):
                act.wait_ge(acc_free, b * 8 + (2 * g + 6))
                act.sem_inc(passed, 1)
                own_head(nc.scalar, b, g, 2).then_inc(act_spread, 1)

            def high_v(b):
                act.wait_ge(kl_ready, b + 1)
                nc.scalar.activation(last[:], klast[:, 0:4], ACT.Copy,
                                     scale=k["sign_k"]).then_inc(kl_signed, 1)
                act.wait_ge(v_ready, b + 1)
                act.sem_inc(passed, 1)
                vb = v0[:, bass.ds(b * 16, 16), :, :]
                for t in range(TPB):
                    nc.scalar.activation(vb[:, :, t, 0:D0],
                                         vacc[:, t * C:(t + 1) * C].rearrange(
                                             "p (h d) -> p h d", h=H), ACT.Copy)
                nc.scalar.activation(vb[0:1, :, TPB, 0:D0],
                                     vlast[0:1, 0:C].rearrange("p (h d) -> p h d", h=H),
                                     ACT.Copy).then_inc(vhi_ready, 1)

            with act.Fori(0, B) as b:
                for u in range(8):
                    act.wait_ge(acc_ready, b * 8 + (u + 1))
                    act.wait_ge(acc_free, b * 8 + (u + 3))
                    nc.scalar.activation(signed[:, u % 2, :], acc[:, u % 4, :], ACT.Copy,
                                         scale=k["sign_q"] if u % 2 == 0 else k["sign_k"]
                                         ).then_inc(signed_ready, 1)
                    if u % 2 == 1 and u > 1:
                        spread(b, u // 2 - 1)
                    if u == 3:
                        high_v(b)
                spread(b, 3)

        @block.tensor
        def _(pe):
            def project_v(b):
                pe.wait_ge(kl_free, b + 1)
                for g in range(4):
                    ins = three_passes(nc, klast[:, g:g + 1], wh[:, 1, g, :], wl[:, 1, g, :],
                                       xh[:, b, S:S + 1], xl[:, b, S:S + 1])
                ins.then_inc(kl_ready, 1)
                pe.wait_ge(v_free, b + 1)
                for t in range(TPB):
                    three_passes(nc, vacc[:, t * C:(t + 1) * C], xh[:, b, t * P:(t + 1) * P],
                                 xl[:, b, t * P:(t + 1) * P], wvh[:], wvl[:])
                three_passes(nc, vlast[0:1, 0:C], xh[:, b, S:S + 1], xl[:, b, S:S + 1],
                             wvh[:], wvl[:]).then_inc(v_ready, 1)

            with pe.Fori(0, B) as b:
                for g in range(4):
                    for s in range(2):
                        u = 2 * g + s
                        pe.wait_ge(acc_free, b * 8 + (u + 1))
                        off = 1 - s
                        three_passes(nc, acc[:, u % 4, :], wh[:, s, g, :], wl[:, s, g, :],
                                     xh[:, b, off:off + S], xl[:, b, off:off + S]
                                     ).then_inc(acc_ready, 1)
                    if g == 1:
                        project_v(b)


def by_groups(eng, count, slot, per=4):
    for c in range(per):
        slot(0, c, c == 0, False)
    with eng.Fori(1, count - 1) as k:
        for c in range(per):
            slot(k, c, False, False)
    for c in range(per):
        slot(count - 1, c, False, c == per - 1)


def shift(k, c, by, per=4):
    return k + (c + by) // per, (c + by) % per



def attention0_phase(nc, k, q4, kz, v0, z0, loads):
    scale = float(D0) ** -0.5
    with ExitStack() as ctx:
        m = Mem(nc, ctx)
        smax = m.ps("a0_smax", [P, 2, 2, 512])
        st = m.ps("a0_st", [P, 3, 512])
        o = m.ps("a0_o", [P, 2, 5, 2 * D0 + 1])
        bm = m.sb("a0_bm", [P, TPB, NBLK])
        bmm = m.sb("a0_bmm", [P, TPB, NBLK])
        mx = m.sb("a0_mx", [P, 2, TPB], F16)
        p32 = m.sb("a0_p32", [P, 2, PW])
        ph = m.sb("a0_ph", [P, 4, PW], F16)
        pl = m.sb("a0_pl", [P, 4, PW], F16)
        r = m.sb("a0_r", [P, 2, 2, 5])
        zu = m.sb("a0_zu", [P, 2, 2, 5, 2 * D0 + 1])
        preset = m.sem("a0_preset")
        smax_ready = m.sem("a0_smax_ready")
        smax_free = m.sem("a0_smax_free")
        bm_ready = m.sem("a0_bm_ready")
        mx_ready = m.sem("a0_mx_ready")
        st_ready = m.sem("a0_st_ready")
        st_free = m.sem("a0_st_free")
        hi_ready = m.sem("a0_hi_ready")
        lo_ready = m.sem("a0_lo_ready")
        pv_done = m.sem("a0_pv_done")
        o_free = m.sem("a0_o_free")
        r_ready = m.sem("a0_r_ready")
        block = ctx.enter_context(nc.Block())
        block.sync(loads)

        @block.tensor
        def _(pe):
            def scores(kk, c, u):
                n = kk * 4 + c
                pe.wait_ge(smax_free, n * 2 + (u + 1))
                for i in (2 * u, 2 * u + 1):
                    w = 5 * BLK if u == 0 else S
                    ins = nc.tensor.matmul(smax[:, u, i % 2, 0:w], q4[:, kk, i * P:(i + 1) * P],
                                           kz[:, n, 0:w], start=True, stop=True)
                if u == 0:
                    ins = nc.tensor.matmul(smax[:, 0, 0, 5 * BLK:5 * BLK + 1],
                                           q4[:, kk, 3 * P:4 * P], kz[:, n, S:S + 1],
                                           start=True, stop=True)
                ins.then_inc(smax_ready, 1)

            def transposed(kk, c, u):
                n = kk * 4 + c
                pe.wait_ge(st_free, n * 3 + (u + 1))
                for ch in ((0,), (1,), (2, 3, 4))[u]:
                    col = BASE[ch] - BASE[2] if u == 2 else 0
                    first = FIRST[ch]
                    keys = slice(ch * P, (ch + 1) * P)
                    nc.tensor.matmul(st[:, u, col:col + WIDTH[ch]], kz[:, n, keys],
                                     q4[:, kk, first - 1:S], start=True, stop=False)
                    if ch < 4:
                        w = P * ch + BLK - first
                        nc.tensor.matmul(st[:, u, col:col + w], k["mask_keys"][:, 0, :],
                                         k["mask_cols"][:, 0:w], start=False, stop=False)
                    else:
                        nc.tensor.matmul(st[:, u, col:col + 1], k["mask_keys"][:, 1, :],
                                         k["mask_cols"][:, 0:1], start=False, stop=False)
                    for i in range(max(ch - 1, 0), TPB):
                        lo = max(first - 1, i * P)
                        at = col + lo - (first - 1)
                        w = (i + 1) * P - lo
                        ins = nc.tensor.matmul(st[:, u, at:at + w],
                                               mx[:, c % 2, i:i + 1].to_broadcast([P, P]),
                                               k["neg_id16"][:, P - w:P],
                                               start=False, stop=i == TPB - 1)
                ins.then_inc(st_ready, 1)

            def weighted(kk, c):
                n = kk * 4 + c
                pe.wait_ge(hi_ready, n + 1)
                pe.wait_ge(lo_ready, n + 3)
                if c % 2 == 0:
                    pe.wait_ge(o_free, kk * 2 + (c // 2 + 1))
                for qi, (q0, cnt) in enumerate(QT):
                    ob = o[0:cnt, c % 2, qi, :]
                    for ch in range(qi + 1):
                        a = BASE[ch] + q0 - FIRST[ch]
                        nc.tensor.matmul(ob, ph[:, c, a:a + cnt], v0[:, n, ch, :],
                                         start=ch == 0, stop=False)
                        ins = nc.tensor.matmul(ob[:, 0:D0 + 1], pl[:, c, a:a + cnt],
                                               v0[:, n, ch, 0:D0 + 1], start=False,
                                               stop=ch == qi)
                ins.then_inc(pv_done, 1)

            pe.sem_inc(pv_done, 4)
            pe.wait_ge(preset, 1)
            scores(0, 0, 0)
            scores(0, 0, 1)

            def slot(kk, c, first, final):
                if not final:
                    scores(*shift(kk, c, 1), 0)
                    scores(*shift(kk, c, 1), 1)
                pe.wait_ge(mx_ready, kk * 4 + (c + 1))
                for u in range(3):
                    transposed(kk, c, u)
                if not (isinstance(kk, int) and kk == 0 and c < 2):
                    weighted(*shift(kk, c, -2))

            by_groups(pe, NG, slot)
            weighted(NG - 1, 2)
            weighted(NG - 1, 3)

        @block.vector
        def _(dve):
            dve.sem_inc(smax_free, 2)
            dve.sem_inc(o_free, 1)
            nc.vector.memset(bm[:], 0.0)
            nc.vector.memset(o[:], 1.0).then_inc(preset, 1)
            dve.wait_ge(preset, 1)

            def maxima(kk, c):
                n = kk * 4 + c
                dve.wait_ge(smax_ready, n * 2 + 1)
                nc.vector.tensor_copy(bm[:, TPB - 1, NBLK - 1:NBLK],
                                      smax[:, 0, 0, 5 * BLK:5 * BLK + 1])
                nc.vector.reduce_max(bm[:, 0:2, 0:5], smax[:, 0, :, 0:5 * BLK].rearrange(
                    "p t (a b) -> p t a b", b=BLK), AXX).then_inc(smax_free, 1)
                dve.wait_ge(smax_ready, n * 2 + 2)
                nc.vector.reduce_max(bm[:, 2:4, 0:8], smax[:, 1, :, :].rearrange(
                    "p t (a b) -> p t a b", b=BLK), AXX).then_inc(smax_free, 1)
                dve.wait_ge(smax_free, n * 2 + 4)
                nc.vector.tensor_tensor(bmm[:], bm[:], k["block_mask"], ALU.add
                                        ).then_inc(bm_ready, 1)
                dve.wait_ge(bm_ready, n + 1)
                nc.vector.reduce_max(mx[:, c % 2, :], bmm[:], AXX).then_inc(mx_ready, 1)

            def normalise(kk, c):
                n = kk * 4 + c
                dve.wait_ge(pv_done, n + 5)
                nc.vector.reciprocal(r[:, c // 2], o[:, :, :, D0]).then_inc(r_ready, 1)
                dve.wait_ge(r_ready, kk * 2 + (c // 2 + 1))
                nc.vector.tensor_tensor(
                    zu[:, c // 2], o[:], r[:, c // 2].unsqueeze(3).to_broadcast(
                        [P, 2, 5, 2 * D0 + 1]), ALU.mult).then_inc(o_free, 1)
                dve.wait_ge(o_free, kk * 2 + (c // 2 + 2))
                parts = zu[:, c // 2].rearrange("p h t d -> p t h d")
                nc.vector.tensor_tensor(z0[:, :, bass.ds(kk * 4 + (c - 1), 2), :],
                                        parts[:, :, :, 0:D0], parts[:, :, :, D0 + 1:], ALU.add)

            maxima(0, 0)

            def slot(kk, c, first, final):
                if c % 2 == 0 and not (isinstance(kk, int) and kk == 0):
                    normalise(*shift(kk, c, -3))
                if not final:
                    maxima(*shift(kk, c, 1))

            by_groups(dve, NG, slot)
            normalise(NG - 1, 1)
            normalise(NG - 1, 3)

        @block.scalar
        def _(act):
            act.sem_inc(st_free, 3)
            act.preload_act_table(ACT.Exp)

            def slot(kk, c, first, final):
                n = kk * 4 + c
                act.wait_ge(lo_ready, n + 1)
                act.wait_ge(pv_done, n + 1)
                for u in range(3):
                    a, w = BASE[u], (PW - BASE[2] if u == 2 else WIDTH[u])
                    act.wait_ge(st_ready, n * 3 + (u + 1))
                    nc.scalar.activation(p32[:, c % 2, a:a + w], st[:, u, 0:w],
                                         ACT.Exp, scale=scale).then_inc(st_free, 1)
                act.wait_ge(st_free, n * 3 + 6)
                nc.scalar.activation(ph[:, c, :], p32[:, c % 2, :], ACT.Copy
                                     ).then_inc(hi_ready, 1)

            by_groups(act, NG, slot)

        @block.gpsimd
        def _(pool):
            pool.sem_inc(lo_ready, 2)

            def slot(kk, c, first, final):
                n = kk * 4 + c
                pool.wait_ge(hi_ready, n + 1)
                pool.wait_ge(pv_done, n + 1)
                nc.gpsimd.tensor_tensor(pl[:, c, :], p32[:, c % 2, :], ph[:, c, :],
                                        ALU.subtract).then_inc(lo_ready, 1)

            by_groups(pool, NG, slot)


def out0_job(nc, m, k, z0, w, s):
    zt = m.ps("o0_zt", [P, 2, S])
    out = m.ps("o0_out", [P, B, S])
    zts = m.sb("o0_zts", [P, 2, S])
    zt_ready = m.sem("o0_zt_ready")
    zts_ready = m.sem("o0_zts_ready")
    out_ready = m.sem("o0_out_ready")
    s_ready = m.sem("o0_s_ready")

    def tensor(pe, between):
        def turn(b):
            for qi, (q0, cnt) in enumerate(QT):
                ins = nc.tensor.transpose(zt[:, b % 2, q0 - 1:q0 - 1 + cnt],
                                          z0[0:cnt, qi, b * H:(b + 1) * H, :],
                                          k["id"][0:cnt, 0:cnt])
            ins.then_inc(zt_ready, 1)

        turn(0)
        turn(1)
        for b in range(B):
            pe.wait_ge(zts_ready, b + 1)
            for i in range(TPB):
                ins = nc.tensor.matmul(out[:, b, i * C:(i + 1) * C],
                                       zts[:, b % 2, i * P:(i + 1) * P], w["proj0"][:],
                                       start=True, stop=True)
            ins.then_inc(out_ready, 1)
            if b + 2 < B:
                turn(b + 2)
        between(0)
        between(1)
        pe.wait_ge(s_ready, B)
        for b in range(2, B + 2):
            between(b)

    def scalar(act, between):
        for b in range(B):
            act.wait_ge(zt_ready, b + 1)
            if b >= 2:
                act.wait_ge(out_ready, b - 1)
            nc.scalar.activation(zts[:, b % 2, :], zt[:, b % 2, :], ACT.Copy
                                 ).then_inc(zts_ready, 1)
        for b in range(B):
            between(b)

    def vector(dve):
        for b in range(B):
            dve.wait_ge(out_ready, b + 1)
            nc.vector.tensor_tensor(
                s[:, b * TPB:(b + 1) * TPB, :], out[:, b, :].rearrange("p (t c) -> p t c", t=TPB),
                w["proj0_b"][:].unsqueeze(1).to_broadcast([P, TPB, C]), ALU.add
                ).then_inc(s_ready, 1)

    return {"tensor": tensor, "scalar": scalar, "vector": vector,
            "banks": (zt, out)}


def router_phase(nc, k, tag, xh, xl, off, w, cw, acc, n_routed, n_all, top, make_job, loads,
                 ahead_vector, ahead_gpsimd=None):
    spare = 8 - top
    wide = n_routed + spare
    with ExitStack() as ctx:
        m = Mem(nc, ctx)
        rwh = m.sb(f"{tag}_rwh", [P, n_routed], F16)
        rwl = m.sb(f"{tag}_rwl", [P, n_routed], F16)
        lg_bank = m.ps(f"{tag}_lg", [P, 1, S])
        lg = lg_bank[:, 0, 0:NT * n_routed].rearrange("p (t e) -> p t e", e=n_routed)
        job = make_job(m)
        ct, ob = job["banks"]
        ct = lg_bank[:, 0:1, :] if ct is None else ct
        depth, ob_depth = min(ob.shape[1], 2), ob.shape[1]
        cts = m.sb(f"{tag}_cts", [n_all, B, S])
        e = m.sb(f"{tag}_e", [P, NT, n_routed])
        red = m.sb(f"{tag}_red", [P, NT])
        row = m.sb(f"{tag}_row", [P, NT, wide])
        rest = m.sb(f"{tag}_rest", [P, NT, wide])
        top8 = m.sb(f"{tag}_top8", [P, NT, 8])
        chain = m.sem(f"{tag}_chain")
        rw_ready = m.sem(f"{tag}_rw_ready")
        lg_ready = m.sem(f"{tag}_lg_ready")
        shifted = m.sem(f"{tag}_shifted")
        exp_ready = m.sem(f"{tag}_exp_ready")
        cw_ready = m.sem(f"{tag}_cw_ready")
        ct_ready = m.sem(f"{tag}_ct_ready")
        cts_ready = m.sem(f"{tag}_cts_ready")
        ob_ready = m.sem(f"{tag}_ob_ready")
        ob_free = m.sem(f"{tag}_ob_free")
        block = ctx.enter_context(nc.Block())
        block.sync(loads)
        if "gpsimd" in job:
            block.gpsimd(job["gpsimd"])
        if ahead_gpsimd is not None:
            block.gpsimd(ahead_gpsimd)

        @block.vector
        def _(dve):
            link = own_chain(dve, chain)
            link(nc.vector.tensor_copy(rwh[:], w["router"][:]))
            nc.vector.tensor_tensor(rwl[:], w["router"][:], rwh[:], ALU.subtract
                                    ).then_inc(rw_ready, 1)
            if "vector_first" in job:
                job["vector_first"](dve)
            for i in range(spare):
                nc.vector.memset(row[:, :, n_routed + i:n_routed + i + 1], 2.0 + i)
            if n_all > n_routed:
                nc.vector.memset(cw[:, :, n_routed:n_all], 1.0)
            dve.wait_ge(lg_ready, 1)
            link(nc.vector.tensor_tensor(e[:], lg, w["router_b"][:].unsqueeze(1).to_broadcast(
                [P, NT, n_routed]), ALU.add))
            link(nc.vector.reduce_max(red[:], e[:], AXX))
            nc.vector.tensor_tensor(e[:], e[:], red[:].unsqueeze(2).to_broadcast(
                [P, NT, n_routed]), ALU.subtract).then_inc(shifted, 1)
            dve.wait_ge(exp_ready, 1)
            link(nc.vector.reduce_sum(red[:], e[:], AXX))
            link(nc.vector.reciprocal(red[:], red[:]))
            link(nc.vector.tensor_tensor(row[:, :, 0:n_routed], e[:], red[:].unsqueeze(2)
                                         .to_broadcast([P, NT, n_routed]), ALU.mult))
            for t in range(NT):
                ins = nc.vector.max(top8[:, t, :], row[:, t, :])
            link(ins)
            for t in range(NT):
                ins = nc.vector.match_replace(rest[:, t, :], top8[:, t, :], row[:, t, :], 0.0)
            link(ins)
            nc.vector.tensor_tensor(cw[:, :, 0:n_routed], row[:, :, 0:n_routed],
                                    rest[:, :, 0:n_routed], ALU.subtract).then_inc(cw_ready, 1)
            job["vector"](dve)
            ahead_vector(dve)
            for b in range(B):
                dve.wait_ge(ob_ready, b + 1)
                nc.vector.tensor_copy(acc[:, b * TPB:(b + 1) * TPB, :],
                                      ob[:, b % ob_depth, :].rearrange("p (t c) -> p t c", t=TPB)
                                      ).then_inc(ob_free, 1)

        @block.scalar
        def _(act):
            act.wait_ge(shifted, 1)
            nc.scalar.activation(e[:], e[:], ACT.Exp).then_inc(exp_ready, 1)

            def between(b):
                if 0 <= b < B:
                    act.wait_ge(ct_ready, b + 1)
                    nc.scalar.activation(cts[:, b, :], ct[0:n_all, b % depth, :], ACT.Copy
                                         ).then_inc(cts_ready, 1)

            job["scalar"](act, between)

        @block.tensor
        def _(pe):
            pe.wait_ge(rw_ready, 1)
            for t in range(NT):
                b, a = t // TPB, off + (t % TPB) * P
                ins = three_passes(nc, lg[:, t, :], xh[:, b, a:a + P], xl[:, b, a:a + P],
                                   rwh[:], rwl[:])
            ins.then_inc(lg_ready, 1)

            def between(b):
                if b == 0:
                    pe.wait_ge(cw_ready, 1)
                done = b - depth
                if 0 <= done < B:
                    pe.wait_ge(cts_ready, done + 1)
                    if done >= ob_depth:
                        pe.wait_ge(ob_free, done - ob_depth + 1)
                    for i in range(TPB):
                        ins = nc.tensor.matmul(ob[:, done % ob_depth, i * C:(i + 1) * C],
                                               cts[:, done, i * P:(i + 1) * P], w["out_b"][:],
                                               start=True, stop=True)
                    ins.then_inc(ob_ready, 1)
                if 0 <= b < B:
                    for i in range(TPB):
                        ins = nc.tensor.transpose(ct[0:n_all, b % depth, i * P:(i + 1) * P],
                                                  cw[:, b * TPB + i, :], k["id"][:])
                    ins.then_inc(ct_ready, 1)

            job["tensor"](pe, between)


def split_experts0(nc, m, w, loaded):
    wh = m.sb("e0_wh", [P, E0, 2 * I0], F16)
    wl = m.sb("e0_wl", [P, E0, 2 * I0], F16)
    high = m.sem("e0_w_high")
    half = E0 // 2

    def vector(dve):
        dve.wait_ge(loaded, 16)
        nc.vector.tensor_copy(wh[:], w["gu"][:]).then_inc(high, 1)
        dve.wait_ge(high, 1)
        nc.vector.tensor_tensor(wl[:, 0:half], w["gu"][:, 0:half], wh[:, 0:half], ALU.subtract)

    def gpsimd(pool):
        pool.wait_ge(high, 1)
        nc.gpsimd.tensor_tensor(wl[:, half:E0], w["gu"][:, half:E0], wh[:, half:E0],
                                ALU.subtract)

    return wh, wl, vector, gpsimd


def experts0_phase(nc, k, xh, xl, w, wh, wl, cw, acc, ahead):
    U = 2 * B
    with ExitStack() as ctx:
        m = Mem(nc, ctx)
        upb = m.sb("e0_upb", [P, E0, 2])
        gate = m.sb("e0_gate", [P, 4, S])
        sig = m.sb("e0_sig", [P, 4, S])
        up = m.sb("e0_up", [P, 8, S])
        hid = m.sb("e0_hid", [P, 4, S])
        gu = m.ps("e0_gu", [P, 2, 2, S])
        out = m.ps("e0_out", [P, 4, S])
        upb_ready = m.sem("e0_upb_ready")
        gate_made = m.sem("e0_gate_made")
        up_made = m.sem("e0_up_made")
        gate_biased = m.sem("e0_gate_biased")
        up_biased = m.sem("e0_up_biased")
        gate_ready = m.sem("e0_gate_ready")
        up_ready = m.sem("e0_up_ready")
        sig_ready = m.sem("e0_sig_ready")
        gs_ready = m.sem("e0_gs_ready")
        hid_ready = m.sem("e0_hid_ready")
        out_ready = m.sem("e0_out_ready")
        out_free = m.sem("e0_out_free")
        passed = m.sem("e0_passed")
        block = ctx.enter_context(nc.Block())
        block.sync(ahead["sync"])

        def before(e, u, by, per=U):
            ge, gu_ = shift(e, u, -by, per)
            return None if isinstance(ge, int) and ge < 0 else (ge, gu_)

        @block.gpsimd
        def _(pool):
            pool.sem_inc(gs_ready, 4)

            def slot(e, u, first, final):
                pool.wait_ge(sig_ready, e * U + (u + 1))
                nc.gpsimd.tensor_tensor(sig[:, u % 4, :], gate[:, u % 4, :], sig[:, u % 4, :],
                                        ALU.mult).then_inc(gs_ready, 1)
                if isinstance(e, int):
                    ahead["split" if e == 0 else "tables"](pool, u)

            by_groups(pool, E0, slot, U)

        @block.scalar
        def _(act):
            act.sem_inc(gate_biased, 2)
            act.sem_inc(up_biased, 2)
            act.preload_act_table(ACT.Sigmoid)
            act.wait_ge(upb_ready, 1)

            def sigmoid(e, u):
                act.wait_ge(gate_ready, e * U + (u + 1))
                act.wait_ge(hid_ready, e * U + (u + 5))
                nc.scalar.activation(sig[:, u % 4, :], gate[:, u % 4, :], ACT.Sigmoid,
                                     scale=ALPHA).then_inc(sig_ready, 1)

            def slot(e, u, first, final):
                n1 = e * U + (u + 1)
                act.wait_ge(gate_made, n1)
                act.wait_ge(gs_ready, n1)
                act.sem_inc(passed, 1)
                nc.scalar.activation(gate[:, u % 4, :], gu[:, u % 2, 0, :], ACT.Identity,
                                     bias=w["gu_b"][:, e, u % 2:u % 2 + 1]
                                     ).then_inc(gate_biased, 1)
                if not first:
                    sigmoid(*before(e, u, 1))
                act.wait_ge(up_made, n1)
                act.wait_ge(hid_ready, n1)
                act.sem_inc(passed, 1)
                nc.scalar.activation(up[:, u, :], gu[:, u % 2, 1, :], ACT.Identity,
                                     bias=upb[:, e, u % 2:u % 2 + 1]).then_inc(up_biased, 1)
                if isinstance(e, int) and e == 0:
                    ahead["scalar"](act, u)

            by_groups(act, E0, slot, U)
            sigmoid(E0 - 1, U - 1)

        @block.vector
        def _(dve):
            dve.sem_inc(hid_ready, 8)
            dve.sem_inc(out_free, 4)
            nc.vector.tensor_scalar_add(upb[:], w["gu_b"][:, :, 2:4], 1.0).then_inc(upb_ready, 1)

            def product(e, u):
                dve.wait_ge(up_ready, e * U + (u + 1))
                dve.wait_ge(gs_ready, e * U + (u + 5))
                dve.wait_ge(out_ready, e * (U // 2) + (u // 2 + 1))
                nc.vector.tensor_tensor(hid[:, u % 4, :], up[:, u, :], sig[:, u % 4, :],
                                        ALU.mult).then_inc(hid_ready, 1)

            def accumulate(e, b):
                g = e * B + b
                dve.wait_ge(out_ready, g + 3)
                dve.wait_ge(out_free, g + 1)
                for i in range(TPB):
                    t = b * TPB + i
                    ins = nc.vector.scalar_tensor_tensor(
                        acc[:, t, :], out[:, b % 4, i * C:(i + 1) * C], cw[:, t, bass.ds(e, 1)],
                        acc[:, t, :], ALU.mult, ALU.add)
                ins.then_inc(out_free, 1)

            def slot(e, u, first, final):
                dve.wait_ge(gate_biased, e * U + (u + 3))
                nc.vector.tensor_scalar(gate[:, u % 4, :], gate[:, u % 4, :], LIMIT, None, ALU.min
                                        ).then_inc(gate_ready, 1)
                if before(e, u, 2):
                    product(*before(e, u, 2))
                dve.wait_ge(up_biased, e * U + (u + 3))
                nc.vector.tensor_scalar(up[:, u, :], up[:, u, :], LIMIT + 1.0, 1.0 - LIMIT,
                                        ALU.min, ALU.max).then_inc(up_ready, 1)
                if u % 2 == 0 and before(e, u // 2, 3, B):
                    accumulate(*before(e, u // 2, 3, B))

            by_groups(dve, E0, slot, U)
            product(E0 - 1, U - 2)
            product(E0 - 1, U - 1)
            for b in range(1, B):
                accumulate(E0 - 1, b)

        @block.tensor
        def _(pe):
            pe.sem_inc(out_ready, 2)

            def down(e, b):
                pe.wait_ge(hid_ready, e * U + (2 * b + 10))
                pe.wait_ge(out_free, e * B + (b + 1))
                for i in range(TPB):
                    for half in range(2):
                        ins = nc.tensor.matmul(out[:, b % 4, i * C:(i + 1) * C],
                                               hid[:, (2 * b + half) % 4, i * P:(i + 1) * P],
                                               w["down"][:, e, half, :],
                                               start=half == 0, stop=half == 1)
                ins.then_inc(out_ready, 1)

            def slot(e, u, first, final):
                b, half = u // 2, u % 2
                pe.wait_ge(gate_biased, e * U + (u + 1))
                pe.wait_ge(up_biased, e * U + (u + 1))
                for s, made in ((0, gate_made), (1, up_made)):
                    rows = slice(s * I0 + half * P, s * I0 + (half + 1) * P)
                    three_passes(nc, gu[:, u % 2, s, :], wh[:, e, rows], wl[:, e, rows],
                                 xh[:, b, 1:1 + S], xl[:, b, 1:1 + S]).then_inc(made, 1)
                if half == 1 and before(e, b, 2, B):
                    down(*before(e, b, 2, B))

            by_groups(pe, E0, slot, U)
            down(E0 - 1, B - 2)
            down(E0 - 1, B - 1)


def split_experts1(nc, m, w, loaded):
    parts = [m.sb(f"e1_{n}", [P, NE1, C], F16) for n in ("w1h", "w1l", "w2h", "w2l")]
    high = m.sem("e1_w_high")

    def vector(dve):
        dve.wait_ge(loaded, 48)
        for i, name in enumerate(("e1_w1", "e1_w2")):
            nc.vector.tensor_copy(parts[2 * i][:], w[name][:]).then_inc(high, 1)
        dve.wait_ge(high, 2)
        for i, name in enumerate(("e1_w1", "e1_w2")):
            nc.vector.tensor_tensor(parts[2 * i + 1][:], w[name][:], parts[2 * i][:],
                                    ALU.subtract)

    return parts, vector


def experts1_phase(nc, k, xh, xl, w, parts, cw, acc):
    with ExitStack() as ctx:
        m = Mem(nc, ctx)
        w1h, w1l, w2h, w2l = parts
        hid = m.sb("e1_hid", [P, 4, S])
        hh = m.sb("e1_hh", [P, 4, S], F16)
        hl = m.sb("e1_hl", [P, 4, S], F16)
        a = m.ps("e1_a", [P, 4, S])
        out = m.ps("e1_out", [P, 4, S])
        a_ready = m.sem("e1_a_ready")
        hid_ready = m.sem("e1_hid_ready")
        lo_ready = m.sem("e1_lo_ready")
        out_ready = m.sem("e1_out_ready")
        out_free = m.sem("e1_out_free")
        passed = m.sem("e1_passed")
        block = ctx.enter_context(nc.Block())

        def before(e, b, by):
            pe_, pb = shift(e, b, -by)
            return None if isinstance(pe_, int) and pe_ < 0 else (pe_, pb)

        @block.scalar
        def _(act):
            act.sem_inc(hid_ready, 4)
            act.preload_act_table(ACT.Relu)

            def slot(e, b, first, final):
                n = e * B + b
                act.wait_ge(a_ready, n + 1)
                act.wait_ge(lo_ready, n + 1)
                act.wait_ge(out_ready, n + 1)
                act.sem_inc(passed, 1)
                for to in (hid, hh):
                    ins = nc.scalar.activation(to[:, b, :], a[:, b, :], ACT.Relu,
                                               bias=w["e1_b"][:, bass.ds(e, 1)])
                ins.then_inc(hid_ready, 1)

            by_groups(act, NE1, slot)
            act.preload_act_table(ACT.Sigmoid)

        @block.vector
        def _(dve):
            dve.sem_inc(out_free, 4)

            def accumulate(e, b):
                n = e * B + b
                dve.wait_ge(out_ready, n + 5)
                dve.wait_ge(out_free, n + 1)
                for i in range(TPB):
                    t = b * TPB + i
                    ins = nc.vector.scalar_tensor_tensor(
                        acc[:, t, :], out[:, b, i * C:(i + 1) * C], cw[:, t, bass.ds(e, 1)],
                        acc[:, t, :], ALU.mult, ALU.add)
                ins.then_inc(out_free, 1)

            by_groups(dve, NE1, lambda e, b, first, final: accumulate(e, b))

        @block.gpsimd
        def _(pool):
            pool.sem_inc(lo_ready, 4)

            def slot(e, b, first, final):
                n = e * B + b
                pool.wait_ge(hid_ready, n + 5)
                pool.wait_ge(out_ready, n + 1)
                nc.gpsimd.tensor_tensor(hl[:, b, :], hid[:, b, :], hh[:, b, :], ALU.subtract
                                        ).then_inc(lo_ready, 1)

            by_groups(pool, NE1, slot)

        @block.tensor
        def _(pe):
            pe.sem_inc(out_ready, 4)

            def down(e, b):
                n = e * B + b
                pe.wait_ge(lo_ready, n + 5)
                pe.wait_ge(out_free, n + 1)
                for i in range(TPB):
                    part = slice(i * P, (i + 1) * P)
                    ins = three_passes(nc, out[:, b, part], hh[:, b, part], hl[:, b, part],
                                       w2h[:, e, :], w2l[:, e, :])
                ins.then_inc(out_ready, 1)

            def slot(e, b, first, final):
                pe.wait_ge(hid_ready, e * B + (b + 1))
                three_passes(nc, a[:, b, :], w1h[:, e, :], w1l[:, e, :],
                             xh[:, b, 1:1 + S], xl[:, b, 1:1 + S]).then_inc(a_ready, 1)
                if before(e, b, 3):
                    down(*before(e, b, 3))

            by_groups(pe, NE1, slot)
            for b in range(1, B):
                down(NE1 - 1, b)


def update_job(nc, m, tag, x, s, acc):
    sig = m.sb(f"{tag}_sig", [P, NT, C])
    sig_ready = m.sem(f"{tag}_sig_ready")
    first_prod = m.sem(f"{tag}_first_prod")
    prod_ready = m.sem(f"{tag}_prod_ready")
    gated = m.sem(f"{tag}_gated")
    x_ready = m.sem(f"{tag}_x_ready")
    part = lambda t, b: t[:, b * TPB:(b + 1) * TPB, :]

    def scalar(act):
        for b in range(B):
            nc.scalar.activation(part(sig, b), part(acc, b), ACT.Sigmoid).then_inc(sig_ready, 1)

    def gpsimd(pool):
        for b in range(1, B):
            nc.gpsimd.tensor_tensor(part(s, b), part(s, b), part(acc, b), ALU.mult
                                    ).then_inc(prod_ready, 1)

    def vector(dve):
        def add(b):
            dve.wait_ge(gated, b + 1)
            nc.vector.tensor_tensor(part(x, b), part(x, b), part(s, b), ALU.add
                                    ).then_inc(x_ready, 1)

        nc.vector.tensor_tensor(part(s, 0), part(s, 0), part(acc, 0), ALU.mult
                                ).then_inc(first_prod, 1)
        for b in range(B):
            dve.wait_ge(sig_ready, b + 1)
            if b == 0:
                dve.wait_ge(first_prod, 1)
            else:
                dve.wait_ge(prod_ready, b)
            nc.vector.tensor_tensor(part(s, b), part(s, b), part(sig, b), ALU.mult
                                    ).then_inc(gated, 1)
            if b >= 1:
                add(b - 1)
        add(B - 1)

    return {"scalar": scalar, "gpsimd": gpsimd, "vector": vector, "x_ready": x_ready}


def last_update_phase(nc, x, s, acc, out_dram):
    with ExitStack() as ctx:
        m = Mem(nc, ctx)
        job = update_job(nc, m, "u1", x, s, acc)
        stored = m.sem("u1_stored")
        block = ctx.enter_context(nc.Block())
        block.scalar(job["scalar"])
        block.gpsimd(job["gpsimd"])
        block.vector(job["vector"])

        @block.sync
        def _(sp):
            for b in range(B):
                sp.wait_ge(job["x_ready"], b + 1)
                sp.dma_start(out_dram[b].rearrange("(t p) c -> p t c", p=P),
                             x[:, b * TPB:(b + 1) * TPB, :]).then_inc(stored, 16)
            sp.wait_ge(stored, 16 * B)


def prepare1_job(nc, m, rb_scratch, rb, wqk, wv, w):
    tab = m.sb("r1_tab", [H, 2, 3 * P])
    parts = m.sb("r1_parts", [H, 3, 3 * P], F16)
    chain = m.sem("r1_chain")
    whi_ready = m.sem("r1_whi_ready")
    saved = m.sem("r1_saved")

    def piece(u):
        return slice(u * H // 8, (u + 1) * H // 8), slice(u * H * D1 // 8, (u + 1) * H * D1 // 8)

    def scalar(act, u):
        heads, cols = piece(u)
        nc.scalar.activation(wqk[:, 0, heads], w["qk1"][:, heads], ACT.Copy)
        nc.scalar.activation(wv[:, 0, cols], w["v1"][:, cols], ACT.Copy).then_inc(whi_ready, 1)

    def split(pool, u):
        heads, cols = piece(u)
        pool.wait_ge(whi_ready, u + 1)
        nc.gpsimd.tensor_tensor(wqk[:, 1, heads], w["qk1"][:, heads], wqk[:, 0, heads],
                                ALU.subtract)
        nc.gpsimd.tensor_tensor(wv[:, 1, cols], w["v1"][:, cols], wv[:, 0, cols], ALU.subtract)

    def tables(pool, u):
        last_row = rb[:, 0, 0:1].to_broadcast([H, 255])
        if 1 <= u <= 4:
            pool.wait_ge(chain, u)
        if u == 0:
            ins = nc.gpsimd.memset(tab[:], 0.0)
        elif u == 1:
            nc.gpsimd.tensor_tensor(tab[:, 0, P:P + 255], rb[:, 0, :], last_row, ALU.subtract)
            ins = nc.gpsimd.tensor_tensor(tab[:, 1, 0:255], rb[:, 1, :], last_row, ALU.subtract)
        elif u == 2:
            ins = nc.gpsimd.tensor_copy(parts[:, 0, :], tab[:, 0, :])
        elif u == 3:
            ins = nc.gpsimd.tensor_copy(parts[:, 2, :], tab[:, 1, :])
        elif u == 4:
            ins = nc.gpsimd.tensor_tensor(parts[:, 1, :], tab[:, 0, :], parts[:, 0, :],
                                          ALU.subtract)
        if u < 5:
            ins.then_inc(chain, 1)

    def sync(sp):
        sp.wait_ge(chain, 5)
        sp.dma_start(rb_scratch.rearrange("a h n -> h a n"), parts[:]).then_inc(saved, 16)
        sp.wait_ge(saved, 16)

    return {"scalar": scalar, "split": split, "tables": tables, "sync": sync}


def attention1_phase(nc, k, xh, xl, wqk, wv, han, q2, k2, v1, z1, loads):
    DV = D1 + 1
    Q, K = slice(0, D1), slice(D1, P)
    scale = float(D1) ** -0.5
    with ExitStack() as ctx:
        m = Mem(nc, ctx)
        smax = m.ps("a1_smax", [P, 2, S])
        st = m.ps("a1_st", [P, 3, S])
        o = m.ps("a1_o", [P, S])
        qk = m.ps("a1_qk", [P, S])
        vp = m.ps("a1_vp", [P, S])
        q1 = m.sb("a1_q1", [P, 4, S], F16)
        k1 = m.sb("a1_k1", [P, 4, S], F16)
        mx = m.sb("a1_mx", [P, 2, TPB], F16)
        p32 = m.sb("a1_p32", [P, 2, TPB, S])
        ph = m.sb("a1_ph", [P, 2, TPB, S], F16)
        pl = m.sb("a1_pl", [P, 2, TPB, S], F16)
        r = m.sb("a1_r", [P, TPB])
        qk_made = m.sem("a1_qk_made")
        q_high = m.sem("a1_q_high")
        k_high = m.sem("a1_k_high")
        qk_split = m.sem("a1_qk_split")
        v_made = m.sem("a1_v_made")
        v_high = m.sem("a1_v_high")
        v_split = m.sem("a1_v_split")
        smax_ready = m.sem("a1_smax_ready")
        smax_free = m.sem("a1_smax_free")
        st_ready = m.sem("a1_st_ready")
        st_free = m.sem("a1_st_free")
        hi_ready = m.sem("a1_hi_ready")
        lo_ready = m.sem("a1_lo_ready")
        pv_done = m.sem("a1_pv_done")
        r_ready = m.sem("a1_r_ready")
        o_free = m.sem("a1_o_free")
        block = ctx.enter_context(nc.Block())
        block.sync(loads)

        UNITS = TPB + 1

        def after(h, b, by):
            return None if isinstance(h, int) and h == H - 1 and b + by >= B else shift(h, b, by)

        def bank(b, i):
            return (UNITS * b + i) % 2

        @block.tensor
        def _(pe):
            def project_qk(h, b):
                pe.wait_ge(qk_split, h * B + (b + 1))
                three_passes(nc, qk[:], wqk[:, 0, h, :], wqk[:, 1, h, :],
                             xh[:, b, 1:1 + S], xl[:, b, 1:1 + S]).then_inc(qk_made, 1)

            def project_v(h, b):
                pe.wait_ge(v_split, h * B + (b + 1))
                cols = bass.ds(h * D1, D1)
                for t in range(TPB):
                    a = 1 + t * P
                    ins = three_passes(nc, vp[:, t * D1:(t + 1) * D1], xh[:, b, a:a + P],
                                       xl[:, b, a:a + P], wv[:, 0, cols], wv[:, 1, cols])
                ins.then_inc(v_made, 1)

            def scores(h, b, i):
                n = h * B + b
                if i == 0:
                    pe.wait_ge(qk_split, n + 2)
                pe.wait_ge(smax_free, n * UNITS + (i + 1))
                ins = nc.tensor.matmul(smax[:, bank(b, i), :], q1[:, b, i * P:(i + 1) * P],
                                       k1[:, b, :], start=True, stop=i < 2)
                if i >= 2:
                    ins = nc.tensor.matmul(smax[:, bank(b, i), 0:(i - 1) * P], k["anti16"],
                                           han[:, 2, h, (3 - i) * P:2 * P],
                                           start=False, stop=True)
                ins.then_inc(smax_ready, 1)

            def row_of_maxima(h, b):
                n = h * B + b
                pe.wait_ge(smax_free, n * UNITS + 6)
                for i in range(TPB):
                    ins = nc.tensor.matmul(smax[0:1, bank(b, TPB), i * P:(i + 1) * P],
                                           mx[:, b % 2, i:i + 1], k["neg_id16"],
                                           start=True, stop=True)
                ins.then_inc(smax_ready, 1)

            def transposed(h, b, ch):
                n = h * B + b
                if ch == 0:
                    pe.wait_ge(smax_free, n * UNITS + 7)
                pe.wait_ge(st_free, n * TPB + (4, 2, 3, 5)[ch])
                ob = st[:, ch % 3, :]
                keys = slice(ch * P, (ch + 1) * P)
                nc.tensor.matmul(ob, k2[:, b, keys], q2[:, b, :], start=True, stop=False)
                ins = nc.tensor.matmul(ob, k1[:, b, keys], q1[:, b, :], start=False,
                                       stop=ch >= 2)
                for part in range(2 if ch < 2 else 0):
                    ins = nc.tensor.matmul(ob[:, (2 + ch) * P:S], k["anti16"],
                                           han[:, part, h, 0:(2 - ch) * P], start=False,
                                           stop=part == 1)
                ins.then_inc(st_ready, 1)

            def weighted(h, b, u):
                n = h * B + b
                if u == 0:
                    pe.wait_ge(v_split, n + 2)
                    pe.wait_ge(o_free, n + 1)
                    pe.wait_ge(lo_ready, n * 2 + 6)
                for i in (2 * u, 2 * u + 1):
                    ob = o[:, i * DV:(i + 1) * DV]
                    for ch in range(TPB):
                        cols = slice(i * P, (i + 1) * P)
                        nc.tensor.matmul(ob, pl[:, b % 2, ch, cols], v1[:, b, ch, 0:DV],
                                         start=ch == 0, stop=False)
                        nc.tensor.matmul(ob[:, 0:D1], ph[:, b % 2, ch, cols],
                                         v1[:, b, ch, DV:], start=False, stop=False)
                        ins = nc.tensor.matmul(ob, ph[:, b % 2, ch, cols], v1[:, b, ch, 0:DV],
                                               start=False, stop=ch == TPB - 1)
                if u == 1:
                    ins.then_inc(pv_done, 1)

            pe.sem_inc(pv_done, 2)
            project_qk(0, 0)
            project_v(0, 0)
            project_qk(0, 1)
            for i in range(TPB):
                scores(0, 0, i)
            row_of_maxima(0, 0)
            project_qk(0, 2)

            def slot(h, b, first, final):
                scored = after(h, b, 2)
                if first:
                    for i in range(TPB):
                        scores(0, 1, i)
                        transposed(0, 0, i)
                    row_of_maxima(0, 1)
                if scored:
                    scores(*scored, 0)
                if not first:
                    transposed(h, b, 0)
                if scored:
                    scores(*scored, 1)
                if after(h, b, 3):
                    project_qk(*after(h, b, 3))
                if scored:
                    scores(*scored, 2)
                if not first:
                    transposed(h, b, 1)
                if scored:
                    scores(*scored, 3)
                if not first:
                    transposed(h, b, 2)
                if after(h, b, 1):
                    project_v(*after(h, b, 1))
                if not first:
                    transposed(h, b, 3)
                    weighted(*shift(h, b, -1), 0)
                    weighted(*shift(h, b, -1), 1)
                if scored:
                    row_of_maxima(*scored)

            by_groups(pe, H, slot)
            weighted(H - 1, B - 1, 0)
            weighted(H - 1, B - 1, 1)

        @block.vector
        def _(dve):
            dve.sem_inc(qk_split, 1)
            dve.sem_inc(v_split, 1)
            dve.sem_inc(smax_free, 2)
            dve.sem_inc(o_free, 1)

            def low_q(h, b):
                dve.wait_ge(q_high, h * B + (b + 1))
                nc.vector.tensor_copy(q2[K, b, :], q1[Q, b, :])
                nc.vector.scalar_tensor_tensor(q1[K, b, :], qk[Q], scale, q1[Q, b, :],
                                               ALU.mult, ALU.subtract)

            def low_k(h, b):
                dve.wait_ge(k_high, h * B + (b + 1))
                nc.vector.tensor_copy(k1[Q, b, :], k1[K, b, :])
                nc.vector.tensor_tensor(k2[K, b, :], qk[K], k1[K, b, :], ALU.subtract
                                        ).then_inc(qk_split, 1)

            def low_v(h, b):
                dve.wait_ge(v_high, h * B + (b + 1))
                nc.vector.tensor_tensor(
                    v1[:, b, :, DV:], vp[:, 0:TPB * D1].rearrange("p (t d) -> p t d", t=TPB),
                    v1[:, b, :, 0:D1], ALU.subtract).then_inc(v_split, 1)

            def maximum(h, b, i):
                dve.wait_ge(smax_ready, (h * B + b) * UNITS + (i + 1))
                nc.vector.reduce_max(mx[:, b % 2, i:i + 1], smax[:, bank(b, i), :], AXX
                                     ).then_inc(smax_free, 1)

            def keep_row(h, b):
                dve.wait_ge(smax_ready, (h * B + b) * UNITS + UNITS)
                nc.vector.tensor_copy(q2[0:1, b, :], smax[0:1, bank(b, TPB), :]
                                      ).then_inc(smax_free, 1)

            def normalise(h, b):
                n = h * B + b
                dve.wait_ge(pv_done, n + 3)
                ob = o[:, 0:TPB * DV].rearrange("p (t d) -> p t d", t=TPB)
                nc.vector.reciprocal(r[:], ob[:, :, D1]).then_inc(r_ready, 1)
                dve.wait_ge(r_ready, n + 1)
                nc.vector.tensor_tensor(z1[:, b * TPB:(b + 1) * TPB, bass.ds(h * D1, D1)],
                                        ob[:, :, 0:D1],
                                        r[:].unsqueeze(2).to_broadcast([P, TPB, D1]), ALU.mult
                                        ).then_inc(o_free, 1)

            low_q(0, 0)
            low_k(0, 0)
            low_v(0, 0)
            low_q(0, 1)
            low_k(0, 1)
            for i in range(TPB):
                maximum(0, 0, i)
            keep_row(0, 0)
            low_q(0, 2)
            low_k(0, 2)

            def slot(h, b, first, final):
                scored, ahead = after(h, b, 2), after(h, b, 3)
                if first:
                    for i in range(TPB):
                        maximum(0, 1, i)
                if after(h, b, 1):
                    keep_row(*after(h, b, 1))
                if scored:
                    maximum(*scored, 0)
                if not (isinstance(h, int) and h == 0 and b < 2):
                    normalise(*shift(h, b, -2))
                if scored:
                    maximum(*scored, 1)
                if ahead:
                    low_q(*ahead)
                if scored:
                    maximum(*scored, 2)
                if ahead:
                    low_k(*ahead)
                if scored:
                    maximum(*scored, 3)
                if after(h, b, 1):
                    low_v(*after(h, b, 1))

            by_groups(dve, H, slot)
            normalise(H - 1, B - 2)
            normalise(H - 1, B - 1)

        @block.scalar
        def _(act):
            act.sem_inc(st_free, 4)
            act.preload_act_table(ACT.Exp)

            def high_q(h, b):
                act.wait_ge(qk_made, h * B + (b + 1))
                nc.scalar.activation(q1[Q, b, :], qk[Q], ACT.Copy, scale=scale
                                     ).then_inc(q_high, 1)

            def high_k(h, b):
                act.wait_ge(qk_made, h * B + (b + 1))
                nc.scalar.activation(k1[K, b, :], qk[K], ACT.Copy).then_inc(k_high, 1)

            def high_v(h, b):
                act.wait_ge(v_made, h * B + (b + 1))
                nc.scalar.activation(
                    v1[:, b, :, 0:D1], vp[:, 0:TPB * D1].rearrange("p (t d) -> p t d", t=TPB),
                    ACT.Copy).then_inc(v_high, 1)

            def exponent(h, b, ch):
                n = h * B + b
                act.wait_ge(st_ready, n * TPB + (ch + 1))
                act.wait_ge(lo_ready, n * 2 + (ch // 2 + 1))
                nc.scalar.activation(p32[:, b % 2, ch, :], st[:, ch % 3, :], ACT.Exp
                                     ).then_inc(st_free, 1)

            def high_p(h, b, u):
                n = h * B + b
                act.wait_ge(st_free, n * TPB + (2 * u + 6))
                act.wait_ge(pv_done, n + 1)
                nc.scalar.activation(ph[:, b % 2, 2 * u:2 * u + 2, :],
                                     p32[:, b % 2, 2 * u:2 * u + 2, :], ACT.Copy
                                     ).then_inc(hi_ready, 1)

            high_q(0, 0)
            high_k(0, 0)
            high_v(0, 0)
            for b in (1, 2):
                high_q(0, b)
                high_k(0, b)

            def slot(h, b, first, final):
                ahead = after(h, b, 3)
                exponent(h, b, 0)
                if ahead and not first:
                    high_q(*ahead)
                exponent(h, b, 1)
                if ahead and not first:
                    high_k(*ahead)
                exponent(h, b, 2)
                high_p(h, b, 0)
                if after(h, b, 1) and not first:
                    high_v(*after(h, b, 1))
                exponent(h, b, 3)
                high_p(h, b, 1)
                if first:
                    high_q(*ahead)
                    high_k(*ahead)
                    high_v(*after(h, b, 1))

            by_groups(act, H, slot)

        @block.gpsimd
        def _(pool):
            pool.sem_inc(lo_ready, 4)

            def slot(h, b, first, final):
                n = h * B + b
                for u in range(2):
                    half = slice(2 * u, 2 * u + 2)
                    pool.wait_ge(hi_ready, n * 2 + (u + 1))
                    pool.wait_ge(pv_done, n + 1)
                    nc.gpsimd.tensor_tensor(pl[:, b % 2, half, :], p32[:, b % 2, half, :],
                                            ph[:, b % 2, half, :], ALU.subtract
                                            ).then_inc(lo_ready, 1)

            by_groups(pool, H, slot)


def out1_job(nc, m, k, z1, w, s):
    NK = H * D1 // P
    zt = m.ps("o1_zt", [P, 4, S])
    out = m.ps("o1_out", [P, 2, S])
    bias_part = m.ps("o1_bias_part", [P, 1, S])
    zts = m.sb("o1_zts", [P, 2, NK, P])
    zh = m.sb("o1_zh", [P, 4, NK, P], F16)
    zl = m.sb("o1_zl", [P, 4, NK, P], F16)
    wh = m.sb("o1_wh", [P, NK, C], F16)
    wl = m.sb("o1_wl", [P, NK, C], F16)
    w_ready = m.sem("o1_w_ready")
    zt_ready = m.sem("o1_zt_ready")
    zts_ready = m.sem("o1_zts_ready")
    zh_ready = m.sem("o1_zh_ready")
    zl_ready = m.sem("o1_zl_ready")
    out_ready = m.sem("o1_out_ready")
    s_ready = m.sem("o1_s_ready")

    def turned(t):
        return zt[:, t % 2 * 2:t % 2 * 2 + 2, :].rearrange("p a (c n) -> p (a c) n", n=P)

    def vector_first(dve):
        nc.vector.tensor_copy(wh[:], w["out1"][:]).then_inc(w_ready, 1)
        dve.wait_ge(w_ready, 1)
        nc.vector.tensor_tensor(wl[:], w["out1"][:], wh[:], ALU.subtract).then_inc(w_ready, 1)

    FROM = 8

    def tensor(pe, between):
        def turn(t):
            if t >= 2:
                pe.wait_ge(zh_ready, t - 1)
            for c in range(NK):
                ins = nc.tensor.transpose(turned(t)[:, c, :], z1[:, t, c * P:(c + 1) * P],
                                          k["id"])
            ins.then_inc(zt_ready, 1)

        def project(t):
            pe.wait_ge(zl_ready, t + 1)
            if t >= 2:
                pe.wait_ge(s_ready, t - 1)
            ob = out[:, t % 2, 0:C]
            for c in range(NK):
                nc.tensor.matmul(ob, zh[:, t % 4, c, :], wl[:, c, :], start=c == 0, stop=False)
                nc.tensor.matmul(ob, zl[:, t % 4, c, :], wh[:, c, :], start=False, stop=False)
                ins = nc.tensor.matmul(ob, zh[:, t % 4, c, :], wh[:, c, :], start=False,
                                       stop=c == NK - 1)
            ins.then_inc(out_ready, 1)

        for t in range(NT):
            turn(t)
            if t == 2:
                pe.wait_ge(w_ready, 2)
            if t >= 2:
                project(t - 2)
            between(t - FROM)
        project(NT - 2)
        project(NT - 1)

    def scalar(act, between):
        def store(t):
            act.wait_ge(out_ready, t + 1)
            nc.scalar.activation(s[:, t, :], out[:, t % 2, 0:C], ACT.Copy).then_inc(s_ready, 1)

        for t in range(NT):
            act.wait_ge(zt_ready, t + 1)
            if t >= 2:
                act.wait_ge(zl_ready, t - 1)
            if t >= 4:
                act.wait_ge(out_ready, t - 3)
            nc.scalar.activation(zts[:, t % 2], turned(t), ACT.Copy).then_inc(zts_ready, 1)
            nc.scalar.activation(zh[:, t % 4], turned(t), ACT.Copy).then_inc(zh_ready, 1)
            if t >= 3:
                store(t - 3)
            between(t - FROM)
        for t in range(NT - 3, NT):
            store(t)

    def gpsimd(pool):
        for t in range(NT):
            pool.wait_ge(zts_ready, t + 1)
            pool.wait_ge(zh_ready, t + 1)
            if t >= 4:
                pool.wait_ge(out_ready, t - 3)
            nc.gpsimd.tensor_tensor(zl[:, t % 4], zts[:, t % 2], zh[:, t % 4], ALU.subtract
                                    ).then_inc(zl_ready, 1)

    return {"tensor": tensor, "scalar": scalar, "vector": lambda dve: None, "gpsimd": gpsimd,
            "vector_first": vector_first, "banks": (None, bias_part)}


CONSTS = [("id", P), ("neg_id", P), ("anti", P), ("mask_keys", 2 * P), ("mask_cols", BLK),
          ("block_mask", TPB * NBLK), ("low_q", 1), ("low_k", 1), ("sign_q", 1), ("sign_k", 1),
          ("own", G)]


def program(nc, a, out):
    with ExitStack() as ctx:
        m = Mem(nc, ctx)
        x = m.sb("x", [P, NT, C])
        s = m.sb("s", [P, NT, C])
        acc = m.sb("acc", [P, NT, C])
        xh = m.sb("xh", [P, B, S + 2], F16)
        xl = m.sb("xl", [P, B, S + 2], F16)
        cw = m.sb("cw", [P, NT, NE1])
        const = m.sb("const", [P, sum(n for _, n in CONSTS)])
        neg16 = m.sb("neg16", [P, P], F16)
        anti16 = m.sb("anti16", [P, P], F16)
        mask_keys = m.sb("mask_keys", [P, 2, P], BF16)
        mask_cols = m.sb("mask_cols", [P, BLK], BF16)
        glob = m.sb("glob", [P, 1])
        wqk = m.sb("wqk1", [P, 2, H, P], F16)
        wv = m.sb("wv1", [P, 2, H * D1], F16)
        rb = m.sb("rb", [H, 2, 255])
        w = {
            "qk0": m.sb("w_qk0", [P, 8, G, D0]), "v0": m.sb("w_v0", [P, C]),
            "proj0": m.sb("w_proj0", [P, C]), "proj0_b": m.sb("w_proj0_b", [P, C]),
            "gu_b": m.sb("w_gu_b", [P, E0, 4]),
            "e1_b": m.sb("w_e1_b", [P, NE1]),
        }
        r0 = {"router": m.sb("r0_w", [P, E0]), "router_b": m.sb("r0_wb", [P, E0]),
              "out_b": m.sb("r0_ob", [E0, C])}
        r1 = {"router": m.sb("r1_w", [P, E1]), "router_b": m.sb("r1_wb", [P, E1]),
              "out_b": m.sb("r1_ob", [NE1, C])}
        k, at = {}, 0
        for name, n in CONSTS:
            k[name] = const[:, at:at + n]
            at += n
        k32 = dict(k)
        k["block_mask"] = k["block_mask"].rearrange("p (t b) -> p t b", t=TPB)
        k["neg_id16"], k["anti16"] = neg16[:], anti16[:]
        k["mask_keys"], k["mask_cols"] = mask_keys[:], mask_cols[:]

        first_loads = m.sem("first_loads")
        x_loads = [m.sem(f"x_loads_{b}") for b in range(B)]
        const_loads = m.sem("const_loads")
        more_loads = m.sem("more_loads")
        first_gu_load = m.sem("first_gu_load")
        gu_loads = m.sem("gu_loads")
        zeroed = m.sem("zeroed")
        hankel_loads = m.sem("hankel_loads")
        late_loads = m.sem("late_loads")

        def first_loads_wait(sp):
            sp.wait_ge(first_loads, 32)

        with nc.Block() as block:
            @block.sync
            def _(sp):
                sp.dma_start(const[:], a["const"]).then_inc(const_loads, 16)
                for b in range(B):
                    sp.dma_start(x[:, b * TPB:(b + 1) * TPB, :],
                                 a["x"][b].rearrange("(t p) c -> p t c", p=P)
                                 ).then_inc(x_loads[b], 16)

            @block.scalar
            def _(act):
                act.dma_start(glob[:], a["glob"]).then_inc(const_loads, 16)
                act.dma_start(w["qk0"][:], a["qk0"]).then_inc(first_loads, 16)
                act.dma_start(w["v0"][:], a["v0"]).then_inc(first_loads, 16)

        def first_scalar(act):
            act.wait_ge(const_loads, 32)
            nc.scalar.activation(neg16[:], k32["neg_id"], ACT.Copy)
            nc.scalar.activation(anti16[:], k32["anti"], ACT.Copy)
            nc.scalar.activation(mask_cols[:], k32["mask_cols"], ACT.Copy)
            nc.scalar.activation(mask_keys[:].rearrange("p a b -> p (a b)"), k32["mask_keys"],
                                 ACT.Copy)
            act.wait_ge(first_loads, 32)

        def loads1(sp):
            for dst, src in ((w["proj0"], "proj0"), (r0["router"], "router0"),
                             (r0["out_b"], "down_b"), (w["gu_b"], "gu_b"),
                             (r1["router"], "router1"),
                             (r1["out_b"], "e1_b2"), (w["e1_b"], "e1_b1"), (rb, "rb")):
                sp.dma_start(dst[:], a[src]).then_inc(more_loads, 16)
            for dst, src in ((w["proj0_b"], "proj0_b"), (r0["router_b"], "router0_b"),
                             (r1["router_b"], "router1_b")):
                sp.dma_start(dst[:], a[src].partition_broadcast(P)).then_inc(more_loads, 16)
            sp.wait_ge(more_loads, 11 * 16)

        def loads_gu(sp):
            sp.dma_start(w["gu"][:], a["gu"]).then_inc(first_gu_load, 16)
            for name in ("down", "qk1", "v1"):
                sp.dma_start(w[name][:], a[name]).then_inc(gu_loads, 16)
            sp.wait_ge(gu_loads, 48)

        def load_hankel(sp):
            scratch = a["rb_scratch"]
            for i in range(3):
                src = bass.AP(scratch.tensor, i * H * 3 * P, [[1, P], [3 * P, H], [1, 2 * P]])
                sp.dma_start(han[:, i], src).then_inc(hankel_loads, 16)
            sp.wait_ge(hankel_loads, 48)

        def loads3(sp):
            sp.dma_start(w["out1"][:], a["out1"]).then_inc(late_loads, 16)
            sp.wait_ge(late_loads, 16)

        def loads4(sp):
            sp.dma_start(w["e1_w1"][:], a["e1_w1"]).then_inc(late_loads, 16)
            sp.dma_start(w["e1_w2"][:], a["e1_w2"]).then_inc(late_loads, 16)
            sp.wait_ge(late_loads, 48)

        with ExitStack() as pa:
            q = Mem(nc, pa)
            z0 = q.sb("z0", [P, 5, NH, D0])
            q4 = q.sb("q4", [P, NG, S], F16)
            v0 = q.sb("v0", [P, NH, 5, 2 * D0 + 1], F16)
            with ExitStack() as pk:
                kz = Mem(nc, pk).sb("kz", [P, NH, KPAD], F16)

                pw = ExitStack()
                parts0, high0, low0 = split_weights0(nc, Mem(nc, pw), w)

                def fills(pool):
                    nc.gpsimd.memset(kz[:, :, S + 1:KPAD], 0.0)
                    nc.gpsimd.memset(v0[:, :, TPB, :], 0.0).then_inc(zeroed, 1)
                    pool.wait_ge(zeroed, 1)
                    nc.gpsimd.memset(v0[:, :, :, D0:D0 + 1], 1.0)
                    low0(pool)

                def first_steps(act):
                    first_scalar(act)
                    high0(act)

                layer_norm_phase(nc, "n0", x, xh, xl, k["id"], glob, first_loads_wait, fills,
                                 x_loads, const_loads, first_steps)
                project0_phase(nc, k, xh, xl, parts0, q4, kz, v0)
                pw.close()
                attention0_phase(nc, k, q4, kz, v0, z0, loads1)
            w["gu"] = q.sb("w_gu", [P, E0, 2 * I0])
            w["down"] = q.sb("w_down", [P, E0, 2, C])
            w["qk1"] = q.sb("w_qk1", [P, H, P])
            w["v1"] = q.sb("w_v1", [P, H * D1])
            wh_gu, wl_gu, vector_gu, gpsimd_gu = split_experts0(nc, q, w, first_gu_load)
            router_phase(nc, k, "g0", xh, xl, 1, r0, cw[:, :, 0:E0], acc, E0, E0, TOP0,
                         lambda m: out0_job(nc, m, k, z0, w, s), loads_gu,
                         vector_gu, gpsimd_gu)
            ahead = prepare1_job(nc, q, a["rb_scratch"], rb, wqk, wv, w)
            experts0_phase(nc, k, xh, xl, w, wh_gu, wl_gu, cw, acc, ahead)
        with ExitStack() as ph:
            p = Mem(nc, ph)
            w["out1"] = p.sb("w_out1", [P, H * D1 // P, C])
            z1 = p.sb("z1", [P, NT, H * D1])
            with ExitStack() as pq:
                q = Mem(nc, pq)
                han = q.sb("han", [P, 3, H, 2 * P], F16)
                q2 = q.sb("a1_q2", [P, 4, S], F16)
                k2 = q.sb("a1_k2", [P, 4, S], F16)
                v1 = q.sb("a1_v1", [P, 4, TPB, 2 * D1 + 1], F16)

                def constant_parts(pool):
                    nc.gpsimd.memset(k2[0:D1], 0.0)
                    nc.gpsimd.memset(q2[0:D1], 0.0)
                    nc.gpsimd.memset(v1[:, :, :, D1:D1 + 1], 1.0).then_inc(zeroed, 1)
                    pool.wait_ge(zeroed, 2)
                    nc.gpsimd.memset(k2[0:1], 1.0)

                with ExitStack() as pu:
                    layer_norm_phase(nc, "n1", x, xh, xl, k["id"], None, load_hankel,
                                     update=update_job(nc, Mem(nc, pu), "u0", x, s, acc),
                                     after_update=constant_parts)
                attention1_phase(nc, k, xh, xl, wqk, wv, han, q2, k2, v1, z1, loads3)
            w["e1_w1"] = p.sb("w_e1_w1", [P, NE1, C])
            w["e1_w2"] = p.sb("w_e1_w2", [P, NE1, C])
            parts_e1, vector_e1 = split_experts1(nc, p, w, late_loads)
            router_phase(nc, k, "g1", xh, xl, 1, r1, cw, acc, E1, NE1, TOP1,
                         lambda m: out1_job(nc, m, k, z1, w, s), loads4, vector_e1)
            experts1_phase(nc, k, xh, xl, w, parts_e1, cw, acc)
        last_update_phase(nc, x, s, acc, out)


def shape_constants():
    import numpy as np

    c = {name: np.zeros((P, n), np.float32) for name, n in CONSTS}
    row = np.arange(P)
    c["id"][row, row] = 1
    c["neg_id"][row, row] = -1
    c["anti"][row, P - 1 - row] = 1
    c["mask_keys"][0, BLK:P] = 1
    c["mask_keys"][0, P + 1:] = 1
    c["mask_cols"][0, :] = BIG
    for t in range(S):
        for blk in range(NBLK):
            if blk > (t + 1) // BLK:
                c["block_mask"][t % P, (t // P) * NBLK + blk] = BIG
    copy = row // D0 % 4
    c["low_q"][:, 0] = copy >= 2
    c["low_k"][:, 0] = copy % 2
    for s in "qk":
        c[f"sign_{s}"][:] = 2 * c[f"low_{s}"] - 1
    c["own"][row, row // 32] = 1
    return np.concatenate([c[name] for name, _ in CONSTS], axis=1)


def laid_out(i):
    import numpy as np

    a = {n: np.asarray(v) for n, v in i.items()}
    o = {"x": a["L0_attn_x"], "const": shape_constants()}
    o["glob"] = a["L0_attn_global_token"].reshape(C, 1)
    o["qk0"] = a["L0_attn_qkv_w"][:2 * C].T.reshape(C, 8, G, D0)
    o["v0"] = a["L0_attn_qkv_w"][2 * C:].T
    o["proj0"] = a["L0_attn_proj_w"].T
    o["proj0_b"] = a["L0_attn_proj_b"]
    o["router0"] = a["L0_ffn_router_weight"].T
    o["router0_b"] = a["L0_ffn_router_bias"]
    o["gu"] = a["L0_ffn_gate_up_proj"].transpose(1, 0, 2)
    o["gu_b"] = a["L0_ffn_gate_up_bias"].reshape(E0, 4, P).transpose(2, 0, 1)
    o["down"] = a["L0_ffn_down_proj"].reshape(E0, 2, P, C).transpose(2, 0, 1, 3)
    o["down_b"] = a["L0_ffn_down_bias"]
    wt = a["L1_attn_w_qkv"].reshape(D1, 3, H, C)
    o["qk1"] = wt[:, :2].transpose(3, 2, 1, 0).reshape(C, H, P)
    o["v1"] = wt[:, 2].transpose(2, 1, 0).reshape(C, H * D1)
    o["out1"] = a["L1_attn_w_out"].T.reshape(H * D1 // P, P, C).transpose(1, 0, 2)
    rb = a["L1_attn_rel_bias"].T
    o["rb"] = np.stack([rb[:, ::-1], rb], axis=1)
    o["router1"] = a["L1_ffn_router_W"]
    o["router1_b"] = a["L1_ffn_router_b"]
    o["e1_w1"] = np.concatenate([a["L1_ffn_eW1"], a["L1_ffn_sW1"][None]]).transpose(1, 0, 2)
    o["e1_b1"] = np.concatenate([a["L1_ffn_eb1"], a["L1_ffn_sb1"][None]]).T
    o["e1_w2"] = np.concatenate([a["L1_ffn_eW2"], a["L1_ffn_sW2"][None]]).transpose(1, 0, 2)
    o["e1_b2"] = np.concatenate([a["L1_ffn_eb2"], a["L1_ffn_sb2"][None]])
    return {n: np.ascontiguousarray(v) for n, v in o.items()}


def kernel(**inputs):
    import concourse.bacc as bacc
    import numpy as np
    from concourse import mybir as mb
    from concourse.bass_utils import run_bass_kernel_spmd

    nc = bacc.Bacc("TRN2", target_bir_lowering=False, num_devices=1)
    arrays = laid_out(inputs)
    a = {n: nc.dram_tensor(f"in_{n}", v.shape, mb.dt.from_np(v.dtype), kind="ExternalInput").ap()
         for n, v in arrays.items()}
    a["rb_scratch"] = nc.dram_tensor("rb_scratch", (3, H, 3 * P), mb.dt.float16,
                                     kind="Internal").ap()
    out = nc.dram_tensor("out", (B, S, C), mb.dt.float32, kind="ExternalOutput").ap()
    program(nc, a, out)
    r = run_bass_kernel_spmd(nc, [{f"in_{n}": v for n, v in arrays.items()}], core_ids=[0])
    return r.results[0]["out"]
```
